# Optimizing a Trainium2 kernel written in Bass

```python
import numpy as np
import jax
import jax.numpy as jnp

def _softmax(x, axis=-1):
    return jax.nn.softmax(x, axis=axis)

def _gelu(x):
    return jax.nn.gelu(x, approximate=True)

def _silu(x):
    return jax.nn.silu(x)

def _sigmoid(x):
    return jax.nn.sigmoid(x)

def _layernorm(x, axis=-1, eps=1e-05):
    m = jnp.mean(x, axis=axis, keepdims=True)
    v = jnp.var(x, axis=axis, keepdims=True)
    return (x - m) / jnp.sqrt(v + eps)

def _scatter_add(tgt, idx, src, axis=0):
    return tgt.at[idx].add(src)

def _segment_sum(src, seg, n):
    return jax.ops.segment_sum(src, seg, n)
kernel_name = 'mk_decoder_postln_d1_seqx_r4_303fdc'

def setup_inputs(seed: int=0):
    np.random.seed(seed)
    _w = jnp.asarray

    def _rec_inputs():
        import jax
        import jax.numpy as jnp
        _rk = jax.random.key(seed)
        x = -0.0002928 + 1 * jax.random.normal(jax.random.fold_in(_rk, 1), (32, 256, 256), jnp.float32)
        _lenS = 256 - jax.random.randint(jax.random.fold_in(_rk, 7), (32,), 0, max(1, 256 // 4) + 1, jnp.int32)
        _lenS2 = 256 - jax.random.randint(jax.random.fold_in(_rk, 8), (32,), 0, max(1, 256 // 4) + 1, jnp.int32)
        _ctx_1024P = jax.random.normal(jax.random.fold_in(_rk, 11), (32, 16, 256), jnp.float32)
        _ctx_1024c = jax.random.dirichlet(jax.random.fold_in(_rk, 511), 0.3 * jnp.ones((16,), jnp.float32), (32, 256))
        _ctx_1024t = jnp.einsum('bsk,bkd->bsd', _ctx_1024c, _ctx_1024P)
        _ctx_1024t = _ctx_1024t * jax.lax.rsqrt(jnp.mean(jnp.square(_ctx_1024t)) + 1e-12) * 0.953939
        ctx_1024 = -1.39393e-06 + 0.999914 * (_ctx_1024t + 0.3 * jax.random.normal(jax.random.fold_in(_rk, 611), (32, 256, 256), jnp.float32))
        return (x, ctx_1024)
    x, ctx_1024 = _rec_inputs()

    def _L0_attn_setup():
        import jax, jax.numpy as jnp
        import numpy as np
        NUM_HEADS = 8
        NORM_EPS = 1e-05

        def _gla_scan(q, k, v, g):
            B, T, H, Dk = q.shape
            Dv = v.shape[-1]
            qs, ks, vs, gs = [jnp.swapaxes(x, 0, 1) for x in (q, k, v, g)]

            def step(S, inp):
                qt, kt, vt, gt = inp
                S = jnp.exp(gt)[..., None] * S + kt[..., None] * vt[..., None, :]
                ot = jnp.einsum('bhk,bhkv->bhv', qt, S)
                return (S, ot)
            S0 = jnp.zeros((B, H, Dk, Dv), jnp.float32)
            _, o = jax.lax.scan(step, S0, (qs, ks, vs, gs))
            return jnp.swapaxes(o, 0, 1)
        key = jax.random.key(seed)
        ks = jax.random.split(key, 5)
        B, T, D = (4, 512, 256)
        s = 0.02
        return {'hidden_states': jax.random.normal(ks[0], (B, T, D), jnp.float32), 'Wq': jax.random.normal(ks[1], (D, D), jnp.float32) * s, 'Wf': jax.random.normal(ks[2], (D, D), jnp.float32) * s, 'Wi': jax.random.normal(ks[3], (D, D), jnp.float32) * s, 'g_weight': jnp.ones((D,), jnp.float32), 'Wo': jax.random.normal(ks[4], (D, D), jnp.float32) * s}
    _L0_attn_all = _L0_attn_setup()
    _L0_attn_in = {k: v for k, v in _L0_attn_all.items() if k in ('Wq', 'Wf', 'Wi', 'g_weight', 'Wo')}
    del _L0_attn_all

    def _L0_xattn_setup():
        import jax, jax.numpy as jnp
        import numpy as np
        DIM = 256
        HEADS = 16
        HEAD_DIM = 64
        INNER = HEADS * HEAD_DIM

        def _split_heads(t):
            b, n, _ = t.shape
            return t.reshape(b, n, HEADS, HEAD_DIM).transpose(0, 2, 1, 3)
        key = jax.random.key(seed)
        ks = jax.random.split(key, 7)
        b, n, m = (2, 512, 512)
        s = 0.02
        return {'x': jax.random.normal(ks[0], (b, n, DIM), dtype=jnp.float32), 'context': jax.random.normal(ks[1], (b, m, DIM), dtype=jnp.float32), 'w_kv': jax.random.normal(ks[2], (DIM, 2 * INNER), dtype=jnp.float32) * s, 'w_q': jax.random.normal(ks[3], (DIM, INNER), dtype=jnp.float32) * s, 'w_out1': jax.random.normal(ks[4], (INNER, DIM), dtype=jnp.float32) * s, 'w_out2': jax.random.normal(ks[5], (DIM, DIM), dtype=jnp.float32) * s, 'gamma': jnp.ones((DIM,), dtype=jnp.float32)}
    _L0_xattn_all = _L0_xattn_setup()
    _L0_xattn_in = {k: v for k, v in _L0_xattn_all.items() if k in ('w_kv', 'w_q', 'w_out1', 'w_out2', 'gamma')}
    del _L0_xattn_all

    def _L0_ffn_setup():
        import jax, jax.numpy as jnp
        import numpy as np
        B, T, C = (4, 512, 256)
        E, H, K = (8, 512, 2)
        key = jax.random.key(seed)
        ks = jax.random.split(key, 7)
        s_in = 1.0 / np.sqrt(C)
        s_hid = 1.0 / np.sqrt(H)
        return {'x': jax.random.normal(ks[0], (B, T, C), dtype=jnp.float32), 'gate_w': jax.random.uniform(ks[1], (C, E), jnp.float32, -s_in, s_in), 'gate_b': jnp.zeros((E,), jnp.float32), 'w1': jax.random.uniform(ks[2], (E, C, H), jnp.float32, -s_in, s_in), 'b1': jax.random.uniform(ks[3], (E, H), jnp.float32, -s_in, s_in), 'w2': jax.random.uniform(ks[4], (E, H, C), jnp.float32, -s_hid, s_hid), 'b2': jax.random.uniform(ks[5], (E, C), jnp.float32, -s_hid, s_hid)}
    _L0_ffn_all = _L0_ffn_setup()
    _L0_ffn_in = {k: v for k, v in _L0_ffn_all.items() if k in ('gate_w', 'gate_b', 'w1', 'b1', 'w2', 'b2')}
    del _L0_ffn_all
    return {'x': x, 'ctx_1024': ctx_1024, 'L0_attn_Wq': _L0_attn_in['Wq'], 'L0_attn_Wf': _L0_attn_in['Wf'], 'L0_attn_Wi': _L0_attn_in['Wi'], 'L0_attn_g_weight': _L0_attn_in['g_weight'], 'L0_attn_Wo': _L0_attn_in['Wo'], 'L0_xattn_w_kv': _L0_xattn_in['w_kv'], 'L0_xattn_w_q': _L0_xattn_in['w_q'], 'L0_xattn_w_out1': _L0_xattn_in['w_out1'], 'L0_xattn_w_out2': _L0_xattn_in['w_out2'], 'L0_xattn_gamma': _L0_xattn_in['gamma'], 'L0_ffn_gate_w': _L0_ffn_in['gate_w'], 'L0_ffn_gate_b': _L0_ffn_in['gate_b'], 'L0_ffn_w1': _L0_ffn_in['w1'], 'L0_ffn_b1': _L0_ffn_in['b1'], 'L0_ffn_w2': _L0_ffn_in['w2'], 'L0_ffn_b2': _L0_ffn_in['b2']}

def reference(x, ctx_1024, L0_attn_Wq, L0_attn_Wf, L0_attn_Wi, L0_attn_g_weight, L0_attn_Wo, L0_xattn_w_kv, L0_xattn_w_q, L0_xattn_w_out1, L0_xattn_w_out2, L0_xattn_gamma, L0_ffn_gate_w, L0_ffn_gate_b, L0_ffn_w1, L0_ffn_b1, L0_ffn_w2, L0_ffn_b2):
    import jax
    import jax.numpy as jnp

    def _L0_attn_ref(hidden_states, Wq, Wf, Wi, g_weight, Wo):
        import jax, jax.numpy as jnp
        import numpy as np
        NUM_HEADS = 8
        NORM_EPS = 1e-05

        def _gla_scan(q, k, v, g):
            B, T, H, Dk = q.shape
            Dv = v.shape[-1]
            qs, ks, vs, gs = [jnp.swapaxes(x, 0, 1) for x in (q, k, v, g)]

            def step(S, inp):
                qt, kt, vt, gt = inp
                S = jnp.exp(gt)[..., None] * S + kt[..., None] * vt[..., None, :]
                ot = jnp.einsum('bhk,bhkv->bhv', qt, S)
                return (S, ot)
            S0 = jnp.zeros((B, H, Dk, Dv), jnp.float32)
            _, o = jax.lax.scan(step, S0, (qs, ks, vs, gs))
            return jnp.swapaxes(o, 0, 1)
        B, T, D = hidden_states.shape
        H = NUM_HEADS
        q = hidden_states @ Wq
        f = (hidden_states @ Wf).astype(jnp.float32)
        i = hidden_states @ Wi
        q = q * jax.nn.sigmoid(q)
        k = 1.0 - jax.nn.sigmoid(f)
        g = jax.nn.log_sigmoid(f)
        split = lambda x: x.reshape(B, T, H, -1)
        q, k, v, g = (split(q), split(k), split(i), split(g))
        scale = q.shape[-1] ** (-0.5)
        o = _gla_scan(q * scale, k, v, g)
        o = o.reshape(B, T, D)
        o = o * jax.lax.rsqrt(jnp.mean(o * o, axis=-1, keepdims=True) + NORM_EPS)
        o = o * g_weight
        return o @ Wo

    def _L0_xattn_ref(x, context, w_kv, w_q, w_out1, w_out2, gamma):
        import jax, jax.numpy as jnp
        import numpy as np
        DIM = 256
        HEADS = 16
        HEAD_DIM = 64
        INNER = HEADS * HEAD_DIM

        def _split_heads(t):
            b, n, _ = t.shape
            return t.reshape(b, n, HEADS, HEAD_DIM).transpose(0, 2, 1, 3)
        scale = HEAD_DIM ** (-0.5)
        kv = context @ w_kv
        k, v = jnp.split(kv, 2, axis=-1)
        q = _split_heads(x @ w_q)
        k = _split_heads(k)
        v = _split_heads(v)
        dots = jnp.einsum('bhid,bhjd->bhij', q, k) * scale
        attn = jax.nn.softmax(dots, axis=-1)
        out = jnp.einsum('bhij,bhjd->bhid', attn, v)
        b, h, n, d = out.shape
        out = out.transpose(0, 2, 1, 3).reshape(b, n, h * d)
        out = jax.nn.relu(out @ w_out1) @ w_out2
        mean = jnp.mean(out, axis=-1, keepdims=True)
        var = jnp.var(out, axis=-1, keepdims=True)
        return (out - mean) * jax.lax.rsqrt(var + 1e-05) * gamma

    def _L0_ffn_ref(x, gate_w, gate_b, w1, b1, w2, b2):
        import jax, jax.numpy as jnp
        import numpy as np
        B, T, C = (4, 512, 256)
        E, H, K = (8, 512, 2)
        b, t, c = x.shape
        xf = x.reshape(b * t, c)
        logits = xf @ gate_w + gate_b
        probs = jax.nn.softmax(logits, axis=-1)
        gates, expert_idx = jax.lax.top_k(probs, K)
        h = jax.nn.relu(jnp.einsum('nc,ech->neh', xf, w1) + b1)
        expert_out = jnp.einsum('neh,ehc->nec', h, w2) + b2
        onehot = jax.nn.one_hot(expert_idx, E, dtype=xf.dtype)
        weights = jnp.einsum('nk,nke->ne', gates, onehot)
        out = jnp.einsum('ne,nec->nc', weights, expert_out)
        return out.reshape(b, t, c)
    x = _layernorm(x + _L0_attn_ref(x, L0_attn_Wq, L0_attn_Wf, L0_attn_Wi, L0_attn_g_weight, L0_attn_Wo), axis=-1)
    x = _layernorm(x + _L0_xattn_ref(x, ctx_1024, L0_xattn_w_kv, L0_xattn_w_q, L0_xattn_w_out1, L0_xattn_w_out2, L0_xattn_gamma), axis=-1)
    x = _layernorm(x + _L0_ffn_ref(x, L0_ffn_gate_w, L0_ffn_gate_b, L0_ffn_w1, L0_ffn_b1, L0_ffn_w2, L0_ffn_b2), axis=-1)
    return x

_drawn_inputs = setup_inputs


def setup_inputs(seed=0):
    import zlib

    import numpy as np

    out = dict(_drawn_inputs(seed))
    spreads = {'L0_attn_g_weight': (1.0, 0.2),
     'L0_xattn_gamma': (1.0, 0.2),
     'L0_ffn_gate_b': (0.0, 0.295)}
    factors = {'L0_ffn_b1': 8.0, 'L0_ffn_b2': 7.015}
    for name, (base, spread) in spreads.items():
        noise = np.random.default_rng([zlib.crc32(name.encode()), seed]).standard_normal(out[name].shape)
        drawn = base * np.exp(spread * noise) if base else spread * noise
        out[name] = jnp.asarray(drawn.astype(out[name].dtype))
    for name, factor in factors.items():
        out[name] = (out[name] * factor).astype(out[name].dtype)
    return out
```

```python
from contextlib import ExitStack

import concourse.bass as bass
from concourse import mybir

F32 = mybir.dt.float32
F32R = mybir.dt.float32r
I32 = mybir.dt.int32
ALU = mybir.AluOpType
ACT = mybir.ActivationFunctionType
AX = mybir.AxisListType

P = 128
EPS = 1e-5


class Split:

    def __init__(self, sb, name, shape):
        self.hi = sb(name + "_hi", shape, F32R)
        self.lo = sb(name + "_lo", shape, F32R)


def product(nc, out, w, m, w_at, m_at, first, last):
    nc.tensor.matmul(out, w_at(w.hi), m_at(m.hi), start=first, stop=False, skip_group_check=True)
    nc.tensor.matmul(out, w_at(w.hi), m_at(m.lo), start=False, stop=False, skip_group_check=True)
    return nc.tensor.matmul(out, w_at(w.lo), m_at(m.hi), start=False, stop=last, skip_group_check=True)


def build_identity(nc, pool, ident, made):
    nc.gpsimd.memset(ident[:], 0.0).then_inc(made, 1)
    pool.wait_ge(made, 1)
    nc.gpsimd.affine_select(out=ident[:], in_=ident[:], compare_op=ALU.not_equal, fill=1.0, base=0,
                            pattern=[[-1, P]], channel_multiplier=1).then_inc(made, 1)


def linear_attention_pass(nc, x, wq, wf, wi, g_weight, wo, x_out):
    B, T, D = x.shape
    H = 8
    DK = D // H
    KT = D // P
    TT = T // P
    HT = P // DK
    N = KT * T
    LEVELS = [8, 16, 32, 64, 128]
    INNER = 4
    A_MIN = 1e-8
    VS = 160

    with ExitStack() as ctx:
        def sb(name, shape, dt=F32):
            return ctx.enter_context(nc.sbuf_tensor("g_" + name, shape, dt))

        def sem(name):
            return ctx.enter_context(nc.semaphore("g_" + name))

        names = ["wq", "wf", "wi", "wo"]
        stage = sb("stage", [P, 4, KT, D])
        W = {n: Split(sb, n, [P, KT, D]) for n in names}
        wo_scaled = sb("wo_scaled", [P, KT, D])
        g_cols = sb("g_cols", [P, KT])
        ident = sb("ident", [P, P])
        ones_col = sb("ones_col", [P, 1])
        neg_half = sb("neg_half", [P, TT])
        base_mask = sb("base_mask", [P, HT, P])
        level_mask = sb("level_mask", [P, INNER, HT, P // 2])
        x_in = sb("x_in", [P, TT, D])
        xT = Split(sb, "xT", [P, KT, T])
        e_f = sb("e_f", [P, N])
        e_q = sb("e_q", [P, N])
        a = sb("a", [P, N])
        k = sb("k", [P, N])
        q = sb("q", [P, N])
        C = sb("C", [P, N])
        Dx = sb("Dx", [P, N])
        R = sb("R", [P, N])
        base_f = sb("base_f", [P, 2, N])
        level_f = sb("level_f", [P, 5, 2, N // 2])
        base = Split(sb, "base", [P, 2, KT, T])
        level_k = Split(sb, "level_k", [P, 5, N])
        level_q = Split(sb, "level_q", [P, 5, KT, P])
        V = Split(sb, "V", [P, TT, KT, HT, VS])
        A = [sb("A0", [P, KT, HT, T]), sb("A1", [P, KT, HT, P])]
        AS = [Split(sb, "AS0", [P, KT, HT, T]), Split(sb, "AS1", [P, KT, HT, P])]
        oT = Split(sb, "oT", [P, KT, T])
        sq = sb("sq", [P, KT, T])
        msq = sb("msq", [P, TT])
        rms = sb("rms", [P, TT])
        z = sb("z", [P, TT, D])
        stats = sb("stats", [P, TT, 6])
        mv = sb("mv", [P, TT, 2])
        var = sb("var", [P, TT])
        rstd = sb("rstd", [P, TT])
        x1 = sb("x1", [P, TT, D])

        ps = ctx.enter_context(nc.psum_tensor("g_ps", [P, 4, 512], F32))
        grp = ctx.enter_context(nc.psum_tensor("g_grp", [P, HT, 512], F32))

        loaded_w = sem("loaded_w"); const_made = sem("const_made"); pool_self = sem("pool_self")
        w_hi_made = sem("w_hi"); w_ready = sem("w_ready"); wo_made = sem("wo_made")
        x_loaded = sem("x_loaded"); x_stored = sem("x_stored"); x1_made = sem("x1_made")
        xT_ps = sem("xT_ps"); xT_hi = sem("xT_hi"); xT_lo = sem("xT_lo")
        f_ps = sem("f_ps"); q_ps = sem("q_ps"); v_ps = sem("v_ps")
        exp_f = sem("exp_f"); exp_q = sem("exp_q"); q_made = sem("q_made")
        v_hi = sem("v_hi"); v_lo = sem("v_lo"); a_made = sem("a_made"); k_made = sem("k_made")
        d_reset = sem("d_reset"); chain = sem("chain"); dve_self = sem("dve_self")
        fac_made = sem("fac_made"); fac_hi = sem("fac_hi"); fac_lo = sem("fac_lo")
        grp_ps = sem("grp_ps"); grp_merged = sem("grp_merged")
        A_hi = sem("A_hi"); A_lo = sem("A_lo")
        o_ps = sem("o_ps"); o_hi = sem("o_hi"); o_lo = sem("o_lo"); sq_made = sem("sq_made")
        y_ps = sem("y_ps"); msq_made = sem("msq_made"); rms_made = sem("rms_made")
        z_made = sem("z_made"); var_made = sem("var_made"); rstd_made = sem("rstd_made")

        dve_gate = sem("dve_gate"); pool_gate = sem("pool_gate")

        counted = [x_loaded, x_stored, x1_made, xT_ps, xT_hi, xT_lo, f_ps, q_ps, v_ps, exp_f, exp_q, q_made, v_hi, v_lo,
                   a_made, k_made, d_reset, chain, fac_made, fac_hi, fac_lo, grp_ps, grp_merged,
                   A_hi, A_lo, o_ps, o_hi, o_lo, sq_made, y_ps, msq_made,
                   rms_made, z_made, var_made, rstd_made]

        xr = x.rearrange("b (t p) d -> b p t d", p=P)
        outr = x_out.rearrange("b (t p) d -> b p t d", p=P)

        def half(t, h, which):
            return t.rearrange("p (n two h) -> p n two h", two=2, h=h)[:, :, which, :]

        def first_half(t, h):
            return half(t, h, 0)

        block = ctx.enter_context(nc.Block())

        @block.sync
        def _(sp):
            for s in counted:
                sp.sem_inc(s, 1)
            for n, w in enumerate([wq, wf, wi, wo]):
                sp.dma_start(stage[:, n], w.rearrange("(k p) n -> p k n", p=P)).then_inc(loaded_w, 16)
            with nc.allow_non_contiguous_dma(reason="256 scales, once"):
                sp.dma_start(g_cols[:], g_weight.rearrange("(k p) -> p k", p=P)).then_inc(loaded_w, 16)
            with sp.Fori(0, B) as i:
                sp.wait_ge(z_made, i * TT + 1)
                sp.dma_start(x_in[:], xr[bass.ds(i, 1)].rearrange("a p t d -> (a p) t d")).then_inc(x_loaded, 16)
                sp.wait_ge(x1_made, i * TT + TT + 1)
                sp.dma_start(outr[bass.ds(i, 1)].rearrange("a p t d -> (a p) t d"), x1[:]).then_inc(x_stored, 16)
            sp.wait_ge(x_stored, 16 * B + 1)

        @block.gpsimd
        def _(pool):
            build_identity(nc, pool, ident, const_made)
            nc.gpsimd.memset(ones_col[:], 1.0).then_inc(const_made, 1)
            nc.gpsimd.memset(neg_half[:], -0.5).then_inc(const_made, 1)
            nc.gpsimd.memset(base_mask[:], 1.0).then_inc(pool_self, 1)
            nc.gpsimd.memset(level_mask[:], 1.0).then_inc(pool_self, 1)
            pool.wait_ge(pool_self, 2)
            nc.gpsimd.affine_select(out=base_mask[:], in_=base_mask[:], compare_op=ALU.is_ge, fill=0.0,
                                    base=0, pattern=[[0, HT], [1, P]], channel_multiplier=-1).then_inc(pool_self, 1)
            pool.wait_ge(pool_self, 3)
            bm = base_mask[:].rearrange("p h (b e) -> p h b e", e=8)
            nc.gpsimd.affine_select(out=bm, in_=bm, compare_op=ALU.is_ge, fill=0.0, base=0,
                                    pattern=[[0, HT], [-8, P // 8], [0, 8]], channel_multiplier=1).then_inc(const_made, 1)
            for n, h in enumerate(LEVELS[:INNER]):
                lm = level_mask[:, n].rearrange("p h (b e) -> p h b e", e=h)
                nc.gpsimd.affine_select(out=lm, in_=lm, compare_op=ALU.is_ge, fill=0.0, base=0,
                                        pattern=[[0, HT], [-2 * h, P // 2 // h], [0, h]],
                                        channel_multiplier=1).then_inc(pool_self, 1)
                pool.wait_ge(pool_self, 4 + n)
                nc.gpsimd.affine_select(out=lm, in_=lm, compare_op=ALU.is_ge, fill=0.0, base=h - 1,
                                        pattern=[[0, HT], [2 * h, P // 2 // h], [0, h]],
                                        channel_multiplier=-1).then_inc(const_made, 1)
            for t in [V.hi, V.lo, level_k.hi, level_k.lo]:
                nc.gpsimd.memset(t[:].bitcast(F32), 0.0).then_inc(const_made, 1)
            for t in A:
                nc.gpsimd.memset(t[:], 0.0).then_inc(const_made, 1)
            pool.wait_ge(const_made, 15)
            with pool.Fori(0, B) as i:
                pool.wait_ge(fac_made, i * 6 + 1)
                pool.sem_inc(pool_gate, 1)
                nc.gpsimd.memset(Dx[:], 1.0).then_inc(d_reset, 1)
                pool.wait_ge(a_made, i + 1 + 1)
                pool.sem_inc(pool_gate, 1)
                nc.gpsimd.tensor_scalar(k[:], a[:], -1.0, 1.0, ALU.mult, ALU.add).then_inc(k_made, 1)
                for n in range(6):
                    pool.wait_ge(fac_hi, i * 6 + n + 1 + 1)
                    if n == 0:
                        nc.gpsimd.tensor_tensor(base.lo[:].rearrange("p s k t -> p s (k t)"), base_f[:],
                                                base.hi[:].bitcast(F32).rearrange("p s k t -> p s (k t)"),
                                                ALU.subtract).then_inc(fac_lo, 1)
                    else:
                        h = LEVELS[n - 1]
                        nc.gpsimd.tensor_tensor(first_half(level_k.lo[:, n - 1], h),
                                                level_f[:, n - 1, 0].rearrange("p (n h) -> p n h", h=h),
                                                first_half(level_k.hi[:, n - 1].bitcast(F32), h), ALU.subtract)
                        nc.gpsimd.tensor_tensor(level_q.lo[:, n - 1].rearrange("p k t -> p (k t)"), level_f[:, n - 1, 1],
                                                level_q.hi[:, n - 1].bitcast(F32).rearrange("p k t -> p (k t)"),
                                                ALU.subtract).then_inc(fac_lo, 1)
                for c in range(KT):
                    for s in range(TT):
                        pool.wait_ge(A_hi, i * 4 + c * 2 + s + 1 + 1)
                        nc.gpsimd.tensor_tensor(AS[s].lo[:, c], A[s][:, c], AS[s].hi[:, c].bitcast(F32),
                                                ALU.subtract).then_inc(A_lo, 1)
                pool.wait_ge(msq_made, i + 1 + 1)
                nc.gpsimd.tensor_tensor(rms[:], msq[:], neg_half[:], ALU.pow).then_inc(rms_made, 1)
                pool.wait_ge(var_made, i + 1 + 1)
                nc.gpsimd.tensor_tensor(rstd[:], var[:], neg_half[:], ALU.pow).then_inc(rstd_made, 1)

        @block.tensor
        def _(pe):
            pe.wait_ge(const_made, 15)
            pe.wait_ge(w_ready, 4)
            with pe.Fori(0, B) as i:
                pe.wait_ge(x_loaded, i * 16 + 16 + 1)
                for kt in range(KT):
                    for tt in range(TT):
                        mm = nc.tensor.transpose(ps[:, 0, kt * T + tt * P:kt * T + tt * P + P],
                                                 x_in[:, tt, kt * P:kt * P + P], ident[:])
                mm.then_inc(xT_ps, 1)
                pe.wait_ge(xT_lo, i + 1 + 1)
                for bank, w, done, freed in ((1, "wf", f_ps, exp_f), (2, "wq", q_ps, q_made)):
                    pe.wait_ge(freed, i + 1)
                    for m in range(KT):
                        for kt in range(KT):
                            mm = product(nc, ps[:, bank, m * T:m * T + T], W[w], xT,
                                         lambda t, kt=kt, m=m: t[:, kt, m * P:m * P + P],
                                         lambda t, kt=kt: t[:, kt, :], kt == 0, kt == KT - 1)
                    mm.then_inc(done, 1)
                pe.wait_ge(v_lo, i * 2 + 1)
                for tt in range(TT):
                    for kt in range(KT):
                        mm = product(nc, ps[:, 3, tt * D:tt * D + D], xT, W["wi"],
                                     lambda t, kt=kt, tt=tt: t[:, kt, tt * P:tt * P + P],
                                     lambda t, kt=kt: t[:, kt, :], kt == 0, kt == KT - 1)
                mm.then_inc(v_ps, 1)
                for g, (c, b) in enumerate([(c, b) for c in range(KT) for b in range(TT)]):
                    pe.wait_ge(grp_merged, i * 4 + g + 1)
                    for n in range(6 if b == 0 else 5):
                        pe.wait_ge(fac_lo, i * 6 + n + 1 + 1)
                        for pw, pm in (("hi", "hi"), ("hi", "lo"), ("lo", "hi")):
                            for j in range(HT):
                                rows = slice(DK * j, DK * j + DK)
                                if n == 0:
                                    w = (base.hi if pw == "hi" else base.lo)[rows, 0, c, b * P:b * P + P]
                                    m = (base.hi if pm == "hi" else base.lo)[rows, 1, c, b * P:b * P + P]
                                    out = grp[:, j, 0:P]
                                elif n <= INNER:
                                    w = (level_k.hi if pw == "hi" else level_k.lo)[rows, n - 1, c * T + b * P:c * T + b * P + P]
                                    m = (level_q.hi if pm == "hi" else level_q.lo)[rows, n - 1, c, b * 64:b * 64 + 64]
                                    out = grp[:, j, P + (n - 1) * 64:P + n * 64]
                                else:
                                    w = (level_k.hi if pw == "hi" else level_k.lo)[rows, n - 1, c * T:c * T + P]
                                    m = (level_q.hi if pm == "hi" else level_q.lo)[rows, n - 1, c, :]
                                    out = grp[:, j, 384:512]
                                mm = nc.tensor.matmul(out, w, m, start=(pw == "hi" and pm == "hi"),
                                                      stop=(pw == "lo"), tile_position=(DK * j, 0),
                                                      skip_group_check=True)
                    mm.then_inc(grp_ps, 1)
                pe.wait_ge(v_lo, i * 2 + 2 + 1)
                pe.wait_ge(A_lo, i * 4 + 4 + 1)
                for c in range(KT):
                    for s in range(TT):
                        for j in range(HT):
                            mm = product(nc, ps[:, 0, c * T + s * P:c * T + T], V, AS[s],
                                         lambda t, c=c, s=s, j=j: t[:, s, c].rearrange("p j v -> p (j v)")[:, P * j:P * j + P],
                                         lambda t, c=c, j=j: t[:, c, j, :],
                                         s == 0 and j == 0, s == TT - 1 and j == HT - 1)
                mm.then_inc(o_ps, 1)
                pe.wait_ge(o_lo, i + 1 + 1)
                pe.wait_ge(sq_made, i + 1 + 1)
                for tt in range(TT):
                    for c in range(KT):
                        mm = nc.tensor.matmul(ps[:, 2, tt:tt + 1], sq[:, c, tt * P:tt * P + P], ones_col[:],
                                              start=(c == 0), stop=(c == KT - 1), skip_group_check=True)
                for tt in range(TT):
                    for c in range(KT):
                        mm = product(nc, ps[:, 1, tt * D:tt * D + D], oT, W["wo"],
                                     lambda t, c=c, tt=tt: t[:, c, tt * P:tt * P + P],
                                     lambda t, c=c: t[:, c, :], c == 0, c == KT - 1)
                mm.then_inc(y_ps, 1)

        @block.scalar
        def _(act):
            act.wait_ge(loaded_w, 16 * 5)
            for n, name in enumerate(names):
                if name == "wo":
                    act.wait_ge(wo_made, 1)
                src = wo_scaled[:] if name == "wo" else stage[:, n]
                nc.scalar.activation(W[name].hi[:], src, ACT.Copy).then_inc(w_hi_made, 1)
            with act.Fori(0, B) as i:
                act.wait_ge(xT_ps, i + 1 + 1)
                nc.scalar.activation(xT.hi[:].rearrange("p k t -> p (k t)"), ps[:, 0], ACT.Copy).then_inc(xT_hi, 1)
                act.wait_ge(f_ps, i + 1 + 1)
                act.wait_ge(a_made, i + 1)
                nc.scalar.activation(e_f[:], ps[:, 1], ACT.Exp, scale=-1.0).then_inc(exp_f, 1)
                act.wait_ge(q_ps, i + 1 + 1)
                act.wait_ge(q_made, i + 1)
                nc.scalar.activation(e_q[:], ps[:, 2], ACT.Exp, scale=-1.0).then_inc(exp_q, 1)
                act.wait_ge(v_ps, i + 1 + 1)
                for tt in range(TT):
                    nc.scalar.activation(V.hi[:, tt, :, :, 0:DK],
                                         ps[:, 3, tt * D:tt * D + D].rearrange("p (c j d) -> p c j d", c=KT, d=DK),
                                         ACT.Copy).then_inc(v_hi, 1)
                act.wait_ge(grp_ps, i * 4 + 1)
                for n in range(6):
                    act.wait_ge(fac_made, i * 6 + n + 1 + 1)
                    if n == 0:
                        nc.scalar.activation(base.hi[:].rearrange("p s k t -> p s (k t)"), base_f[:],
                                             ACT.Copy).then_inc(fac_hi, 1)
                    else:
                        h = LEVELS[n - 1]
                        nc.scalar.activation(first_half(level_k.hi[:, n - 1], h),
                                             level_f[:, n - 1, 0].rearrange("p (n h) -> p n h", h=h), ACT.Copy)
                        nc.scalar.activation(level_q.hi[:, n - 1].rearrange("p k t -> p (k t)"), level_f[:, n - 1, 1],
                                             ACT.Copy).then_inc(fac_hi, 1)
                act.wait_ge(o_ps, i + 1)
                for c in range(KT):
                    act.wait_ge(grp_merged, i * 4 + 2 * c + 2 + 1)
                    for s in range(TT):
                        nc.scalar.activation(AS[s].hi[:, c], A[s][:, c], ACT.Copy).then_inc(A_hi, 1)
                act.wait_ge(o_ps, i + 1 + 1)
                nc.scalar.activation(oT.hi[:].rearrange("p k t -> p (k t)"), ps[:, 0], ACT.Copy).then_inc(o_hi, 1)
                nc.scalar.activation(sq[:].rearrange("p k t -> p (k t)"), ps[:, 0], ACT.Square).then_inc(sq_made, 1)

        @block.vector
        def _(ve):
            dve = nc.vector
            ve.wait_ge(loaded_w, 16 * 5)
            for kt in range(KT):
                ins = dve.tensor_scalar(wo_scaled[:, kt], stage[:, 3, kt], g_cols[:, kt:kt + 1], None, ALU.mult)
            ins.then_inc(wo_made, 1)
            for n, name in enumerate(names):
                ve.wait_ge(w_hi_made, n + 1)
                if name == "wo":
                    ve.wait_ge(wo_made, 1)
                src = wo_scaled[:] if name == "wo" else stage[:, n]
                dve.tensor_tensor(W[name].lo[:], src, W[name].hi[:].bitcast(F32), ALU.subtract).then_inc(w_ready, 1)
            ve.wait_ge(const_made, 15)
            LINKS = 39
            with ve.Fori(0, B) as i:
                linked = [0]

                def link(ins):
                    linked[0] += 1
                    ins.then_inc(chain, 1)
                    ve.wait_ge(chain, i * LINKS + linked[0] + 1)

                ve.wait_ge(xT_hi, i + 1 + 1)
                dve.tensor_tensor(xT.lo[:].rearrange("p k t -> p (k t)"), ps[:, 0],
                                  xT.hi[:].bitcast(F32).rearrange("p k t -> p (k t)"), ALU.subtract).then_inc(xT_lo, 1)
                ve.wait_ge(exp_f, i + 1 + 1)
                ve.wait_ge(k_made, i + 1)
                link(dve.tensor_scalar(C[:], e_f[:], 1.0, None, ALU.add))
                dve.reciprocal(a[:], C[:]).then_inc(a_made, 1)
                ve.wait_ge(a_made, i + 1 + 1)
                link(dve.tensor_scalar(C[:], a[:], A_MIN, None, ALU.max))
                ve.wait_ge(exp_q, i + 1 + 1)
                link(dve.tensor_scalar(R[:], e_q[:], 1.0, None, ALU.add))
                link(dve.reciprocal(q[:], R[:]))
                dve.scalar_tensor_tensor(out=q[:], in0=ps[:, 2], scalar=float(DK) ** -0.5, in1=q[:],
                                         op0=ALU.mult, op1=ALU.mult).then_inc(q_made, 1)
                ve.wait_ge(q_made, i + 1 + 1)
                for tt in range(TT):
                    ve.wait_ge(v_hi, i * 2 + 2 + 1)
                    dve.tensor_tensor(V.lo[:, tt, :, :, 0:DK],
                                      ps[:, 3, tt * D:tt * D + D].rearrange("p (c j d) -> p c j d", c=KT, d=DK),
                                      V.hi[:, tt, :, :, 0:DK].bitcast(F32), ALU.subtract).then_inc(v_lo, 1)
                ve.wait_ge(d_reset, i + 1 + 1)
                ve.wait_ge(k_made, i + 1 + 1)

                def grow(h):
                    shape = [P, N // (2 * h), h]
                    c1 = half(C[:], h, 1)
                    if h > 1:
                        link(dve.tensor_tensor(half(Dx[:], h, 0), half(Dx[:], h, 0),
                                               c1[:, :, h - 1:h].broadcast_to(shape), ALU.mult))
                    else:
                        link(dve.tensor_copy(half(Dx[:], h, 0), c1))
                    link(dve.tensor_tensor(c1, c1, half(C[:], h, 0)[:, :, h - 1:h].broadcast_to(shape), ALU.mult))

                for h in (1, 2):
                    grow(h)
                dve.reciprocal(half(R[:], 4, 0), half(Dx[:], 4, 0))
                link(dve.reciprocal(half(R[:], 4, 1), half(C[:], 4, 1)))
                ve.wait_ge(fac_lo, i * 6 + 1)
                for side, t, f0, f1 in ((0, k, Dx, R), (1, q, R, C)):
                    for w, f in ((0, f0), (1, f1)):
                        ins = dve.tensor_tensor(half(base_f[:, side], 4, w), half(t[:], 4, w), half(f[:], 4, w), ALU.mult)
                ins.then_inc(fac_made, 1)
                grow(4)
                for n, h in enumerate(LEVELS):
                    dve.tensor_tensor(level_f[:, n, 0].rearrange("p (n h) -> p n h", h=h), half(k[:], h, 0),
                                      half(Dx[:], h, 0), ALU.mult)
                    dve.tensor_tensor(level_f[:, n, 1].rearrange("p (n h) -> p n h", h=h), half(q[:], h, 1),
                                      half(C[:], h, 1), ALU.mult).then_inc(fac_made, 1)
                    if h < LEVELS[-1]:
                        ve.wait_ge(fac_made, i * 6 + n + 2 + 1)
                        grow(h)
                ve.wait_ge(A_lo, i * 4 + 1)
                for g, (c, b) in enumerate([(c, b) for c in range(KT) for b in range(TT)]):
                    ve.wait_ge(grp_ps, i * 4 + g + 1 + 1)
                    tile = A[b][:, c, :, 0:P]
                    ve.sem_inc(dve_gate, 1)
                    link(dve.copy_predicated(tile, base_mask[:].bitcast(I32), grp[:, :, 0:P]))
                    for n, h in enumerate(LEVELS[:INNER]):
                        to = tile.rearrange("p j (n two h) -> p j n two h", two=2, h=h)[:, :, :, 1, :]
                        data = grp[:, :, P + 64 * n:P + 64 * n + 64].rearrange("p j (n h) -> p j n h", h=h)
                        mask = level_mask[:, n].rearrange("p j (n h) -> p j n h", h=h)
                        ve.sem_inc(dve_gate, 1)
                        ins = dve.copy_predicated(to, mask.bitcast(I32), data)
                        if n < INNER - 1 or b == 0:
                            link(ins)
                    if b == 0:
                        ins = dve.tensor_copy(A[0][:, c, :, P:2 * P], grp[:, :, 384:512])
                    ins.then_inc(grp_merged, 1)
                ve.wait_ge(o_hi, i + 1 + 1)
                ve.wait_ge(sq_made, i + 1 + 1)
                dve.tensor_tensor(oT.lo[:].rearrange("p k t -> p (k t)"), ps[:, 0],
                                  oT.hi[:].bitcast(F32).rearrange("p k t -> p (k t)"), ALU.subtract).then_inc(o_lo, 1)
                ve.wait_ge(y_ps, i + 1 + 1)
                dve.tensor_scalar(msq[:], ps[:, 2, 0:TT], 1.0 / D, EPS, ALU.mult, ALU.add).then_inc(msq_made, 1)
                ve.wait_ge(rms_made, i + 1 + 1)
                for tt in range(TT):
                    dve.scalar_tensor_tensor(out=z[:, tt], in0=ps[:, 1, tt * D:tt * D + D], scalar=rms[:, tt:tt + 1],
                                             in1=x_in[:, tt], op0=ALU.mult, op1=ALU.add).then_inc(z_made, 1)
                ve.wait_ge(z_made, i * 2 + 2 + 1)
                for tt in range(TT):
                    ins = dve.bn_stats(stats[:, tt], z[:, tt])
                link(ins)
                for tt in range(TT):
                    ve.sem_inc(dve_gate, 1)
                    ins = dve.bn_aggr(mv[:, tt], stats[:, tt])
                link(ins)
                dve.tensor_scalar(var[:], mv[:, :, 1], EPS, None, ALU.add).then_inc(var_made, 1)
                ve.wait_ge(rstd_made, i + 1 + 1)
                ve.wait_ge(x_stored, i * 16 + 1)
                for tt in range(TT):
                    dve.tensor_scalar(x1[:, tt], z[:, tt], mv[:, tt, 0:1], rstd[:, tt:tt + 1],
                                      ALU.subtract, ALU.mult).then_inc(x1_made, 1)
                assert linked[0] == LINKS, linked


def cross_attention_pass(nc, x, context, w_kv, w_q, w_out1, w_out2, gamma, x_out):
    B, T, D = x.shape
    INNER = w_q.shape[1]
    DH = 64
    PAIRS = INNER // P
    KT = D // P
    TT = T // P
    SCALE = float(DH) ** -0.5

    UNITS = ["c"] + [f"k{n}" for n in range(4)] + [f"v{n}" for n in range(4)] + ["x"] + [f"q{n}" for n in range(4)]
    UNITS += ["t0,0", "t0,1"]
    for p in range(1, PAIRS):
        UNITS += [f"t{p},0", f"t{p},1", f"o{p - 1}"]
    UNITS += [f"o{PAIRS - 1}", "h", "z"]
    NU = len(UNITS)
    assert NU % 4 == 0
    AT = {u: n for n, u in enumerate(UNITS)}

    with ExitStack() as ctx:
        def sb(name, shape, dt=F32):
            return ctx.enter_context(nc.sbuf_tensor("c_" + name, shape, dt))

        def sem(name):
            return ctx.enter_context(nc.semaphore("c_" + name))

        stage = sb("stage", [P, 2, 2048])
        wkv = Split(sb, "wkv", [P, KT, 2 * INNER])
        wq = Split(sb, "wq", [P, KT, INNER])
        w1 = Split(sb, "w1", [P, PAIRS, D])
        w2 = Split(sb, "w2", [P, KT, D])
        gam = sb("gamma", [P, D])
        ident = sb("ident", [P, P])
        neg_half = sb("neg_half", [P, TT])
        c_in = sb("c_in", [P, TT, D])
        x_in = sb("x_in", [P, TT, D])
        cT = Split(sb, "cT", [P, KT, T])
        xT = Split(sb, "xT", [P, KT, T])
        kT = Split(sb, "kT", [P, PAIRS, T])
        qT = Split(sb, "qT", [P, PAIRS, T])
        V = Split(sb, "V", [P, TT, PAIRS, 3, DH])
        E = sb("E", [P, 2, 2, TT, T])
        PT = Split(sb, "PT", [P, 2, 4, T])
        oT = Split(sb, "oT", [P, PAIRS, T])
        hT = Split(sb, "hT", [P, KT, T])
        top = sb("top", [P, 2, 2, TT])
        bias = sb("bias", [P, 2, 2, TT])
        total = sb("total", [P, 2, 2, TT])
        recip = sb("recip", [P, 2, 2, TT])
        stats = sb("stats", [P, TT, 6])
        mv = sb("mv", [P, TT, 2])
        var = sb("var", [P, 2, TT])
        rstd = sb("rstd", [P, 2, TT])
        y = sb("y", [P, TT, D])
        yg = sb("yg", [P, TT, D])
        z = sb("z", [P, TT, D])
        x2 = sb("x2", [P, TT, D])

        ring = ctx.enter_context(nc.psum_tensor("c_ring", [P, 4, 512], F32))
        score = ctx.enter_context(nc.psum_tensor("c_score", [P, 4, TT, T], F32))

        w_loaded = [sem(f"w_loaded{n}") for n in range(2)]
        w_hi = sem("w_hi"); w_lo = sem("w_lo"); gamma_loaded = sem("gamma_loaded")
        const_made = sem("const_made")
        c_loaded = sem("c_loaded"); x_loaded = sem("x_loaded"); x_stored = sem("x_stored")
        unit_ready = sem("unit_ready"); unit_hi = sem("unit_hi"); unit_lo = sem("unit_lo")
        scores = sem("scores"); bias_made = sem("bias_made"); exp_made = sem("exp_made")
        recip_made = sem("recip_made"); normal = sem("normal")
        chain = sem("chain"); z_made = sem("z_made"); var_made = sem("var_made"); rstd_made = sem("rstd_made")
        x2_made = sem("x2_made")
        dve_gate = sem("dve_gate"); pool_gate = sem("pool_gate")
        counted = [c_loaded, x_loaded, x_stored, unit_ready, unit_hi, unit_lo, scores, bias_made, exp_made,
                   recip_made, normal, chain, z_made, var_made, rstd_made, x2_made]

        xr = x.rearrange("b (t p) d -> b p t d", p=P)
        cr = context.rearrange("b (t p) d -> b p t d", p=P)
        outr = x_out.rearrange("b (t p) d -> b p t d", p=P)
        flat = lambda t: t.rearrange("p k t -> p (k t)")

        kvr = w_kv.rearrange("(k p) n -> p k n", p=P)
        pieces = [(kvr[:, k], wkv, (lambda t, k=k: t[:, k, :]), 2048) for k in range(KT)]
        pieces += [(w_q.rearrange("(k p) n -> p k n", p=P), wq, lambda t: flat(t[:]), 2048)]
        pieces += [(w_out1.rearrange("(k p) n -> p k n", p=P), w1, lambda t: flat(t[:]), 2048)]
        pieces += [(w_out2.rearrange("(k p) n -> p k n", p=P), w2, lambda t: flat(t[:]), 512)]

        block = ctx.enter_context(nc.Block())

        @block.sync
        def _(sp):
            for s in counted:
                sp.sem_inc(s, 1)
            sp.dma_start(gam[:], gamma.rearrange("(a d) -> a d", a=1).broadcast_to([P, D])).then_inc(gamma_loaded, 16)
            for n, (src, _, _, cols) in enumerate(pieces):
                if n >= 2:
                    sp.wait_ge(w_lo, n - 1)
                dst = stage[:, n % 2, 0:cols]
                if len(src.shape) == 3:
                    dst = dst.rearrange("p (k n) -> p k n", k=src.shape[1])
                sp.dma_start(dst, src).then_inc(w_loaded[n % 2], 16)
            with sp.Fori(0, B) as i:
                sp.wait_ge(unit_ready, i * NU + 1)
                sp.dma_start(c_in[:], cr[bass.ds(i, 1)].rearrange("a p t d -> (a p) t d")).then_inc(c_loaded, 16)
                sp.wait_ge(z_made, i * TT + 1)
                sp.dma_start(x_in[:], xr[bass.ds(i, 1)].rearrange("a p t d -> (a p) t d")).then_inc(x_loaded, 16)
                sp.wait_ge(x2_made, i * TT + TT + 1)
                sp.dma_start(outr[bass.ds(i, 1)].rearrange("a p t d -> (a p) t d"), x2[:]).then_inc(x_stored, 16)
            sp.wait_ge(x_stored, 16 * B + 1)

        @block.gpsimd
        def _(pool):
            build_identity(nc, pool, ident, const_made)
            nc.gpsimd.memset(neg_half[:], -0.5).then_inc(const_made, 1)
            for t in (V.hi, V.lo):
                nc.gpsimd.memset(t[:].bitcast(F32), 0.0).then_inc(const_made, 1)
            with pool.Fori(0, B) as i:
                for p in range(PAIRS):
                    for j in range(2):
                        for tt in range(TT):
                            if j == 0 and tt == 0:
                                pool.wait_ge(recip_made, i * PAIRS + p + 2)
                                pool.sem_inc(pool_gate, 1)
                            e = E[:, p % 2, j, tt, :]
                            ins = nc.gpsimd.tensor_scalar(e, e, recip[:, p % 2, j, tt:tt + 1], 1.0, ALU.mult, ALU.mult)
                    ins.then_inc(normal, 1)
                for n in range(2):
                    pool.wait_ge(var_made, i * 2 + n + 2)
                    nc.gpsimd.tensor_tensor(rstd[:, n], var[:, n], neg_half[:], ALU.pow).then_inc(rstd_made, 1)

        @block.tensor
        def _(pe):
            pe.wait_ge(const_made, 5)
            pe.wait_ge(w_lo, len(pieces))
            with pe.Fori(0, B) as i:
                def bank(unit):
                    n = AT[unit]
                    pe.wait_ge(unit_lo, i * NU + max(n - 3, 0) + 1)
                    return ring[:, n % 4]

                def transposed(unit, src):
                    to = bank(unit)
                    for kt in range(KT):
                        for tt in range(TT):
                            mm = nc.tensor.transpose(to[:, kt * T + tt * P:kt * T + tt * P + P],
                                                     src[:, tt, kt * P:kt * P + P], ident[:])
                    mm.then_inc(unit_ready, 1)

                def drained(unit):
                    pe.wait_ge(unit_lo, i * NU + AT[unit] + 2)

                pe.wait_ge(c_loaded, i * 16 + 17)
                transposed("c", c_in)
                drained("c")
                for n in range(4):
                    to = bank(f"k{n}")
                    for m in range(2):
                        p = 2 * n + m
                        for kt in range(KT):
                            mm = product(nc, to[:, m * T:m * T + T], wkv, cT,
                                         lambda t, kt=kt, p=p: t[:, kt, p * P:p * P + P],
                                         lambda t, kt=kt: t[:, kt, :], kt == 0, kt == KT - 1)
                    mm.then_inc(unit_ready, 1)
                for n in range(4):
                    to = bank(f"v{n}")
                    st, half = divmod(n, 2)
                    for kt in range(KT):
                        mm = product(nc, to[:, :], cT, wkv,
                                     lambda t, kt=kt, st=st: t[:, kt, st * P:st * P + P],
                                     lambda t, kt=kt, half=half: t[:, kt, INNER + half * 512:INNER + half * 512 + 512],
                                     kt == 0, kt == KT - 1)
                    mm.then_inc(unit_ready, 1)
                pe.wait_ge(x_loaded, i * 16 + 17)
                transposed("x", x_in)
                drained("x")
                for n in range(4):
                    to = bank(f"q{n}")
                    for m in range(2):
                        p = 2 * n + m
                        for kt in range(KT):
                            mm = product(nc, to[:, m * T:m * T + T], wq, xT,
                                         lambda t, kt=kt, p=p: t[:, kt, p * P:p * P + P],
                                         lambda t, kt=kt: t[:, kt, :], kt == 0, kt == KT - 1)
                    mm.then_inc(unit_ready, 1)

                def score_pair(p):
                    if p % 2 == 0:
                        drained(f"q{p // 2}")
                    pe.wait_ge(exp_made, i * PAIRS + max(p - 1, 0) + 1)
                    for tt in range(TT):
                        for wpart, mpart in ((qT.hi, kT.hi), (qT.hi, kT.lo), (qT.lo, kT.hi)):
                            for j in range(2):
                                rows = slice(DH * j, DH * j + DH)
                                mm = nc.tensor.matmul(score[:, 2 * (p % 2) + j, tt, :],
                                                      wpart[rows, p, tt * P:tt * P + P], mpart[rows, p, :],
                                                      start=(wpart is qT.hi and mpart is kT.hi), stop=(wpart is qT.lo),
                                                      tile_position=(DH * j, 0), skip_group_check=True)
                    mm.then_inc(scores, 1)

                def weigh_values(p):
                    drained(f"t{p},1")
                    to = bank(f"o{p}")
                    for j in range(2):
                        for st in range(TT):
                            mm = product(nc, to[:, 0:T], V, PT,
                                         lambda t, st=st, j=j, p=p: t[:, st, p, j:j + 2, :].rearrange("p a d -> p (a d)"),
                                         lambda t, st=st, j=j, p=p: t[:, p % 2, 2 * j + st, :],
                                         j == 0 and st == 0, j == 1 and st == TT - 1)
                    mm.then_inc(unit_ready, 1)

                score_pair(0)
                score_pair(1)
                for p in range(PAIRS):
                    pe.wait_ge(normal, i * PAIRS + p + 2)
                    for tt in range(TT):
                        to = bank(f"t{p},{tt}")
                        for j in range(2):
                            for st in range(TT):
                                n = 2 * j + st
                                mm = nc.tensor.transpose(to[:, n * P:n * P + P], E[:, p % 2, j, tt, st * P:st * P + P],
                                                         ident[:])
                        mm.then_inc(unit_ready, 1)
                    if p + 2 < PAIRS:
                        score_pair(p + 2)
                    if p >= 1:
                        weigh_values(p - 1)
                weigh_values(PAIRS - 1)
                drained(f"o{PAIRS - 1}")
                to = bank("h")
                for m in range(KT):
                    for p in range(PAIRS):
                        mm = product(nc, to[:, m * T:m * T + T], w1, oT,
                                     lambda t, p=p, m=m: t[:, p, m * P:m * P + P],
                                     lambda t, p=p: t[:, p, :], p == 0, p == PAIRS - 1)
                mm.then_inc(unit_ready, 1)
                drained("h")
                to = bank("z")
                for tt in range(TT):
                    for kt in range(KT):
                        mm = product(nc, to[:, tt * D:tt * D + D], hT, w2,
                                     lambda t, kt=kt, tt=tt: t[:, kt, tt * P:tt * P + P],
                                     lambda t, kt=kt: t[:, kt, :], kt == 0, kt == KT - 1)
                mm.then_inc(unit_ready, 1)

        def unit_tiles(unit):
            kind = unit[0]
            if kind in "cx":
                t = cT if kind == "c" else xT
                return t, lambda part: flat(part[:]), lambda b: b
            if kind in "kq":
                t, n = (kT if kind == "k" else qT), int(unit[1])
                return t, lambda part: flat(part[:, 2 * n:2 * n + 2]), lambda b: b
            if kind == "v":
                st, half = divmod(int(unit[1]), 2)
                return (V, lambda part: part[:, st, 4 * half:4 * half + 4, 0:3:2, :],
                        lambda b: b.rearrange("p (q j d) -> p q j d", j=2, d=DH))
            if kind == "t":
                p, tt = (int(s) for s in unit[1:].split(","))
                return (PT, lambda part: part[:, p % 2, :, tt * P:tt * P + P],
                        lambda b: b.rearrange("p (n t) -> p n t", n=4))
            if kind == "o":
                return oT, lambda part: part[:, int(unit[1]), :], lambda b: b[:, 0:T]
            return hT, lambda part: flat(part[:]), lambda b: b

        @block.scalar
        def _(act):
            for n, (_, split, at, cols) in enumerate(pieces):
                act.wait_ge(w_loaded[n % 2], 16 * (n // 2 + 1))
                nc.scalar.activation(at(split.hi), stage[:, n % 2, 0:cols], ACT.Copy).then_inc(w_hi, 1)
            act.wait_ge(const_made, 5)
            with act.Fori(0, B) as i:
                def round_unit(unit):
                    split, at, view = unit_tiles(unit)
                    act.wait_ge(unit_ready, i * NU + AT[unit] + 2)
                    nc.scalar.activation(at(split.hi), view(ring[:, AT[unit] % 4]),
                                         ACT.Relu if unit == "h" else ACT.Copy).then_inc(unit_hi, 1)

                def exponentials(p):
                    act.wait_ge(bias_made, i * PAIRS + p + 2)
                    for j in range(2):
                        for tt in range(TT):
                            ins = nc.scalar.activation(E[:, p % 2, j, tt, :], score[:, 2 * (p % 2) + j, tt, :], ACT.Exp,
                                                       bias=bias[:, p % 2, j, tt:tt + 1], scale=SCALE,
                                                       accum_out=total[:, p % 2, j, tt:tt + 1])
                    ins.then_inc(exp_made, 1)

                for unit in UNITS[:AT["t0,0"]]:
                    round_unit(unit)
                exponentials(0)
                exponentials(1)
                for p in range(PAIRS):
                    round_unit(f"t{p},0")
                    round_unit(f"t{p},1")
                    if p + 2 < PAIRS:
                        exponentials(p + 2)
                    if p >= 1:
                        round_unit(f"o{p - 1}")
                round_unit(f"o{PAIRS - 1}")
                round_unit("h")

        @block.vector
        def _(ve):
            dve = nc.vector
            for n, (_, split, at, cols) in enumerate(pieces):
                ve.wait_ge(w_hi, n + 1)
                dve.tensor_tensor(at(split.lo), stage[:, n % 2, 0:cols], at(split.hi).bitcast(F32),
                                  ALU.subtract).then_inc(w_lo, 1)
            ve.wait_ge(const_made, 5)
            ve.wait_ge(gamma_loaded, 16)
            LINKS = 13
            with ve.Fori(0, B) as i:
                linked = [0]

                def link(ins):
                    linked[0] += 1
                    ins.then_inc(chain, 1)
                    ve.wait_ge(chain, i * LINKS + linked[0] + 1)

                def rest_unit(unit):
                    split, at, view = unit_tiles(unit)
                    ve.wait_ge(unit_hi, i * (NU - 1) + AT[unit] + 2)
                    src, hi, lo = view(ring[:, AT[unit] % 4]), at(split.hi).bitcast(F32), at(split.lo)
                    if unit == "h":
                        dve.scalar_tensor_tensor(out=lo, in0=src, scalar=0.0, in1=hi, op0=ALU.max,
                                                 op1=ALU.subtract).then_inc(unit_lo, 1)
                    else:
                        dve.tensor_tensor(lo, src, hi, ALU.subtract).then_inc(unit_lo, 1)

                def maxima(p):
                    ve.wait_ge(scores, i * PAIRS + p + 2)
                    link(dve.tensor_reduce(top[:, p % 2], score[:, 2 * (p % 2):2 * (p % 2) + 2], AX.X, ALU.max))
                    dve.tensor_scalar(bias[:, p % 2], top[:, p % 2], -SCALE, None, ALU.mult).then_inc(bias_made, 1)

                def reciprocals(p):
                    ve.wait_ge(exp_made, i * PAIRS + p + 2)
                    dve.reciprocal(recip[:, p % 2], total[:, p % 2]).then_inc(recip_made, 1)

                for unit in UNITS[:AT["t0,0"]]:
                    rest_unit(unit)
                maxima(0)
                maxima(1)
                reciprocals(0)
                reciprocals(1)
                for p in range(PAIRS):
                    rest_unit(f"t{p},0")
                    rest_unit(f"t{p},1")
                    if p + 2 < PAIRS:
                        maxima(p + 2)
                    if p >= 1:
                        rest_unit(f"o{p - 1}")
                    if p + 2 < PAIRS:
                        reciprocals(p + 2)
                rest_unit(f"o{PAIRS - 1}")
                rest_unit("h")

                def moments(n, src):
                    for tt in range(TT):
                        ins = dve.bn_stats(stats[:, tt], src(tt))
                    link(ins)
                    ve.sem_inc(dve_gate, 1)
                    for tt in range(TT):
                        ins = dve.bn_aggr(mv[:, tt], stats[:, tt])
                    link(ins)
                    dve.tensor_scalar(var[:, n], mv[:, :, 1], EPS, None, ALU.add).then_inc(var_made, 1)
                    ve.wait_ge(rstd_made, i * 2 + n + 2)

                bank = ring[:, AT["z"] % 4]
                ve.wait_ge(unit_ready, i * NU + AT["z"] + 2)
                moments(0, lambda tt: bank[:, tt * D:tt * D + D])
                for tt in range(TT):
                    ins = dve.tensor_scalar(y[:, tt], bank[:, tt * D:tt * D + D], mv[:, tt, 0:1], rstd[:, 0, tt:tt + 1],
                                            ALU.subtract, ALU.mult)
                ins.then_inc(unit_lo, 1)
                ve.wait_ge(unit_lo, i * NU + NU + 1)
                for tt in range(TT):
                    ins = dve.tensor_tensor(yg[:, tt], y[:, tt], gam[:], ALU.mult)
                link(ins)
                for tt in range(TT):
                    dve.tensor_tensor(z[:, tt], yg[:, tt], x_in[:, tt], ALU.add).then_inc(z_made, 1)
                ve.wait_ge(z_made, i * TT + TT + 1)
                moments(1, lambda tt: z[:, tt])
                ve.wait_ge(x_stored, i * 16 + 1)
                for tt in range(TT):
                    dve.tensor_scalar(x2[:, tt], z[:, tt], mv[:, tt, 0:1], rstd[:, 1, tt:tt + 1],
                                      ALU.subtract, ALU.mult).then_inc(x2_made, 1)
                assert linked[0] == LINKS, linked


def experts_pass(nc, x, gate_w, gate_b, w1, b1, w2, b2, out):
    BATCH, T, D = x.shape
    TOKENS = 512
    B = BATCH * T // TOKENS
    NE, _, HID = w1.shape
    KT = D // P
    HT = HID // P
    TT = TOKENS // P

    with ExitStack() as ctx:
        def sb(name, shape, dt=F32):
            return ctx.enter_context(nc.sbuf_tensor("e_" + name, shape, dt))

        def sem(name):
            return ctx.enter_context(nc.semaphore("e_" + name))

        stage = sb("stage", [P, 2, KT * HID])
        W1 = Split(sb, "w1", [P, NE, KT, HID])
        W2 = Split(sb, "w2", [P, NE, HT, D])
        gate_f = sb("gate_f", [P, KT, NE])
        GW = Split(sb, "gate_w", [P, KT, NE])
        gb = sb("gate_b", [P, NE])
        b1_cols = sb("b1", [P, NE, HT])
        b2_rows = sb("b2", [NE, D])
        ident = sb("ident", [P, P])
        neg_half = sb("neg_half", [P, TT])
        x_in = sb("x_in", [P, TT, D])
        xT = Split(sb, "xT", [P, KT, TOKENS])
        h_f = sb("h_f", [P, 2, TOKENS])
        hT = Split(sb, "hT", [P, 2, HT, TOKENS])
        logit = sb("logit", [P, TT, NE])
        peak = sb("peak", [P, TT])
        shifted = sb("shifted", [P, TT, NE])
        e = sb("e", [P, TT, NE])
        total = sb("total", [P, TT])
        recip = sb("recip", [P, TT])
        prob = sb("prob", [P, TT, 16])
        best = sb("best", [P, TT, 8])
        chosen = sb("chosen", [P, TT, 8])
        others = sb("others", [P, TT, 16])
        weight = sb("weight", [P, TT, NE])
        wT = sb("wT", [NE, TOKENS])
        acc = sb("acc", [P, TT, D])
        stats = sb("stats", [P, TT, 6])
        mv = sb("mv", [P, TT, 2])
        var = sb("var", [P, TT])
        rstd = sb("rstd", [P, TT])
        res = sb("res", [P, TT, D])

        hps = ctx.enter_context(nc.psum_tensor("e_hps", [P, 4, 512], F32))
        yps = ctx.enter_context(nc.psum_tensor("e_yps", [P, 4, 2, D], F32))

        w_loaded = [sem(f"w_loaded{n}") for n in range(2)]
        small_loaded = sem("small_loaded")
        w_hi = sem("w_hi"); w_lo = sem("w_lo"); gate_split = sem("gate_split")
        const_made = sem("const_made")
        x_loaded = sem("x_loaded"); stored = sem("stored")
        xT_ps = sem("xT_ps"); xT_hi = sem("xT_hi"); xT_lo = sem("xT_lo")
        gate_ps = sem("gate_ps"); gate_read = sem("gate_read"); shifted_made = sem("shifted_made")
        e_made = sem("e_made"); weight_made = sem("weight_made")
        wT_ps = sem("wT_ps"); wT_made = sem("wT_made"); b_ps = sem("b_ps"); acc_started = sem("acc_started")
        h_ps = sem("h_ps"); h_made = sem("h_made"); h_split = sem("h_split")
        y_ps = sem("y_ps"); y_added = sem("y_added")
        var_made = sem("var_made"); rstd_made = sem("rstd_made"); res_made = sem("res_made")
        chain = sem("chain"); dve_gate = sem("dve_gate")
        counted = [x_loaded, stored, xT_ps, xT_hi, xT_lo, gate_ps, gate_read, shifted_made, e_made, weight_made,
                   wT_ps, wT_made, b_ps, acc_started, h_ps, h_made, h_split, y_ps, y_added, var_made, rstd_made,
                   res_made, chain]

        xr = x.rearrange("(g b) (t p) d -> g p (b t) d", b=TOKENS // T, p=P)
        outr = out.rearrange("(g b) (t p) d -> g p (b t) d", b=TOKENS // T, p=P)
        flat = lambda t: t.rearrange("p k t -> p (k t)")

        pieces = []
        for n in range(NE):
            pieces.append((w1[n].rearrange("(k p) h -> p k h", p=P), W1, n, KT))
            pieces.append((w2[n].rearrange("(k p) c -> p k c", p=P), W2, n, HT))

        block = ctx.enter_context(nc.Block())

        @block.sync
        def _(sp):
            for s in counted:
                sp.sem_inc(s, 1)
            with nc.allow_non_contiguous_dma(reason="small, once"):
                sp.dma_start(b1_cols[:], b1.rearrange("e (k p) -> p e k", p=P)).then_inc(small_loaded, 16)
                sp.dma_start(gate_f[:], gate_w.rearrange("(k p) e -> p k e", p=P)).then_inc(small_loaded, 16)
            sp.dma_start(gb[:], gate_b.rearrange("(a e) -> a e", a=1).broadcast_to([P, NE])).then_inc(small_loaded, 16)
            sp.dma_start(b2_rows[:], b2).then_inc(small_loaded, 16)
            for n, (src, _, _, k) in enumerate(pieces):
                if n >= 2:
                    sp.wait_ge(w_lo, n - 1)
                sp.dma_start(stage[:, n % 2].rearrange("p (k n) -> p k n", k=k), src).then_inc(w_loaded[n % 2], 16)
            with sp.Fori(0, B) as i:
                sp.wait_ge(acc_started, i * TT + 1)
                sp.dma_start(x_in[:], xr[bass.ds(i, 1)].rearrange("a p t d -> (a p) t d")).then_inc(x_loaded, 16)
                sp.wait_ge(res_made, i * TT + TT + 1)
                for b in range(TOKENS // T):
                    t = slice(b * (T // P), (b + 1) * (T // P))
                    sp.dma_start(outr[bass.ds(i, 1)].rearrange("a p t d -> (a p) t d")[:, t], res[:, t]).then_inc(stored, 16)
            sp.wait_ge(stored, 16 * B * (TOKENS // T) + 1)

        @block.gpsimd
        def _(pool):
            build_identity(nc, pool, ident, const_made)
            nc.gpsimd.memset(neg_half[:], -0.5).then_inc(const_made, 1)
            nc.gpsimd.memset(prob[:], -1.0).then_inc(const_made, 1)
            nc.gpsimd.memset(chosen[:], -1.0).then_inc(const_made, 1)
            with pool.Fori(0, B) as i:
                pool.wait_ge(var_made, i + 2)
                nc.gpsimd.tensor_tensor(rstd[:], var[:], neg_half[:], ALU.pow).then_inc(rstd_made, 1)

        @block.tensor
        def _(pe):
            pe.wait_ge(const_made, 5)
            pe.wait_ge(small_loaded, 64)
            pe.wait_ge(gate_split, 2)
            pe.wait_ge(w_lo, len(pieces))
            with pe.Fori(0, B) as i:
                pe.wait_ge(x_loaded, i * 16 + 17)
                pe.wait_ge(h_split, i * NE * HT + 1)
                for kt in range(KT):
                    for tt in range(TT):
                        mm = nc.tensor.transpose(hps[:, kt, tt * P:tt * P + P], x_in[:, tt, kt * P:kt * P + P], ident[:])
                mm.then_inc(xT_ps, 1)
                pe.wait_ge(xT_lo, i + 2)
                for tt in range(TT):
                    for kt in range(KT):
                        mm = product(nc, hps[:, 2, tt * NE:tt * NE + NE], xT, GW,
                                     lambda t, kt=kt, tt=tt: t[:, kt, tt * P:tt * P + P],
                                     lambda t, kt=kt: t[:, kt, :], kt == 0, kt == KT - 1)
                mm.then_inc(gate_ps, 1)

                def hidden(n):
                    for m in range(HT):
                        if n == 0 and m == 2:
                            pe.wait_ge(gate_read, i + 2)
                        pe.wait_ge(h_made, i * NE * HT + max(n * HT + m - 3, 0) + 1)
                        for kt in range(KT):
                            mm = product(nc, hps[:, m, :], W1, xT,
                                         lambda t, kt=kt, m=m, n=n: t[:, n, kt, m * P:m * P + P],
                                         lambda t, kt=kt: t[:, kt, :], kt == 0, kt == KT - 1)
                        mm.then_inc(h_ps, 1)

                def combine(n):
                    pe.wait_ge(h_split, i * NE * HT + n * HT + HT + 1)
                    for pair in range(TT // 2):
                        if n >= 2:
                            pe.wait_ge(y_added, i * NE * 2 + 2 * (n - 2) + pair + 2)
                        elif n == 1:
                            pe.wait_ge(acc_started, i * TT + 2 * pair + 3)
                        else:
                            pe.wait_ge(y_added, i * NE * 2 + 1)
                        for half in range(2):
                            tt = 2 * pair + half
                            for k in range(HT):
                                mm = product(nc, yps[:, 2 * (n % 2) + pair, half, :], hT, W2,
                                             lambda t, k=k, tt=tt, n=n: t[:, n % 2, k, tt * P:tt * P + P],
                                             lambda t, k=k, n=n: t[:, n, k, :], k == 0, k == HT - 1)
                        mm.then_inc(y_ps, 1)

                hidden(0)
                pe.wait_ge(weight_made, i + 2)
                pe.wait_ge(y_added, i * NE * 2 + 1)
                for tt in range(TT):
                    mm = nc.tensor.transpose(yps[0:NE, 0, tt // 2, (tt % 2) * P:(tt % 2) * P + P], weight[:, tt, :], ident[:])
                mm.then_inc(wT_ps, 1)
                pe.wait_ge(wT_made, i + 2)
                for tt in range(TT):
                    mm = nc.tensor.matmul(yps[:, 2 + tt // 2, tt % 2, :], wT[:, tt * P:tt * P + P], b2_rows[:],
                                          start=True, stop=True, skip_group_check=True)
                mm.then_inc(b_ps, 1)
                hidden(1)
                for n in range(NE):
                    combine(n)
                    if n + 2 < NE:
                        hidden(n + 2)

        @block.scalar
        def _(act):
            act.wait_ge(small_loaded, 64)
            nc.scalar.activation(GW.hi[:], gate_f[:], ACT.Copy).then_inc(gate_split, 1)
            for n, (_, split, at, k) in enumerate(pieces):
                act.wait_ge(w_loaded[n % 2], 16 * (n // 2 + 1))
                nc.scalar.activation(flat(split.hi[:, at]), stage[:, n % 2], ACT.Copy).then_inc(w_hi, 1)
            with act.Fori(0, B) as i:
                def hidden(n):
                    for m in range(HT):
                        t = n * HT + m
                        act.wait_ge(h_ps, i * NE * HT + t + 2)
                        act.wait_ge(h_split, i * NE * HT + max(t - 1, 0) + 1)
                        nc.scalar.activation(h_f[:, t % 2], hps[:, m, :], ACT.Relu,
                                             bias=b1_cols[:, n, m:m + 1]).then_inc(h_made, 1)

                act.wait_ge(xT_ps, i + 2)
                nc.scalar.activation(xT.hi[:], hps[:, 0:KT], ACT.Copy).then_inc(xT_hi, 1)
                act.wait_ge(shifted_made, i + 2)
                nc.scalar.activation(e[:], shifted[:], ACT.Exp).then_inc(e_made, 1)
                for n in range(NE):
                    hidden(n)

        @block.vector
        def _(ve):
            dve = nc.vector
            ve.wait_ge(gate_split, 1)
            dve.tensor_tensor(GW.lo[:], gate_f[:], GW.hi[:].bitcast(F32), ALU.subtract).then_inc(gate_split, 1)
            for n, (_, split, at, k) in enumerate(pieces):
                ve.wait_ge(w_hi, n + 1)
                dve.tensor_tensor(flat(split.lo[:, at]), stage[:, n % 2], flat(split.hi[:, at]).bitcast(F32),
                                  ALU.subtract).then_inc(w_lo, 1)
            ve.wait_ge(const_made, 5)
            LINKS = 41
            with ve.Fori(0, B) as i:
                linked = [0]

                def link(ins):
                    linked[0] += 1
                    ins.then_inc(chain, 1)
                    ve.wait_ge(chain, i * LINKS + linked[0] + 1)

                def split_hidden(n):
                    for m in range(HT):
                        t = n * HT + m
                        ve.wait_ge(h_made, i * NE * HT + t + 2)
                        if m == 0:
                            ve.wait_ge(y_ps, i * NE * 2 + max(2 * (n - 1), 0) + 1)
                        hi = hT.hi[:, n % 2, m]
                        link(dve.tensor_copy(hi, h_f[:, t % 2]))
                        dve.tensor_tensor(hT.lo[:, n % 2, m], h_f[:, t % 2], hi.bitcast(F32), ALU.subtract).then_inc(h_split, 1)

                def add_expert(n):
                    for pair in range(TT // 2):
                        ve.wait_ge(y_ps, i * NE * 2 + 2 * n + pair + 2)
                        for half in range(2):
                            tt = 2 * pair + half
                            ins = dve.scalar_tensor_tensor(out=acc[:, tt], in0=yps[:, 2 * (n % 2) + pair, half, :],
                                                           scalar=weight[:, tt, n:n + 1], in1=acc[:, tt],
                                                           op0=ALU.mult, op1=ALU.add)
                        ins.then_inc(y_added, 1)

                ve.wait_ge(xT_hi, i + 2)
                dve.tensor_tensor(xT.lo[:], hps[:, 0:KT], xT.hi[:].bitcast(F32), ALU.subtract).then_inc(xT_lo, 1)
                ve.wait_ge(gate_ps, i + 2)
                gates = hps[:, 2, 0:TT * NE].rearrange("p (t e) -> p t e", e=NE)
                dve.tensor_tensor(logit[:], gates, gb[:].unsqueeze(1).broadcast_to([P, TT, NE]), ALU.add).then_inc(gate_read, 1)
                ve.wait_ge(gate_read, i + 2)
                link(dve.tensor_reduce(peak[:], logit[:], AX.X, ALU.max))
                dve.tensor_tensor(shifted[:], logit[:], peak[:].unsqueeze(2).broadcast_to([P, TT, NE]),
                                  ALU.subtract).then_inc(shifted_made, 1)
                ve.wait_ge(e_made, i + 2)
                link(dve.tensor_reduce(total[:], e[:], AX.X, ALU.add))
                link(dve.reciprocal(recip[:], total[:]))
                link(dve.tensor_tensor(prob[:, :, 0:NE], e[:], recip[:].unsqueeze(2).broadcast_to([P, TT, NE]), ALU.mult))
                ve.sem_inc(dve_gate, 1)
                for tt in range(TT):
                    ins = dve.max(best[:, tt], prob[:, tt])
                link(ins)
                link(dve.tensor_copy(chosen[:, :, 0:2], best[:, :, 0:2]))
                ve.sem_inc(dve_gate, 1)
                for tt in range(TT):
                    ins = dve.match_replace(others[:, tt], chosen[:, tt], prob[:, tt], 0.0)
                link(ins)
                dve.tensor_tensor(weight[:], prob[:, :, 0:NE], others[:, :, 0:NE], ALU.subtract).then_inc(weight_made, 1)
                split_hidden(0)
                ve.wait_ge(wT_ps, i + 2)
                dve.tensor_copy(wT[:].rearrange("p (a t) -> p a t", a=2), yps[0:NE, 0, :, :]).then_inc(wT_made, 1)
                ve.wait_ge(b_ps, i + 2)
                for tt in range(TT):
                    dve.tensor_tensor(acc[:, tt], yps[:, 2 + tt // 2, tt % 2, :], x_in[:, tt], ALU.add).then_inc(acc_started, 1)
                ve.wait_ge(acc_started, i * TT + TT + 1)
                split_hidden(1)
                for n in range(NE):
                    if n >= 1:
                        ve.wait_ge(y_added, i * NE * 2 + 2 * n + 1)
                    add_expert(n)
                    if n + 2 < NE:
                        split_hidden(n + 2)
                ve.wait_ge(y_added, i * NE * 2 + 2 * NE + 1)
                for tt in range(TT):
                    ins = dve.bn_stats(stats[:, tt], acc[:, tt])
                link(ins)
                ve.sem_inc(dve_gate, 1)
                for tt in range(TT):
                    ins = dve.bn_aggr(mv[:, tt], stats[:, tt])
                link(ins)
                dve.tensor_scalar(var[:], mv[:, :, 1], EPS, None, ALU.add).then_inc(var_made, 1)
                ve.wait_ge(rstd_made, i + 2)
                ve.wait_ge(stored, i * 16 * (TOKENS // T) + 1)
                for tt in range(TT):
                    dve.tensor_scalar(res[:, tt], acc[:, tt], mv[:, tt, 0:1], rstd[:, tt:tt + 1],
                                      ALU.subtract, ALU.mult).then_inc(res_made, 1)
                assert linked[0] == LINKS, linked



def decoder_layer(nc, x, context, wq, wf, wi, g_weight, wo, w_kv, w_q, w_out1, w_out2, gamma,
                  gate_w, gate_b, w1, b1, w2, b2, out):
    x1 = nc.dram_tensor("after_linear_attention", x.shape, F32, kind="Internal").ap()
    x2 = nc.dram_tensor("after_cross_attention", x.shape, F32, kind="Internal").ap()
    linear_attention_pass(nc, x, wq, wf, wi, g_weight, wo, x1)
    cross_attention_pass(nc, x1, context, w_kv, w_q, w_out1, w_out2, gamma, x2)
    experts_pass(nc, x2, gate_w, gate_b, w1, b1, w2, b2, out)


_INS = ["x", "ctx_1024", "L0_attn_Wq", "L0_attn_Wf", "L0_attn_Wi", "L0_attn_g_weight", "L0_attn_Wo",
        "L0_xattn_w_kv", "L0_xattn_w_q", "L0_xattn_w_out1", "L0_xattn_w_out2", "L0_xattn_gamma",
        "L0_ffn_gate_w", "L0_ffn_gate_b", "L0_ffn_w1", "L0_ffn_b1", "L0_ffn_w2", "L0_ffn_b2"]


def kernel(**inputs):
    import numpy as _np
    import concourse.bacc as _bacc
    from concourse import mybir as _mybir
    from concourse.bass_utils import run_bass_kernel_spmd as _run

    nc = _bacc.Bacc("TRN2", target_bir_lowering=False, num_devices=1)
    arrays, args = {}, []
    for name in _INS:
        a = _np.ascontiguousarray(inputs[name])
        arrays[f"in_{name}_dram"] = a
        args.append(nc.dram_tensor(f"in_{name}_dram", a.shape, _mybir.dt.from_np(a.dtype), kind="ExternalInput").ap())
    out = nc.dram_tensor("out_dram", inputs["x"].shape, _mybir.dt.float32, kind="ExternalOutput").ap()
    decoder_layer(nc, *args, out)
    r = _run(nc, [arrays], core_ids=[0])
    return r.results[0]["out_dram"]
```

```python
from contextlib import ExitStack

import concourse.bass as bass
from concourse import mybir

F32 = mybir.dt.float32
F32R = mybir.dt.float32r
I32 = mybir.dt.int32
ALU = mybir.AluOpType
ACT = mybir.ActivationFunctionType
AX = mybir.AxisListType

P = 128
EPS = 1e-5


class Split:

    def __init__(self, sb, name, shape):
        self.hi = sb(name + "_hi", shape, F32R)
        self.lo = sb(name + "_lo", shape, F32R)


def product(nc, out, w, m, w_at, m_at, first, last):
    nc.tensor.matmul(out, w_at(w.hi), m_at(m.hi), start=first, stop=False, skip_group_check=True)
    nc.tensor.matmul(out, w_at(w.hi), m_at(m.lo), start=False, stop=False, skip_group_check=True)
    return nc.tensor.matmul(out, w_at(w.lo), m_at(m.hi), start=False, stop=last, skip_group_check=True)


def build_identity(nc, pool, ident, made):
    nc.gpsimd.memset(ident[:], 0.0).then_inc(made, 1)
    pool.wait_ge(made, 1)
    nc.gpsimd.affine_select(out=ident[:], in_=ident[:], compare_op=ALU.not_equal, fill=1.0, base=0,
                            pattern=[[-1, P]], channel_multiplier=1).then_inc(made, 1)


def linear_attention_pass(nc, x, wq, wf, wi, g_weight, wo, x_out):
    B, T, D = x.shape
    H = 8
    DK = D // H
    KT = D // P
    TT = T // P
    HT = P // DK
    N = KT * T
    LEVELS = [8, 16, 32, 64, 128]
    INNER = 4
    A_MIN = 1e-8
    VS = 160
    USES = [(c, b, u) for c in range(KT) for b in range(TT) for u in ("base", "low", "high", "cross")
            if not (b == 1 and u == "cross")]
    PER_C = len(USES) // KT
    USES += [(0, 0, "squares"), (0, 0, "y")]
    NU = len(USES)
    CONSTS = 4 + 1 + INNER + 6 + 2
    assert NU % 4 == 0

    with ExitStack() as ctx:
        def sb(name, shape, dt=F32):
            return ctx.enter_context(nc.sbuf_tensor("g_" + name, shape, dt))

        def sem(name):
            return ctx.enter_context(nc.semaphore("g_" + name))

        names = ["wq", "wf", "wi", "wo"]
        W = {n: Split(sb, n, [P, KT, D]) for n in names}
        g_cols = sb("g_cols", [P, KT])
        ident = sb("ident", [P, P])
        ones_col = sb("ones_col", [P, 1])
        neg_half = sb("neg_half", [P, TT])
        base_mask = sb("base_mask", [P, P])
        level_mask = sb("level_mask", [P, INNER, P // 2])
        x_in = sb("x_in", [P, TT, D])
        xT = Split(sb, "xT", [P, KT, T])
        a = sb("a", [P, N])
        k = sb("k", [P, N])
        q = sb("q", [P, N])
        C = sb("C", [P, N])
        Dx = sb("Dx", [P, N])
        R = a
        base_f = sb("base_f", [P, 2, N])
        level_f = sb("level_f", [P, 5, 2, N // 2])
        base_k = Split(sb, "base_k", [P, KT, T])
        level_k = Split(sb, "level_k", [P, INNER, N])
        cross_k = Split(sb, "cross_k", [P, KT, P])
        base_q = sb("base_q", [P, 2, KT, T], F32R)
        level_q = sb("level_q", [P, 5, 2, KT, P], F32R)
        base_x = sb("base_x", [P, 2, KT, HT, T], F32R)
        level_x = sb("level_x", [P, 5, 2, KT, HT, P], F32R)
        V = Split(sb, "V", [P, TT, KT, HT, VS])
        A = [sb("A0", [P, KT, HT, T]), sb("A1", [P, KT, HT, P])]
        AS = [Split(sb, "AS0", [P, KT, HT, T]), Split(sb, "AS1", [P, KT, HT, P])]
        oT = Split(sb, "oT", [P, KT, T])
        sq = sb("sq", [P, KT, T])
        msq = sb("msq", [P, TT])
        rms = sb("rms", [P, TT])
        z = sb("z", [P, TT, D])
        stage = z
        stats = sb("stats", [P, TT, 6])
        mv = sb("mv", [P, TT, 2])
        var = sb("var", [P, TT])
        rstd = sb("rstd", [P, TT])

        ps = ctx.enter_context(nc.psum_tensor("g_ps", [P, 4, 512], F32))
        grp = ctx.enter_context(nc.psum_tensor("g_grp", [P, 4, 512], F32))

        loaded_w = sem("loaded_w"); const_made = sem("const_made"); pool_self = sem("pool_self")
        g_loaded = sem("g_loaded"); w_hi_made = sem("w_hi"); w_ready = sem("w_ready"); wo_made = sem("wo_made")
        x_loaded = sem("x_loaded"); res_loaded = sem("res_loaded"); x_stored = sem("x_stored"); x1_made = sem("x1_made")
        xT_ps = sem("xT_ps"); xT_hi = sem("xT_hi"); xT_lo = sem("xT_lo")
        f_ps = sem("f_ps"); q_ps = sem("q_ps"); v_ps = sem("v_ps")
        a_made = sem("a_made"); gate_made = sem("gate_made"); q_made = sem("q_made")
        v_hi = sem("v_hi"); v_lo = sem("v_lo"); k_made = sem("k_made")
        d_reset = sem("d_reset"); chain = sem("chain"); tail_chain = sem("tail_chain"); merge_chain = sem("merge_chain")
        fac_made = sem("fac_made"); fac_hi = sem("fac_hi"); fac_lo = sem("fac_lo"); spread = [sem("spread_base"), sem("spread_low"), sem("spread_high")]
        use_ready = sem("use_ready"); use_read = sem("use_read")
        A_hi = sem("A_hi"); A_lo = sem("A_lo")
        o_ps = sem("o_ps"); o_hi = sem("o_hi"); o_lo = sem("o_lo"); sq_made = sem("sq_made")
        msq_made = sem("msq_made"); rms_made = sem("rms_made")
        z_made = sem("z_made"); var_made = sem("var_made"); rstd_made = sem("rstd_made")
        counted = [x_loaded, res_loaded, x_stored, x1_made, xT_ps, xT_hi, xT_lo, f_ps, q_ps, v_ps, a_made, gate_made,
                   q_made, v_hi, v_lo, k_made, d_reset, chain, tail_chain, merge_chain, fac_made, fac_hi, fac_lo,
                   *spread, use_ready, use_read, A_hi, A_lo, o_ps, o_hi, o_lo, sq_made, msq_made, rms_made, z_made,
                   var_made, rstd_made]
        dve_gate = sem("dve_gate"); pool_gate = sem("pool_gate")
        SPREADS = HT * 16

        xr = x.rearrange("b (t p) d -> b p t d", p=P)
        outr = x_out.rearrange("b (t p) d -> b p t d", p=P)
        flat = lambda t: t.rearrange("p k t -> p (k t)")

        def half(t, h, which):
            return t.rearrange("p (n two h) -> p n two h", two=2, h=h)[:, :, which, :]

        def key_parts(n, part):
            if n == 4:
                return flat(part_of(cross_k, part)[:]), level_f[:, n, 0]
            h = LEVELS[n]
            return (half(part_of(level_k, part)[:, n], h, 0),
                    level_f[:, n, 0].rearrange("p (n h) -> p n h", h=h))

        def part_of(split, part):
            return split.hi if part == 0 else split.lo

        def element(t, n):
            return t[bass.ds(n, 1)].rearrange("a p t d -> (a p) t d")

        block = ctx.enter_context(nc.Block())

        @block.sync
        def _(sp):
            for s in counted:
                sp.sem_inc(s, 1)
            sp.dma_start(x_in[:], element(xr, 0)).then_inc(x_loaded, 16)
            with nc.allow_non_contiguous_dma(reason="256 scales, once"):
                sp.dma_start(g_cols[:], g_weight.rearrange("(k p) -> p k", p=P)).then_inc(g_loaded, 16)
            for n, w in enumerate([wq, wf, wi, wo]):
                if n:
                    sp.wait_ge(w_ready, n)
                sp.dma_start(stage[:], w.rearrange("(k p) n -> p k n", p=P)).then_inc(loaded_w, 16)

            def spread_heads(n):
                for piece, (lo, hi) in enumerate(((0, 1), (1, 4), (4, 6))):
                    sp.wait_ge(fac_lo, n * 6 + hi + 1)
                    if piece == 0:
                        sp.wait_ge(A_hi, n * 4 + 1)
                    for j in range(HT):
                        rows = slice(DK * j, DK * j + DK)
                        if piece == 0:
                            src, dst = base_q[rows], base_x[rows, :, :, j, :]
                            src = src.rearrange("p s k t -> p (s k) t")
                            dst = dst.rearrange("p s k t -> p (s k) t")
                        else:
                            src, dst = level_q[rows, lo - 1:hi - 1], level_x[rows, lo - 1:hi - 1, :, :, j, :]
                            src = src.rearrange("p n s k t -> p (n s k) t")
                            dst = dst.rearrange("p n s k t -> p (n s k) t")
                        sp.dma_start(dst.bitcast(F32), src.bitcast(F32)).then_inc(spread[piece], 16)

            def residual(n):
                sp.wait_ge(x_stored, n * 16 + 1)
                sp.dma_start(z[:], element(xr, n)).then_inc(res_loaded, 16)

            def store(n):
                sp.wait_ge(x1_made, n * TT + TT + 1)
                sp.dma_start(element(outr, n), z[:]).then_inc(x_stored, 16)

            def next_input(n):
                sp.wait_ge(xT_ps, n + 1)
                sp.dma_start(x_in[:], element(xr, n)).then_inc(x_loaded, 16)

            spread_heads(0)
            next_input(1)
            sp.wait_ge(w_ready, 4)
            with sp.Fori(0, B - 2) as i:
                residual(i)
                spread_heads(i + 1)
                next_input(i + 2)
                store(i)
            residual(B - 2)
            spread_heads(B - 1)
            store(B - 2)
            residual(B - 1)
            store(B - 1)
            sp.wait_ge(x_stored, 16 * B + 1)

        @block.gpsimd
        def _(pool):
            build_identity(nc, pool, ident, const_made)
            nc.gpsimd.memset(ones_col[:], 1.0).then_inc(const_made, 1)
            nc.gpsimd.memset(neg_half[:], -0.5).then_inc(const_made, 1)
            nc.gpsimd.memset(base_mask[:], 1.0).then_inc(pool_self, 1)
            nc.gpsimd.memset(level_mask[:], 1.0).then_inc(pool_self, 1)
            pool.wait_ge(pool_self, 2)
            nc.gpsimd.affine_select(out=base_mask[:], in_=base_mask[:], compare_op=ALU.is_ge, fill=0.0,
                                    base=0, pattern=[[1, P]], channel_multiplier=-1).then_inc(pool_self, 1)
            pool.wait_ge(pool_self, 3)
            bm = base_mask[:].rearrange("p (b e) -> p b e", e=8)
            nc.gpsimd.affine_select(out=bm, in_=bm, compare_op=ALU.is_ge, fill=0.0, base=0,
                                    pattern=[[-8, P // 8], [0, 8]], channel_multiplier=1).then_inc(const_made, 1)
            for n, h in enumerate(LEVELS[:INNER]):
                lm = level_mask[:, n].rearrange("p (b e) -> p b e", e=h)
                nc.gpsimd.affine_select(out=lm, in_=lm, compare_op=ALU.is_ge, fill=0.0, base=0,
                                        pattern=[[-2 * h, P // 2 // h], [0, h]],
                                        channel_multiplier=1).then_inc(pool_self, 1)
                pool.wait_ge(pool_self, 4 + n)
                nc.gpsimd.affine_select(out=lm, in_=lm, compare_op=ALU.is_ge, fill=0.0, base=h - 1,
                                        pattern=[[2 * h, P // 2 // h], [0, h]],
                                        channel_multiplier=-1).then_inc(const_made, 1)
            for t in (V.hi, V.lo, level_k.hi, level_k.lo, base_x, level_x):
                nc.gpsimd.memset(t[:].bitcast(F32), 0.0).then_inc(const_made, 1)
            for t in A:
                nc.gpsimd.memset(t[:], 0.0).then_inc(const_made, 1)
            pool.wait_ge(const_made, CONSTS)

            def keys(n):
                pool.wait_ge(fac_made, n * 6 + 1)
                pool.sem_inc(pool_gate, 1)
                nc.gpsimd.memset(Dx[:], 1.0).then_inc(d_reset, 1)
                pool.wait_ge(a_made, n + 2)
                pool.sem_inc(pool_gate, 1)
                nc.gpsimd.tensor_scalar(k[:], a[:], -1.0, 1.0, ALU.mult, ALU.add).then_inc(k_made, 1)

            def factor_rests(n):
                for m in range(6):
                    pool.wait_ge(fac_hi, n * 6 + m + 2)
                    if m == 0:
                        nc.gpsimd.tensor_tensor(flat(base_k.lo[:]), base_f[:, 0], flat(base_k.hi[:]).bitcast(F32), ALU.subtract)
                        nc.gpsimd.tensor_tensor(flat(base_q[:, 1]), base_f[:, 1], flat(base_q[:, 0]).bitcast(F32),
                                                ALU.subtract).then_inc(fac_lo, 1)
                    else:
                        lo, src = key_parts(m - 1, 1)
                        hi, _ = key_parts(m - 1, 0)
                        nc.gpsimd.tensor_tensor(lo, src, hi.bitcast(F32), ALU.subtract)
                        nc.gpsimd.tensor_tensor(flat(level_q[:, m - 1, 1]), level_f[:, m - 1, 1],
                                                flat(level_q[:, m - 1, 0]).bitcast(F32), ALU.subtract).then_inc(fac_lo, 1)

            def score_rests(n):
                for c in range(KT):
                    for s in range(TT):
                        pool.wait_ge(A_hi, n * 4 + c * 2 + s + 2)
                        nc.gpsimd.tensor_tensor(AS[s].lo[:, c], A[s][:, c], AS[s].hi[:, c].bitcast(F32),
                                                ALU.subtract).then_inc(A_lo, 1)

            def powers(n):
                pool.wait_ge(msq_made, n + 2)
                nc.gpsimd.tensor_tensor(rms[:], msq[:], neg_half[:], ALU.pow).then_inc(rms_made, 1)
                pool.wait_ge(var_made, n + 2)
                nc.gpsimd.tensor_tensor(rstd[:], var[:], neg_half[:], ALU.pow).then_inc(rstd_made, 1)

            keys(0)
            factor_rests(0)
            with pool.Fori(0, B - 1) as i:
                keys(i + 1)
                score_rests(i)
                factor_rests(i + 1)
                powers(i)
            score_rests(B - 1)
            powers(B - 1)

        @block.tensor
        def _(pe):
            pe.wait_ge(const_made, CONSTS)
            pe.wait_ge(w_ready, 4)

            def project(n):
                pe.wait_ge(x_loaded, n * 16 + 17)
                for kt in range(KT):
                    for tt in range(TT):
                        mm = nc.tensor.transpose(ps[:, 0, kt * T + tt * P:kt * T + tt * P + P],
                                                 x_in[:, tt, kt * P:kt * P + P], ident[:])
                mm.then_inc(xT_ps, 1)
                pe.wait_ge(xT_lo, n + 2)
                for bank, w, done, freed in ((1, "wf", f_ps, a_made), (2, "wq", q_ps, q_made)):
                    pe.wait_ge(freed, n + 1)
                    for m in range(KT):
                        for kt in range(KT):
                            mm = product(nc, ps[:, bank, m * T:m * T + T], W[w], xT,
                                         lambda t, kt=kt, m=m: t[:, kt, m * P:m * P + P],
                                         lambda t, kt=kt: t[:, kt, :], kt == 0, kt == KT - 1)
                    mm.then_inc(done, 1)

            def values(n):
                pe.wait_ge(v_lo, n * 2 + 1)
                for tt in range(TT):
                    for kt in range(KT):
                        mm = product(nc, ps[:, 3, tt * D:tt * D + D], xT, W["wi"],
                                     lambda t, kt=kt, tt=tt: t[:, kt, tt * P:tt * P + P],
                                     lambda t, kt=kt: t[:, kt, :], kt == 0, kt == KT - 1)
                mm.then_inc(v_ps, 1)

            def bank(n, u):
                pe.wait_ge(use_read, n * NU + max(u - 3, 0) + 1)
                return grp[:, u % 4]

            def scores(n):
                for u, (c, b, kind) in enumerate(USES[:KT * PER_C]):
                    to = bank(n, u)
                    if u == 0:
                        pe.wait_ge(spread[0], n * SPREADS + SPREADS + 1)
                    if u == 1:
                        pe.wait_ge(spread[1], n * SPREADS + SPREADS + 1)
                    if u == 2:
                        pe.wait_ge(spread[2], n * SPREADS + SPREADS + 1)
                    for part_k, part_q in ((0, 0), (0, 1), (1, 0)):
                        first, last = (part_k, part_q) == (0, 0), part_k == 1
                        if kind == "base":
                            mm = nc.tensor.matmul(to, part_of(base_k, part_k)[:, c, b * P:b * P + P],
                                                  base_x[:, part_q, c, :, b * P:b * P + P], start=first, stop=last,
                                                  skip_group_check=True)
                        elif kind == "cross":
                            mm = nc.tensor.matmul(to, part_of(cross_k, part_k)[:, c, :],
                                                  level_x[:, 4, part_q, c, :, :], start=first, stop=last,
                                                  skip_group_check=True)
                    if kind in ("low", "high"):
                        for m in range(2):
                            lev = m + (2 if kind == "high" else 0)
                            for part_k, part_q in ((0, 0), (0, 1), (1, 0)):
                                mm = nc.tensor.matmul(to[:, 256 * m:256 * m + 256],
                                                      part_of(level_k, part_k)[:, lev, c * T + b * P:c * T + b * P + P],
                                                      level_x[:, lev, part_q, c, :, b * 64:b * 64 + 64],
                                                      start=(part_k, part_q) == (0, 0), stop=part_k == 1,
                                                      skip_group_check=True)
                    mm.then_inc(use_ready, 1)

            def weigh_values(n):
                pe.wait_ge(v_lo, n * 2 + 3)
                pe.wait_ge(xT_lo, n + 2)
                for c in range(KT):
                    pe.wait_ge(A_lo, n * 4 + 2 * c + 3)
                    for s in range(TT):
                        for j in range(HT):
                            mm = product(nc, ps[:, 0, c * T + s * P:c * T + T], V, AS[s],
                                         lambda t, c=c, s=s, j=j: t[:, s, c].rearrange("p j v -> p (j v)")[:, P * j:P * j + P],
                                         lambda t, c=c, j=j: t[:, c, j, :],
                                         s == 0 and j == 0, s == TT - 1 and j == HT - 1)
                mm.then_inc(o_ps, 1)

            def outputs(n):
                to = bank(n, NU - 2)
                pe.wait_ge(sq_made, n + 2)
                for tt in range(TT):
                    for c in range(KT):
                        mm = nc.tensor.matmul(to[:, tt:tt + 1], sq[:, c, tt * P:tt * P + P], ones_col[:],
                                              start=(c == 0), stop=(c == KT - 1), skip_group_check=True)
                mm.then_inc(use_ready, 1)
                to = bank(n, NU - 1)
                pe.wait_ge(o_lo, n + 2)
                for tt in range(TT):
                    for c in range(KT):
                        mm = product(nc, to[:, tt * D:tt * D + D], oT, W["wo"],
                                     lambda t, c=c, tt=tt: t[:, c, tt * P:tt * P + P],
                                     lambda t, c=c: t[:, c, :], c == 0, c == KT - 1)
                mm.then_inc(use_ready, 1)

            project(0)
            values(0)
            with pe.Fori(0, B - 1) as i:
                project(i + 1)
                scores(i)
                weigh_values(i)
                values(i + 1)
                outputs(i)
            scores(B - 1)
            weigh_values(B - 1)
            outputs(B - 1)

        @block.scalar
        def _(act):
            for n, name in enumerate(names):
                act.wait_ge(loaded_w, 16 * (n + 1))
                if name == "wo":
                    act.wait_ge(wo_made, KT)
                nc.scalar.activation(W[name].hi[:], stage[:], ACT.Copy).then_inc(w_hi_made, 1)
            act.wait_ge(const_made, CONSTS)

            def gates(n):
                act.wait_ge(xT_ps, n + 2)
                nc.scalar.activation(flat(xT.hi[:]), ps[:, 0], ACT.Copy).then_inc(xT_hi, 1)
                act.wait_ge(f_ps, n + 2)
                act.wait_ge(fac_made, n * 6 + 1)
                nc.scalar.activation(a[:], ps[:, 1], ACT.Sigmoid).then_inc(a_made, 1)
                act.wait_ge(q_ps, n + 2)
                nc.scalar.activation(q[:], ps[:, 2], ACT.Sigmoid).then_inc(gate_made, 1)

            def value_round(n):
                act.wait_ge(v_ps, n + 2)
                for tt in range(TT):
                    nc.scalar.activation(V.hi[:, tt, :, :, 0:DK],
                                         ps[:, 3, tt * D:tt * D + D].rearrange("p (c j d) -> p c j d", c=KT, d=DK),
                                         ACT.Copy).then_inc(v_hi, 1)

            def factor_round(n):
                for s in spread:
                    act.wait_ge(s, n * SPREADS + 1)
                for m in range(6):
                    act.wait_ge(fac_made, n * 6 + m + 2)
                    if m == 0:
                        nc.scalar.activation(flat(base_k.hi[:]), base_f[:, 0], ACT.Copy)
                        nc.scalar.activation(flat(base_q[:, 0]), base_f[:, 1], ACT.Copy).then_inc(fac_hi, 1)
                    else:
                        hi, src = key_parts(m - 1, 0)
                        nc.scalar.activation(hi, src, ACT.Copy)
                        nc.scalar.activation(flat(level_q[:, m - 1, 0]), level_f[:, m - 1, 1], ACT.Copy).then_inc(fac_hi, 1)

            def score_round(n):
                act.wait_ge(o_ps, n + 1)
                for c in range(KT):
                    act.wait_ge(use_read, n * NU + (c + 1) * PER_C + 1)
                    for s in range(TT):
                        nc.scalar.activation(AS[s].hi[:, c], A[s][:, c], ACT.Copy).then_inc(A_hi, 1)

            def output_round(n):
                act.wait_ge(o_ps, n + 2)
                nc.scalar.activation(flat(oT.hi[:]), ps[:, 0], ACT.Copy).then_inc(o_hi, 1)
                nc.scalar.activation(flat(sq[:]), ps[:, 0], ACT.Square).then_inc(sq_made, 1)

            gates(0)
            value_round(0)
            factor_round(0)
            with act.Fori(0, B - 1) as i:
                gates(i + 1)
                score_round(i)
                factor_round(i + 1)
                output_round(i)
                value_round(i + 1)
            score_round(B - 1)
            output_round(B - 1)

        @block.vector
        def _(ve):
            dve = nc.vector
            ve.wait_ge(g_loaded, 16)
            for n, name in enumerate(names):
                if name == "wo":
                    ve.wait_ge(loaded_w, 64)
                    for kt in range(KT):
                        dve.tensor_scalar(stage[:, kt], stage[:, kt], g_cols[:, kt:kt + 1], None, ALU.mult).then_inc(wo_made, 1)
                ve.wait_ge(w_hi_made, n + 1)
                dve.tensor_tensor(W[name].lo[:], stage[:], W[name].hi[:].bitcast(F32), ALU.subtract).then_inc(w_ready, 1)
            ve.wait_ge(const_made, CONSTS)

            def linker(sem_, n, total):
                linked = [0]

                def link(ins):
                    linked[0] += 1
                    assert linked[0] <= total
                    ins.then_inc(sem_, 1)
                    ve.wait_ge(sem_, n * total + linked[0] + 1)
                return link

            def x_rest(n):
                ve.wait_ge(xT_hi, n + 2)
                dve.tensor_tensor(flat(xT.lo[:]), ps[:, 0], flat(xT.hi[:]).bitcast(F32), ALU.subtract).then_inc(xT_lo, 1)

            def factors(n):
                link = linker(chain, n, 16)
                shape = lambda h: [P, N // (2 * h), h]
                ve.wait_ge(gate_made, n + 2)
                dve.scalar_tensor_tensor(out=q[:], in0=ps[:, 2], scalar=float(DK) ** -0.5, in1=q[:],
                                         op0=ALU.mult, op1=ALU.mult).then_inc(q_made, 1)
                link(dve.tensor_scalar(C[:], a[:], A_MIN, None, ALU.max))
                ve.wait_ge(d_reset, n + 2)

                def grow(h):
                    c1 = half(C[:], h, 1)
                    if h > 1:
                        link(dve.tensor_tensor(half(Dx[:], h, 0), half(Dx[:], h, 0),
                                               c1[:, :, h - 1:h].broadcast_to(shape(h)), ALU.mult))
                    else:
                        link(dve.tensor_copy(half(Dx[:], h, 0), c1))
                    link(dve.tensor_tensor(c1, c1, half(C[:], h, 0)[:, :, h - 1:h].broadcast_to(shape(h)), ALU.mult))

                for h in (1, 2):
                    grow(h)
                ve.wait_ge(k_made, n + 2)
                dve.reciprocal(half(R[:], 4, 0), half(Dx[:], 4, 0))
                link(dve.reciprocal(half(R[:], 4, 1), half(C[:], 4, 1)))
                ve.wait_ge(fac_lo, n * 6 + 1)
                ve.wait_ge(q_made, n + 2)
                for side, t, f0, f1 in ((0, k, Dx, R), (1, q, R, C)):
                    for w, f in ((0, f0), (1, f1)):
                        ins = dve.tensor_tensor(half(base_f[:, side], 4, w), half(t[:], 4, w), half(f[:], 4, w), ALU.mult)
                ins.then_inc(fac_made, 1)
                ve.wait_ge(fac_made, n * 6 + 2)
                grow(4)
                for m, h in enumerate(LEVELS):
                    dve.tensor_tensor(level_f[:, m, 0].rearrange("p (n h) -> p n h", h=h), half(k[:], h, 0),
                                      half(Dx[:], h, 0), ALU.mult)
                    dve.tensor_tensor(level_f[:, m, 1].rearrange("p (n h) -> p n h", h=h), half(q[:], h, 1),
                                      half(C[:], h, 1), ALU.mult).then_inc(fac_made, 1)
                    if h < LEVELS[-1]:
                        ve.wait_ge(fac_made, n * 6 + m + 3)
                        grow(h)

            def value_rest(n):
                ve.wait_ge(v_hi, n * 2 + 3)
                for tt in range(TT):
                    dve.tensor_tensor(V.lo[:, tt, :, :, 0:DK],
                                      ps[:, 3, tt * D:tt * D + D].rearrange("p (c j d) -> p c j d", c=KT, d=DK),
                                      V.hi[:, tt, :, :, 0:DK].bitcast(F32), ALU.subtract).then_inc(v_lo, 1)

            def merge(n):
                link = linker(merge_chain, n, 8)
                ve.wait_ge(A_lo, n * 4 + 1)
                for u, (c, b, kind) in enumerate(USES[:KT * PER_C]):
                    tile = A[b][:, c, :, 0:P]
                    bank = grp[:, u % 4]
                    ve.wait_ge(use_ready, n * NU + u + 2)
                    if kind == "cross":
                        dve.tensor_copy(A[0][:, c, :, P:2 * P], bank.rearrange("p (j t) -> p j t", j=HT)).then_inc(use_read, 1)
                        continue
                    if kind != "base":
                        ve.wait_ge(use_read, n * NU + u + 1)
                    ve.sem_inc(dve_gate, 1)
                    if kind == "base":
                        mask = base_mask[:].unsqueeze(1).broadcast_to([P, HT, P]).bitcast(I32)
                        dve.copy_predicated(tile, mask, bank.rearrange("p (j t) -> p j t", j=HT)).then_inc(use_read, 1)
                        continue
                    for m in range(2):
                        lev = m + (2 if kind == "high" else 0)
                        h = LEVELS[lev]
                        to = tile.rearrange("p j (n two h) -> p j n two h", two=2, h=h)[:, :, :, 1, :]
                        data = bank[:, 256 * m:256 * m + 256].rearrange("p (j n h) -> p j n h", j=HT, h=h)
                        mask = level_mask[:, lev].rearrange("p (n h) -> p n h", h=h).unsqueeze(1)
                        mask = mask.broadcast_to([P, HT, P // 2 // h, h]).bitcast(I32)
                        ins = dve.copy_predicated(to, mask, data)
                        if m == 0:
                            link(ins)
                            ve.sem_inc(dve_gate, 1)
                    ins.then_inc(use_read, 1)

            def output_rest(n):
                ve.wait_ge(o_hi, n + 2)
                ve.wait_ge(sq_made, n + 2)
                dve.tensor_tensor(flat(oT.lo[:]), ps[:, 0], flat(oT.hi[:]).bitcast(F32), ALU.subtract).then_inc(o_lo, 1)

            def normalise(n):
                link = linker(tail_chain, n, 2)
                ve.wait_ge(use_ready, n * NU + NU)
                dve.tensor_scalar(msq[:], grp[:, (NU - 2) % 4, 0:TT], 1.0 / D, EPS, ALU.mult, ALU.add).then_inc(msq_made, 1)
                ve.wait_ge(msq_made, n + 2)
                ve.sem_inc(use_read, 1)
                ve.wait_ge(use_ready, n * NU + NU + 1)
                ve.wait_ge(rms_made, n + 2)
                ve.wait_ge(res_loaded, n * 16 + 17)
                for tt in range(TT):
                    dve.scalar_tensor_tensor(out=z[:, tt], in0=grp[:, (NU - 1) % 4, tt * D:tt * D + D],
                                             scalar=rms[:, tt:tt + 1], in1=z[:, tt],
                                             op0=ALU.mult, op1=ALU.add).then_inc(z_made, 1)
                ve.wait_ge(z_made, n * 2 + 3)
                ve.sem_inc(use_read, 1)
                for tt in range(TT):
                    ins = dve.bn_stats(stats[:, tt], z[:, tt])
                link(ins)
                ve.sem_inc(dve_gate, 1)
                for tt in range(TT):
                    ins = dve.bn_aggr(mv[:, tt], stats[:, tt])
                link(ins)
                dve.tensor_scalar(var[:], mv[:, :, 1], EPS, None, ALU.add).then_inc(var_made, 1)
                ve.wait_ge(rstd_made, n + 2)
                for tt in range(TT):
                    dve.tensor_scalar(z[:, tt], z[:, tt], mv[:, tt, 0:1], rstd[:, tt:tt + 1],
                                      ALU.subtract, ALU.mult).then_inc(x1_made, 1)

            x_rest(0)
            value_rest(0)
            factors(0)
            with ve.Fori(0, B - 1) as i:
                x_rest(i + 1)
                merge(i)
                factors(i + 1)
                output_rest(i)
                value_rest(i + 1)
                normalise(i)
            merge(B - 1)
            output_rest(B - 1)
            normalise(B - 1)


def cross_attention_pass(nc, x, context, w_kv, w_q, w_out1, w_out2, gamma, x_out):
    B, T, D = x.shape
    INNER = w_q.shape[1]
    DH = 64
    PAIRS = INNER // P
    KT = D // P
    TT = T // P
    SCALE = float(DH) ** -0.5

    UNITS = ["c"] + [f"k{n}" for n in range(4)] + [f"v{n}" for n in range(4)] + ["x"] + [f"q{n}" for n in range(4)]
    UNITS += ["t0,0", "t0,1"]
    for p in range(1, PAIRS):
        UNITS += [f"t{p},0", f"t{p},1", f"o{p - 1}"]
    UNITS += [f"o{PAIRS - 1}", "h", "z"]
    NU = len(UNITS)
    assert NU % 4 == 0
    AT = {u: n for n, u in enumerate(UNITS)}

    with ExitStack() as ctx:
        def sb(name, shape, dt=F32):
            return ctx.enter_context(nc.sbuf_tensor("c_" + name, shape, dt))

        def sem(name):
            return ctx.enter_context(nc.semaphore("c_" + name))

        stage = sb("stage", [P, 2, 2048])
        wkv = Split(sb, "wkv", [P, KT, 2 * INNER])
        wq = Split(sb, "wq", [P, KT, INNER])
        w1 = Split(sb, "w1", [P, PAIRS, D])
        w2 = Split(sb, "w2", [P, KT, D])
        gam = sb("gamma", [P, D])
        ident = sb("ident", [P, P])
        neg_half = sb("neg_half", [P, TT])
        c_in = sb("c_in", [P, TT, D])
        x_in = sb("x_in", [P, TT, D])
        cT = Split(sb, "cT", [P, KT, T])
        xT = Split(sb, "xT", [P, KT, T])
        kT = Split(sb, "kT", [P, PAIRS, T])
        qT = Split(sb, "qT", [P, PAIRS, T])
        V = Split(sb, "V", [P, TT, PAIRS, 3, DH])
        E = sb("E", [P, 2, 2, TT, T])
        PT = Split(sb, "PT", [P, 2, 4, T])
        oT = Split(sb, "oT", [P, PAIRS, T])
        hT = Split(sb, "hT", [P, KT, T])
        top = sb("top", [P, 2, 2, TT])
        bias = sb("bias", [P, 2, 2, TT])
        total = sb("total", [P, 2, 2, TT])
        recip = sb("recip", [P, 2, 2, TT])
        stats = sb("stats", [P, TT, 6])
        mv = sb("mv", [P, TT, 2])
        var = sb("var", [P, 2, TT])
        rstd = sb("rstd", [P, 2, TT])
        y = sb("y", [P, TT, D])
        yg = sb("yg", [P, TT, D])
        z = sb("z", [P, TT, D])
        x2 = sb("x2", [P, TT, D])

        ring = ctx.enter_context(nc.psum_tensor("c_ring", [P, 4, 512], F32))
        score = ctx.enter_context(nc.psum_tensor("c_score", [P, 4, TT, T], F32))

        w_loaded = [sem(f"w_loaded{n}") for n in range(2)]
        w_hi = sem("w_hi"); w_lo = sem("w_lo"); gamma_loaded = sem("gamma_loaded")
        const_made = sem("const_made")
        c_loaded = sem("c_loaded"); x_loaded = sem("x_loaded"); x_stored = sem("x_stored")
        unit_ready = sem("unit_ready"); unit_hi = sem("unit_hi"); unit_lo = sem("unit_lo")
        scores = sem("scores"); bias_made = sem("bias_made"); exp_made = sem("exp_made")
        recip_made = sem("recip_made"); normal = sem("normal")
        chain = sem("chain"); z_made = sem("z_made"); var_made = sem("var_made"); rstd_made = sem("rstd_made")
        x2_made = sem("x2_made")
        dve_gate = sem("dve_gate"); pool_gate = sem("pool_gate")
        counted = [c_loaded, x_loaded, x_stored, unit_ready, unit_hi, unit_lo, scores, bias_made, exp_made,
                   recip_made, normal, chain, z_made, var_made, rstd_made, x2_made]

        xr = x.rearrange("b (t p) d -> b p t d", p=P)
        cr = context.rearrange("b (t p) d -> b p t d", p=P)
        outr = x_out.rearrange("b (t p) d -> b p t d", p=P)
        flat = lambda t: t.rearrange("p k t -> p (k t)")

        kvr = w_kv.rearrange("(k p) n -> p k n", p=P)
        pieces = [(kvr[:, k], wkv, (lambda t, k=k: t[:, k, :]), 2048) for k in range(KT)]
        pieces += [(w_q.rearrange("(k p) n -> p k n", p=P), wq, lambda t: flat(t[:]), 2048)]
        pieces += [(w_out1.rearrange("(k p) n -> p k n", p=P), w1, lambda t: flat(t[:]), 2048)]
        pieces += [(w_out2.rearrange("(k p) n -> p k n", p=P), w2, lambda t: flat(t[:]), 512)]

        block = ctx.enter_context(nc.Block())

        @block.sync
        def _(sp):
            for s in counted:
                sp.sem_inc(s, 1)
            sp.dma_start(gam[:], gamma.rearrange("(a d) -> a d", a=1).broadcast_to([P, D])).then_inc(gamma_loaded, 16)
            for n, (src, _, _, cols) in enumerate(pieces):
                if n >= 2:
                    sp.wait_ge(w_lo, n - 1)
                dst = stage[:, n % 2, 0:cols]
                if len(src.shape) == 3:
                    dst = dst.rearrange("p (k n) -> p k n", k=src.shape[1])
                sp.dma_start(dst, src).then_inc(w_loaded[n % 2], 16)
            with sp.Fori(0, B) as i:
                sp.wait_ge(unit_ready, i * NU + 1)
                sp.dma_start(c_in[:], cr[bass.ds(i, 1)].rearrange("a p t d -> (a p) t d")).then_inc(c_loaded, 16)
                sp.wait_ge(z_made, i * TT + 1)
                sp.dma_start(x_in[:], xr[bass.ds(i, 1)].rearrange("a p t d -> (a p) t d")).then_inc(x_loaded, 16)
                sp.wait_ge(x2_made, i * TT + TT + 1)
                sp.dma_start(outr[bass.ds(i, 1)].rearrange("a p t d -> (a p) t d"), x2[:]).then_inc(x_stored, 16)
            sp.wait_ge(x_stored, 16 * B + 1)

        @block.gpsimd
        def _(pool):
            build_identity(nc, pool, ident, const_made)
            nc.gpsimd.memset(neg_half[:], -0.5).then_inc(const_made, 1)
            for t in (V.hi, V.lo):
                nc.gpsimd.memset(t[:].bitcast(F32), 0.0).then_inc(const_made, 1)
            with pool.Fori(0, B) as i:
                for p in range(PAIRS):
                    for j in range(2):
                        for tt in range(TT):
                            if j == 0 and tt == 0:
                                pool.wait_ge(recip_made, i * PAIRS + p + 2)
                                pool.sem_inc(pool_gate, 1)
                            e = E[:, p % 2, j, tt, :]
                            ins = nc.gpsimd.tensor_scalar(e, e, recip[:, p % 2, j, tt:tt + 1], 1.0, ALU.mult, ALU.mult)
                    ins.then_inc(normal, 1)
                for n in range(2):
                    pool.wait_ge(var_made, i * 2 + n + 2)
                    nc.gpsimd.tensor_tensor(rstd[:, n], var[:, n], neg_half[:], ALU.pow).then_inc(rstd_made, 1)

        @block.tensor
        def _(pe):
            pe.wait_ge(const_made, 5)
            pe.wait_ge(w_lo, len(pieces))
            with pe.Fori(0, B) as i:
                def bank(unit):
                    n = AT[unit]
                    pe.wait_ge(unit_lo, i * NU + max(n - 3, 0) + 1)
                    return ring[:, n % 4]

                def transposed(unit, src):
                    to = bank(unit)
                    for kt in range(KT):
                        for tt in range(TT):
                            mm = nc.tensor.transpose(to[:, kt * T + tt * P:kt * T + tt * P + P],
                                                     src[:, tt, kt * P:kt * P + P], ident[:])
                    mm.then_inc(unit_ready, 1)

                def drained(unit):
                    pe.wait_ge(unit_lo, i * NU + AT[unit] + 2)

                pe.wait_ge(c_loaded, i * 16 + 17)
                transposed("c", c_in)
                drained("c")
                for n in range(4):
                    to = bank(f"k{n}")
                    for m in range(2):
                        p = 2 * n + m
                        for kt in range(KT):
                            mm = product(nc, to[:, m * T:m * T + T], wkv, cT,
                                         lambda t, kt=kt, p=p: t[:, kt, p * P:p * P + P],
                                         lambda t, kt=kt: t[:, kt, :], kt == 0, kt == KT - 1)
                    mm.then_inc(unit_ready, 1)
                for n in range(4):
                    to = bank(f"v{n}")
                    st, half = divmod(n, 2)
                    for kt in range(KT):
                        mm = product(nc, to[:, :], cT, wkv,
                                     lambda t, kt=kt, st=st: t[:, kt, st * P:st * P + P],
                                     lambda t, kt=kt, half=half: t[:, kt, INNER + half * 512:INNER + half * 512 + 512],
                                     kt == 0, kt == KT - 1)
                    mm.then_inc(unit_ready, 1)
                pe.wait_ge(x_loaded, i * 16 + 17)
                transposed("x", x_in)
                drained("x")
                for n in range(4):
                    to = bank(f"q{n}")
                    for m in range(2):
                        p = 2 * n + m
                        for kt in range(KT):
                            mm = product(nc, to[:, m * T:m * T + T], wq, xT,
                                         lambda t, kt=kt, p=p: t[:, kt, p * P:p * P + P],
                                         lambda t, kt=kt: t[:, kt, :], kt == 0, kt == KT - 1)
                    mm.then_inc(unit_ready, 1)

                def score_pair(p):
                    if p % 2 == 0:
                        drained(f"q{p // 2}")
                    pe.wait_ge(exp_made, i * PAIRS + max(p - 1, 0) + 1)
                    for tt in range(TT):
                        for wpart, mpart in ((qT.hi, kT.hi), (qT.hi, kT.lo), (qT.lo, kT.hi)):
                            for j in range(2):
                                rows = slice(DH * j, DH * j + DH)
                                mm = nc.tensor.matmul(score[:, 2 * (p % 2) + j, tt, :],
                                                      wpart[rows, p, tt * P:tt * P + P], mpart[rows, p, :],
                                                      start=(wpart is qT.hi and mpart is kT.hi), stop=(wpart is qT.lo),
                                                      tile_position=(DH * j, 0), skip_group_check=True)
                    mm.then_inc(scores, 1)

                def weigh_values(p):
                    drained(f"t{p},1")
                    to = bank(f"o{p}")
                    for j in range(2):
                        for st in range(TT):
                            mm = product(nc, to[:, 0:T], V, PT,
                                         lambda t, st=st, j=j, p=p: t[:, st, p, j:j + 2, :].rearrange("p a d -> p (a d)"),
                                         lambda t, st=st, j=j, p=p: t[:, p % 2, 2 * j + st, :],
                                         j == 0 and st == 0, j == 1 and st == TT - 1)
                    mm.then_inc(unit_ready, 1)

                score_pair(0)
                score_pair(1)
                for p in range(PAIRS):
                    pe.wait_ge(normal, i * PAIRS + p + 2)
                    for tt in range(TT):
                        to = bank(f"t{p},{tt}")
                        for j in range(2):
                            for st in range(TT):
                                n = 2 * j + st
                                mm = nc.tensor.transpose(to[:, n * P:n * P + P], E[:, p % 2, j, tt, st * P:st * P + P],
                                                         ident[:])
                        mm.then_inc(unit_ready, 1)
                    if p + 2 < PAIRS:
                        score_pair(p + 2)
                    if p >= 1:
                        weigh_values(p - 1)
                weigh_values(PAIRS - 1)
                drained(f"o{PAIRS - 1}")
                to = bank("h")
                for m in range(KT):
                    for p in range(PAIRS):
                        mm = product(nc, to[:, m * T:m * T + T], w1, oT,
                                     lambda t, p=p, m=m: t[:, p, m * P:m * P + P],
                                     lambda t, p=p: t[:, p, :], p == 0, p == PAIRS - 1)
                mm.then_inc(unit_ready, 1)
                drained("h")
                to = bank("z")
                for tt in range(TT):
                    for kt in range(KT):
                        mm = product(nc, to[:, tt * D:tt * D + D], hT, w2,
                                     lambda t, kt=kt, tt=tt: t[:, kt, tt * P:tt * P + P],
                                     lambda t, kt=kt: t[:, kt, :], kt == 0, kt == KT - 1)
                mm.then_inc(unit_ready, 1)

        def unit_tiles(unit):
            kind = unit[0]
            if kind in "cx":
                t = cT if kind == "c" else xT
                return t, lambda part: flat(part[:]), lambda b: b
            if kind in "kq":
                t, n = (kT if kind == "k" else qT), int(unit[1])
                return t, lambda part: flat(part[:, 2 * n:2 * n + 2]), lambda b: b
            if kind == "v":
                st, half = divmod(int(unit[1]), 2)
                return (V, lambda part: part[:, st, 4 * half:4 * half + 4, 0:3:2, :],
                        lambda b: b.rearrange("p (q j d) -> p q j d", j=2, d=DH))
            if kind == "t":
                p, tt = (int(s) for s in unit[1:].split(","))
                return (PT, lambda part: part[:, p % 2, :, tt * P:tt * P + P],
                        lambda b: b.rearrange("p (n t) -> p n t", n=4))
            if kind == "o":
                return oT, lambda part: part[:, int(unit[1]), :], lambda b: b[:, 0:T]
            return hT, lambda part: flat(part[:]), lambda b: b

        @block.scalar
        def _(act):
            for n, (_, split, at, cols) in enumerate(pieces):
                act.wait_ge(w_loaded[n % 2], 16 * (n // 2 + 1))
                nc.scalar.activation(at(split.hi), stage[:, n % 2, 0:cols], ACT.Copy).then_inc(w_hi, 1)
            act.wait_ge(const_made, 5)
            with act.Fori(0, B) as i:
                def round_unit(unit):
                    split, at, view = unit_tiles(unit)
                    act.wait_ge(unit_ready, i * NU + AT[unit] + 2)
                    nc.scalar.activation(at(split.hi), view(ring[:, AT[unit] % 4]),
                                         ACT.Relu if unit == "h" else ACT.Copy).then_inc(unit_hi, 1)

                def exponentials(p):
                    act.wait_ge(bias_made, i * PAIRS + p + 2)
                    for j in range(2):
                        for tt in range(TT):
                            ins = nc.scalar.activation(E[:, p % 2, j, tt, :], score[:, 2 * (p % 2) + j, tt, :], ACT.Exp,
                                                       bias=bias[:, p % 2, j, tt:tt + 1], scale=SCALE,
                                                       accum_out=total[:, p % 2, j, tt:tt + 1])
                    ins.then_inc(exp_made, 1)

                for unit in UNITS[:AT["t0,0"]]:
                    round_unit(unit)
                exponentials(0)
                exponentials(1)
                for p in range(PAIRS):
                    round_unit(f"t{p},0")
                    round_unit(f"t{p},1")
                    if p + 2 < PAIRS:
                        exponentials(p + 2)
                    if p >= 1:
                        round_unit(f"o{p - 1}")
                round_unit(f"o{PAIRS - 1}")
                round_unit("h")

        @block.vector
        def _(ve):
            dve = nc.vector
            for n, (_, split, at, cols) in enumerate(pieces):
                ve.wait_ge(w_hi, n + 1)
                dve.tensor_tensor(at(split.lo), stage[:, n % 2, 0:cols], at(split.hi).bitcast(F32),
                                  ALU.subtract).then_inc(w_lo, 1)
            ve.wait_ge(const_made, 5)
            ve.wait_ge(gamma_loaded, 16)
            LINKS = 13
            with ve.Fori(0, B) as i:
                linked = [0]

                def link(ins):
                    linked[0] += 1
                    ins.then_inc(chain, 1)
                    ve.wait_ge(chain, i * LINKS + linked[0] + 1)

                def rest_unit(unit):
                    split, at, view = unit_tiles(unit)
                    ve.wait_ge(unit_hi, i * (NU - 1) + AT[unit] + 2)
                    src, hi, lo = view(ring[:, AT[unit] % 4]), at(split.hi).bitcast(F32), at(split.lo)
                    if unit == "h":
                        dve.scalar_tensor_tensor(out=lo, in0=src, scalar=0.0, in1=hi, op0=ALU.max,
                                                 op1=ALU.subtract).then_inc(unit_lo, 1)
                    else:
                        dve.tensor_tensor(lo, src, hi, ALU.subtract).then_inc(unit_lo, 1)

                def maxima(p):
                    ve.wait_ge(scores, i * PAIRS + p + 2)
                    link(dve.tensor_reduce(top[:, p % 2], score[:, 2 * (p % 2):2 * (p % 2) + 2], AX.X, ALU.max))
                    dve.tensor_scalar(bias[:, p % 2], top[:, p % 2], -SCALE, None, ALU.mult).then_inc(bias_made, 1)

                def reciprocals(p):
                    ve.wait_ge(exp_made, i * PAIRS + p + 2)
                    dve.reciprocal(recip[:, p % 2], total[:, p % 2]).then_inc(recip_made, 1)

                for unit in UNITS[:AT["t0,0"]]:
                    rest_unit(unit)
                maxima(0)
                maxima(1)
                reciprocals(0)
                reciprocals(1)
                for p in range(PAIRS):
                    rest_unit(f"t{p},0")
                    rest_unit(f"t{p},1")
                    if p + 2 < PAIRS:
                        maxima(p + 2)
                    if p >= 1:
                        rest_unit(f"o{p - 1}")
                    if p + 2 < PAIRS:
                        reciprocals(p + 2)
                rest_unit(f"o{PAIRS - 1}")
                rest_unit("h")

                def moments(n, src):
                    for tt in range(TT):
                        ins = dve.bn_stats(stats[:, tt], src(tt))
                    link(ins)
                    ve.sem_inc(dve_gate, 1)
                    for tt in range(TT):
                        ins = dve.bn_aggr(mv[:, tt], stats[:, tt])
                    link(ins)
                    dve.tensor_scalar(var[:, n], mv[:, :, 1], EPS, None, ALU.add).then_inc(var_made, 1)
                    ve.wait_ge(rstd_made, i * 2 + n + 2)

                bank = ring[:, AT["z"] % 4]
                ve.wait_ge(unit_ready, i * NU + AT["z"] + 2)
                moments(0, lambda tt: bank[:, tt * D:tt * D + D])
                for tt in range(TT):
                    ins = dve.tensor_scalar(y[:, tt], bank[:, tt * D:tt * D + D], mv[:, tt, 0:1], rstd[:, 0, tt:tt + 1],
                                            ALU.subtract, ALU.mult)
                ins.then_inc(unit_lo, 1)
                ve.wait_ge(unit_lo, i * NU + NU + 1)
                for tt in range(TT):
                    ins = dve.tensor_tensor(yg[:, tt], y[:, tt], gam[:], ALU.mult)
                link(ins)
                for tt in range(TT):
                    dve.tensor_tensor(z[:, tt], yg[:, tt], x_in[:, tt], ALU.add).then_inc(z_made, 1)
                ve.wait_ge(z_made, i * TT + TT + 1)
                moments(1, lambda tt: z[:, tt])
                ve.wait_ge(x_stored, i * 16 + 1)
                for tt in range(TT):
                    dve.tensor_scalar(x2[:, tt], z[:, tt], mv[:, tt, 0:1], rstd[:, 1, tt:tt + 1],
                                      ALU.subtract, ALU.mult).then_inc(x2_made, 1)
                assert linked[0] == LINKS, linked


def experts_pass(nc, x, gate_w, gate_b, w1, b1, w2, b2, out):
    BATCH, T, D = x.shape
    TOKENS = 512
    B = BATCH * T // TOKENS
    NE, _, HID = w1.shape
    KT = D // P
    HT = HID // P
    TT = TOKENS // P

    with ExitStack() as ctx:
        def sb(name, shape, dt=F32):
            return ctx.enter_context(nc.sbuf_tensor("e_" + name, shape, dt))

        def sem(name):
            return ctx.enter_context(nc.semaphore("e_" + name))

        stage = sb("stage", [P, 2, KT * HID])
        W1 = Split(sb, "w1", [P, NE, KT, HID])
        W2 = Split(sb, "w2", [P, NE, HT, D])
        gate_f = sb("gate_f", [P, KT, NE])
        GW = Split(sb, "gate_w", [P, KT, NE])
        gb = sb("gate_b", [P, NE])
        b1_cols = sb("b1", [P, NE, HT])
        b2_rows = sb("b2", [NE, D])
        ident = sb("ident", [P, P])
        neg_half = sb("neg_half", [P, TT])
        x_in = sb("x_in", [P, TT, D])
        xT = Split(sb, "xT", [P, KT, TOKENS])
        h_f = sb("h_f", [P, 2, TOKENS])
        hT = Split(sb, "hT", [P, 2, HT, TOKENS])
        logit = sb("logit", [P, TT, NE])
        peak = sb("peak", [P, TT])
        shifted = sb("shifted", [P, TT, NE])
        e = sb("e", [P, TT, NE])
        total = sb("total", [P, TT])
        recip = sb("recip", [P, TT])
        prob = sb("prob", [P, TT, 16])
        best = sb("best", [P, TT, 8])
        chosen = sb("chosen", [P, TT, 8])
        others = sb("others", [P, TT, 16])
        weight = sb("weight", [P, TT, NE])
        wT = sb("wT", [NE, TOKENS])
        acc = sb("acc", [P, TT, D])
        stats = sb("stats", [P, TT, 6])
        mv = sb("mv", [P, TT, 2])
        var = sb("var", [P, TT])
        rstd = sb("rstd", [P, TT])
        res = sb("res", [P, TT, D])

        hps = ctx.enter_context(nc.psum_tensor("e_hps", [P, 4, 512], F32))
        yps = ctx.enter_context(nc.psum_tensor("e_yps", [P, 4, 2, D], F32))

        w_loaded = [sem(f"w_loaded{n}") for n in range(2)]
        small_loaded = sem("small_loaded")
        w_hi = sem("w_hi"); w_lo = sem("w_lo"); gate_split = sem("gate_split")
        const_made = sem("const_made")
        x_loaded = sem("x_loaded"); stored = sem("stored")
        xT_ps = sem("xT_ps"); xT_hi = sem("xT_hi"); xT_lo = sem("xT_lo")
        gate_ps = sem("gate_ps"); gate_read = sem("gate_read"); shifted_made = sem("shifted_made")
        e_made = sem("e_made"); weight_made = sem("weight_made")
        wT_ps = sem("wT_ps"); wT_made = sem("wT_made"); b_ps = sem("b_ps"); acc_started = sem("acc_started")
        h_ps = sem("h_ps"); h_made = sem("h_made"); h_split = sem("h_split")
        y_ps = sem("y_ps"); y_added = sem("y_added")
        var_made = sem("var_made"); rstd_made = sem("rstd_made"); res_made = sem("res_made")
        chain = sem("chain"); dve_gate = sem("dve_gate")
        counted = [x_loaded, stored, xT_ps, xT_hi, xT_lo, gate_ps, gate_read, shifted_made, e_made, weight_made,
                   wT_ps, wT_made, b_ps, acc_started, h_ps, h_made, h_split, y_ps, y_added, var_made, rstd_made,
                   res_made, chain]

        xr = x.rearrange("(g b) (t p) d -> g p (b t) d", b=TOKENS // T, p=P)
        outr = out.rearrange("(g b) (t p) d -> g p (b t) d", b=TOKENS // T, p=P)
        flat = lambda t: t.rearrange("p k t -> p (k t)")

        pieces = []
        for n in range(NE):
            pieces.append((w1[n].rearrange("(k p) h -> p k h", p=P), W1, n, KT))
            pieces.append((w2[n].rearrange("(k p) c -> p k c", p=P), W2, n, HT))

        block = ctx.enter_context(nc.Block())

        @block.sync
        def _(sp):
            for s in counted:
                sp.sem_inc(s, 1)
            with nc.allow_non_contiguous_dma(reason="small, once"):
                sp.dma_start(b1_cols[:], b1.rearrange("e (k p) -> p e k", p=P)).then_inc(small_loaded, 16)
                sp.dma_start(gate_f[:], gate_w.rearrange("(k p) e -> p k e", p=P)).then_inc(small_loaded, 16)
            sp.dma_start(gb[:], gate_b.rearrange("(a e) -> a e", a=1).broadcast_to([P, NE])).then_inc(small_loaded, 16)
            sp.dma_start(b2_rows[:], b2).then_inc(small_loaded, 16)
            for n, (src, _, _, k) in enumerate(pieces):
                if n >= 2:
                    sp.wait_ge(w_lo, n - 1)
                sp.dma_start(stage[:, n % 2].rearrange("p (k n) -> p k n", k=k), src).then_inc(w_loaded[n % 2], 16)
            with sp.Fori(0, B) as i:
                sp.wait_ge(acc_started, i * TT + 1)
                sp.dma_start(x_in[:], xr[bass.ds(i, 1)].rearrange("a p t d -> (a p) t d")).then_inc(x_loaded, 16)
                sp.wait_ge(res_made, i * TT + TT + 1)
                for b in range(TOKENS // T):
                    t = slice(b * (T // P), (b + 1) * (T // P))
                    sp.dma_start(outr[bass.ds(i, 1)].rearrange("a p t d -> (a p) t d")[:, t], res[:, t]).then_inc(stored, 16)
            sp.wait_ge(stored, 16 * B * (TOKENS // T) + 1)

        @block.gpsimd
        def _(pool):
            build_identity(nc, pool, ident, const_made)
            nc.gpsimd.memset(neg_half[:], -0.5).then_inc(const_made, 1)
            nc.gpsimd.memset(prob[:], -1.0).then_inc(const_made, 1)
            nc.gpsimd.memset(chosen[:], -1.0).then_inc(const_made, 1)
            with pool.Fori(0, B) as i:
                pool.wait_ge(var_made, i + 2)
                nc.gpsimd.tensor_tensor(rstd[:], var[:], neg_half[:], ALU.pow).then_inc(rstd_made, 1)

        @block.tensor
        def _(pe):
            pe.wait_ge(const_made, 5)
            pe.wait_ge(small_loaded, 64)
            pe.wait_ge(gate_split, 2)
            pe.wait_ge(w_lo, len(pieces))
            with pe.Fori(0, B) as i:
                pe.wait_ge(x_loaded, i * 16 + 17)
                pe.wait_ge(h_split, i * NE * HT + 1)
                for kt in range(KT):
                    for tt in range(TT):
                        mm = nc.tensor.transpose(hps[:, kt, tt * P:tt * P + P], x_in[:, tt, kt * P:kt * P + P], ident[:])
                mm.then_inc(xT_ps, 1)
                pe.wait_ge(xT_lo, i + 2)
                for tt in range(TT):
                    for kt in range(KT):
                        mm = product(nc, hps[:, 2, tt * NE:tt * NE + NE], xT, GW,
                                     lambda t, kt=kt, tt=tt: t[:, kt, tt * P:tt * P + P],
                                     lambda t, kt=kt: t[:, kt, :], kt == 0, kt == KT - 1)
                mm.then_inc(gate_ps, 1)

                def hidden(n):
                    for m in range(HT):
                        if n == 0 and m == 2:
                            pe.wait_ge(gate_read, i + 2)
                        pe.wait_ge(h_made, i * NE * HT + max(n * HT + m - 3, 0) + 1)
                        for kt in range(KT):
                            mm = product(nc, hps[:, m, :], W1, xT,
                                         lambda t, kt=kt, m=m, n=n: t[:, n, kt, m * P:m * P + P],
                                         lambda t, kt=kt: t[:, kt, :], kt == 0, kt == KT - 1)
                        mm.then_inc(h_ps, 1)

                def combine(n):
                    pe.wait_ge(h_split, i * NE * HT + n * HT + HT + 1)
                    for pair in range(TT // 2):
                        if n >= 2:
                            pe.wait_ge(y_added, i * NE * 2 + 2 * (n - 2) + pair + 2)
                        elif n == 1:
                            pe.wait_ge(acc_started, i * TT + 2 * pair + 3)
                        else:
                            pe.wait_ge(y_added, i * NE * 2 + 1)
                        for half in range(2):
                            tt = 2 * pair + half
                            for k in range(HT):
                                mm = product(nc, yps[:, 2 * (n % 2) + pair, half, :], hT, W2,
                                             lambda t, k=k, tt=tt, n=n: t[:, n % 2, k, tt * P:tt * P + P],
                                             lambda t, k=k, n=n: t[:, n, k, :], k == 0, k == HT - 1)
                        mm.then_inc(y_ps, 1)

                hidden(0)
                pe.wait_ge(weight_made, i + 2)
                pe.wait_ge(y_added, i * NE * 2 + 1)
                for tt in range(TT):
                    mm = nc.tensor.transpose(yps[0:NE, 0, tt // 2, (tt % 2) * P:(tt % 2) * P + P], weight[:, tt, :], ident[:])
                mm.then_inc(wT_ps, 1)
                pe.wait_ge(wT_made, i + 2)
                for tt in range(TT):
                    mm = nc.tensor.matmul(yps[:, 2 + tt // 2, tt % 2, :], wT[:, tt * P:tt * P + P], b2_rows[:],
                                          start=True, stop=True, skip_group_check=True)
                mm.then_inc(b_ps, 1)
                hidden(1)
                for n in range(NE):
                    combine(n)
                    if n + 2 < NE:
                        hidden(n + 2)

        @block.scalar
        def _(act):
            act.wait_ge(small_loaded, 64)
            nc.scalar.activation(GW.hi[:], gate_f[:], ACT.Copy).then_inc(gate_split, 1)
            for n, (_, split, at, k) in enumerate(pieces):
                act.wait_ge(w_loaded[n % 2], 16 * (n // 2 + 1))
                nc.scalar.activation(flat(split.hi[:, at]), stage[:, n % 2], ACT.Copy).then_inc(w_hi, 1)
            with act.Fori(0, B) as i:
                def hidden(n):
                    for m in range(HT):
                        t = n * HT + m
                        act.wait_ge(h_ps, i * NE * HT + t + 2)
                        act.wait_ge(h_split, i * NE * HT + max(t - 1, 0) + 1)
                        nc.scalar.activation(h_f[:, t % 2], hps[:, m, :], ACT.Relu,
                                             bias=b1_cols[:, n, m:m + 1]).then_inc(h_made, 1)

                act.wait_ge(xT_ps, i + 2)
                nc.scalar.activation(xT.hi[:], hps[:, 0:KT], ACT.Copy).then_inc(xT_hi, 1)
                act.wait_ge(shifted_made, i + 2)
                nc.scalar.activation(e[:], shifted[:], ACT.Exp).then_inc(e_made, 1)
                for n in range(NE):
                    hidden(n)

        @block.vector
        def _(ve):
            dve = nc.vector
            ve.wait_ge(gate_split, 1)
            dve.tensor_tensor(GW.lo[:], gate_f[:], GW.hi[:].bitcast(F32), ALU.subtract).then_inc(gate_split, 1)
            for n, (_, split, at, k) in enumerate(pieces):
                ve.wait_ge(w_hi, n + 1)
                dve.tensor_tensor(flat(split.lo[:, at]), stage[:, n % 2], flat(split.hi[:, at]).bitcast(F32),
                                  ALU.subtract).then_inc(w_lo, 1)
            ve.wait_ge(const_made, 5)
            LINKS = 41
            with ve.Fori(0, B) as i:
                linked = [0]

                def link(ins):
                    linked[0] += 1
                    ins.then_inc(chain, 1)
                    ve.wait_ge(chain, i * LINKS + linked[0] + 1)

                def split_hidden(n):
                    for m in range(HT):
                        t = n * HT + m
                        ve.wait_ge(h_made, i * NE * HT + t + 2)
                        if m == 0:
                            ve.wait_ge(y_ps, i * NE * 2 + max(2 * (n - 1), 0) + 1)
                        hi = hT.hi[:, n % 2, m]
                        link(dve.tensor_copy(hi, h_f[:, t % 2]))
                        dve.tensor_tensor(hT.lo[:, n % 2, m], h_f[:, t % 2], hi.bitcast(F32), ALU.subtract).then_inc(h_split, 1)

                def add_expert(n):
                    for pair in range(TT // 2):
                        ve.wait_ge(y_ps, i * NE * 2 + 2 * n + pair + 2)
                        for half in range(2):
                            tt = 2 * pair + half
                            ins = dve.scalar_tensor_tensor(out=acc[:, tt], in0=yps[:, 2 * (n % 2) + pair, half, :],
                                                           scalar=weight[:, tt, n:n + 1], in1=acc[:, tt],
                                                           op0=ALU.mult, op1=ALU.add)
                        ins.then_inc(y_added, 1)

                ve.wait_ge(xT_hi, i + 2)
                dve.tensor_tensor(xT.lo[:], hps[:, 0:KT], xT.hi[:].bitcast(F32), ALU.subtract).then_inc(xT_lo, 1)
                ve.wait_ge(gate_ps, i + 2)
                gates = hps[:, 2, 0:TT * NE].rearrange("p (t e) -> p t e", e=NE)
                dve.tensor_tensor(logit[:], gates, gb[:].unsqueeze(1).broadcast_to([P, TT, NE]), ALU.add).then_inc(gate_read, 1)
                ve.wait_ge(gate_read, i + 2)
                link(dve.tensor_reduce(peak[:], logit[:], AX.X, ALU.max))
                dve.tensor_tensor(shifted[:], logit[:], peak[:].unsqueeze(2).broadcast_to([P, TT, NE]),
                                  ALU.subtract).then_inc(shifted_made, 1)
                ve.wait_ge(e_made, i + 2)
                link(dve.tensor_reduce(total[:], e[:], AX.X, ALU.add))
                link(dve.reciprocal(recip[:], total[:]))
                link(dve.tensor_tensor(prob[:, :, 0:NE], e[:], recip[:].unsqueeze(2).broadcast_to([P, TT, NE]), ALU.mult))
                ve.sem_inc(dve_gate, 1)
                for tt in range(TT):
                    ins = dve.max(best[:, tt], prob[:, tt])
                link(ins)
                link(dve.tensor_copy(chosen[:, :, 0:2], best[:, :, 0:2]))
                ve.sem_inc(dve_gate, 1)
                for tt in range(TT):
                    ins = dve.match_replace(others[:, tt], chosen[:, tt], prob[:, tt], 0.0)
                link(ins)
                dve.tensor_tensor(weight[:], prob[:, :, 0:NE], others[:, :, 0:NE], ALU.subtract).then_inc(weight_made, 1)
                split_hidden(0)
                ve.wait_ge(wT_ps, i + 2)
                dve.tensor_copy(wT[:].rearrange("p (a t) -> p a t", a=2), yps[0:NE, 0, :, :]).then_inc(wT_made, 1)
                ve.wait_ge(b_ps, i + 2)
                for tt in range(TT):
                    dve.tensor_tensor(acc[:, tt], yps[:, 2 + tt // 2, tt % 2, :], x_in[:, tt], ALU.add).then_inc(acc_started, 1)
                ve.wait_ge(acc_started, i * TT + TT + 1)
                split_hidden(1)
                for n in range(NE):
                    if n >= 1:
                        ve.wait_ge(y_added, i * NE * 2 + 2 * n + 1)
                    add_expert(n)
                    if n + 2 < NE:
                        split_hidden(n + 2)
                ve.wait_ge(y_added, i * NE * 2 + 2 * NE + 1)
                for tt in range(TT):
                    ins = dve.bn_stats(stats[:, tt], acc[:, tt])
                link(ins)
                ve.sem_inc(dve_gate, 1)
                for tt in range(TT):
                    ins = dve.bn_aggr(mv[:, tt], stats[:, tt])
                link(ins)
                dve.tensor_scalar(var[:], mv[:, :, 1], EPS, None, ALU.add).then_inc(var_made, 1)
                ve.wait_ge(rstd_made, i + 2)
                ve.wait_ge(stored, i * 16 * (TOKENS // T) + 1)
                for tt in range(TT):
                    dve.tensor_scalar(res[:, tt], acc[:, tt], mv[:, tt, 0:1], rstd[:, tt:tt + 1],
                                      ALU.subtract, ALU.mult).then_inc(res_made, 1)
                assert linked[0] == LINKS, linked



def decoder_layer(nc, x, context, wq, wf, wi, g_weight, wo, w_kv, w_q, w_out1, w_out2, gamma,
                  gate_w, gate_b, w1, b1, w2, b2, out):
    x1 = nc.dram_tensor("after_linear_attention", x.shape, F32, kind="Internal").ap()
    x2 = nc.dram_tensor("after_cross_attention", x.shape, F32, kind="Internal").ap()
    linear_attention_pass(nc, x, wq, wf, wi, g_weight, wo, x1)
    cross_attention_pass(nc, x1, context, w_kv, w_q, w_out1, w_out2, gamma, x2)
    experts_pass(nc, x2, gate_w, gate_b, w1, b1, w2, b2, out)


_INS = ["x", "ctx_1024", "L0_attn_Wq", "L0_attn_Wf", "L0_attn_Wi", "L0_attn_g_weight", "L0_attn_Wo",
        "L0_xattn_w_kv", "L0_xattn_w_q", "L0_xattn_w_out1", "L0_xattn_w_out2", "L0_xattn_gamma",
        "L0_ffn_gate_w", "L0_ffn_gate_b", "L0_ffn_w1", "L0_ffn_b1", "L0_ffn_w2", "L0_ffn_b2"]


def kernel(**inputs):
    import numpy as _np
    import concourse.bacc as _bacc
    from concourse import mybir as _mybir
    from concourse.bass_utils import run_bass_kernel_spmd as _run

    nc = _bacc.Bacc("TRN2", target_bir_lowering=False, num_devices=1)
    arrays, args = {}, []
    for name in _INS:
        a = _np.ascontiguousarray(inputs[name])
        arrays[f"in_{name}_dram"] = a
        args.append(nc.dram_tensor(f"in_{name}_dram", a.shape, _mybir.dt.from_np(a.dtype), kind="ExternalInput").ap())
    out = nc.dram_tensor("out_dram", inputs["x"].shape, _mybir.dt.float32, kind="ExternalOutput").ap()
    decoder_layer(nc, *args, out)
    r = _run(nc, [arrays], core_ids=[0])
    return r.results[0]["out_dram"]
```

```python
from contextlib import ExitStack

import concourse.bass as bass
from concourse import mybir

F32 = mybir.dt.float32
F32R = mybir.dt.float32r
I32 = mybir.dt.int32
ALU = mybir.AluOpType
ACT = mybir.ActivationFunctionType
AX = mybir.AxisListType

P = 128
EPS = 1e-5


class Split:

    def __init__(self, sb, name, shape):
        self.hi = sb(name + "_hi", shape, F32R)
        self.lo = sb(name + "_lo", shape, F32R)


def product(nc, out, w, m, w_at, m_at, first, last):
    nc.tensor.matmul(out, w_at(w.hi), m_at(m.hi), start=first, stop=False, skip_group_check=True)
    nc.tensor.matmul(out, w_at(w.hi), m_at(m.lo), start=False, stop=False, skip_group_check=True)
    return nc.tensor.matmul(out, w_at(w.lo), m_at(m.hi), start=False, stop=last, skip_group_check=True)


def build_identity(nc, pool, ident, made):
    nc.gpsimd.memset(ident[:], 0.0).then_inc(made, 1)
    pool.wait_ge(made, 1)
    nc.gpsimd.affine_select(out=ident[:], in_=ident[:], compare_op=ALU.not_equal, fill=1.0, base=0,
                            pattern=[[-1, P]], channel_multiplier=1).then_inc(made, 1)


def linear_attention_pass(nc, x, wq, wf, wi, g_weight, wo, x_out):
    B, T, D = x.shape
    H = 8
    DK = D // H
    KT = D // P
    TT = T // P
    HT = P // DK
    N = KT * T
    LEVELS = [8, 16, 32, 64, 128]
    INNER = 4
    A_MIN = 1e-8
    VS = 160
    KINDS = [(u, b) for u in ("base", "low", "high") for b in range(TT)] + [("cross", 0)]
    USES = [(c, b, u) for c in range(KT) for u, b in KINDS]
    PER_C = len(KINDS)
    USES += [(0, 0, "squares"), (0, 0, "y")]
    MERGES = []
    for c in range(KT):
        MERGES += [(c * PER_C, 0), (c * PER_C + 1, 0)]
        MERGES += [(c * PER_C + u + b, m) for u in (2, 4) for m in range(2) for b in range(TT)]
    NM = len(MERGES) + 2
    SPARE = 4

    def merged_after(u):
        if u >= KT * PER_C:
            return len(MERGES) + 1 + u - KT * PER_C
        return max(k for k, (use, _) in enumerate(MERGES) if use == u) + 1

    CHAIN = ["clamp", "D1", "C1", "D2", "C2", "R0", "R1", "base0", "base1", "base2", "base3", "D4", "C4"]
    for h in LEVELS:
        CHAIN += [f"K{h}", f"Q{h}"] + ([f"D{h}", f"C{h}"] if h < LEVELS[-1] else [])
    NC = len(CHAIN)
    FACTORS = ["base3"] + [f"Q{h}" for h in LEVELS]
    NU = len(USES)
    CONSTS = 4 + 1 + INNER + 6 + 2
    assert NU % 4 == 0

    with ExitStack() as ctx:
        def sb(name, shape, dt=F32):
            return ctx.enter_context(nc.sbuf_tensor("g_" + name, shape, dt))

        def sem(name):
            return ctx.enter_context(nc.semaphore("g_" + name))

        names = ["wq", "wf", "wi", "wo"]
        W = {n: Split(sb, n, [P, KT, D]) for n in names}
        g_cols = sb("g_cols", [P, KT])
        ident = sb("ident", [P, P])
        ones_col = sb("ones_col", [P, 1])
        neg_half = sb("neg_half", [P, TT])
        base_mask = sb("base_mask", [P, P])
        level_mask = sb("level_mask", [P, INNER, P // 2])
        x_in = sb("x_in", [P, TT, D])
        xT = Split(sb, "xT", [P, KT, T])
        a = sb("a", [P, N])
        k = sb("k", [P, N])
        q = sb("q", [P, N])
        C = sb("C", [P, N])
        Dx = sb("Dx", [P, N])
        R = a
        base_f = sb("base_f", [P, 2, N])
        level_f = sb("level_f", [P, 5, 2, N // 2])
        base_k = Split(sb, "base_k", [P, KT, T])
        level_k = Split(sb, "level_k", [P, INNER, N])
        cross_k = Split(sb, "cross_k", [P, KT, P])
        base_q = sb("base_q", [P, 2, KT, T], F32R)
        level_q = sb("level_q", [P, 5, 2, KT, P], F32R)
        base_x = sb("base_x", [P, 2, KT, HT, T], F32R)
        level_x = sb("level_x", [P, 5, 2, KT, HT, P], F32R)
        V = Split(sb, "V", [P, TT, KT, HT, VS])
        A = [sb("A0", [P, KT, HT, T]), sb("A1", [P, KT, HT, P])]
        AS = [Split(sb, "AS0", [P, KT, HT, T]), Split(sb, "AS1", [P, KT, HT, P])]
        oT = Split(sb, "oT", [P, KT, T])
        sq = sb("sq", [P, KT, T])
        msq = sb("msq", [P, TT])
        rms = sb("rms", [P, TT])
        z = sb("z", [P, TT, D])
        stage = z
        stats = sb("stats", [P, TT, 6])
        mv = sb("mv", [P, TT, 2])
        var = sb("var", [P, TT])
        rstd = sb("rstd", [P, TT])

        ps = ctx.enter_context(nc.psum_tensor("g_ps", [P, 4, 512], F32))
        grp = ctx.enter_context(nc.psum_tensor("g_grp", [P, 4, 512], F32))

        loaded_w = sem("loaded_w"); const_made = sem("const_made"); pool_self = sem("pool_self")
        g_loaded = sem("g_loaded"); w_hi_made = sem("w_hi"); w_ready = sem("w_ready"); wo_made = sem("wo_made")
        x_loaded = sem("x_loaded"); res_loaded = sem("res_loaded"); x_stored = sem("x_stored"); x1_made = sem("x1_made")
        xT_ps = sem("xT_ps"); xT_hi = sem("xT_hi"); xT_lo = sem("xT_lo")
        f_ps = sem("f_ps"); q_ps = sem("q_ps"); v_ps = sem("v_ps")
        a_made = sem("a_made"); gate_made = sem("gate_made"); q_made = sem("q_made")
        v_hi = sem("v_hi"); v_lo = sem("v_lo"); k_made = sem("k_made")
        d_reset = sem("d_reset"); chain = sem("chain"); tail_chain = sem("tail_chain")
        fac_hi = sem("fac_hi"); fac_lo = sem("fac_lo"); spread = [sem("spread_base"), sem("spread_low"), sem("spread_high")]
        use_ready = sem("use_ready"); merged = sem("merged"); cross_read = sem("cross_read")
        A_hi = sem("A_hi"); A_lo = sem("A_lo")
        o_ps = sem("o_ps"); o_hi = sem("o_hi"); o_lo = sem("o_lo"); sq_made = sem("sq_made")
        msq_made = sem("msq_made"); rms_made = sem("rms_made")
        z_made = sem("z_made"); var_made = sem("var_made"); rstd_made = sem("rstd_made")
        counted = [x_loaded, res_loaded, x_stored, x1_made, xT_ps, xT_hi, xT_lo, f_ps, q_ps, v_ps, a_made, gate_made,
                   q_made, v_hi, v_lo, k_made, d_reset, chain, tail_chain, cross_read, fac_hi, fac_lo,
                   *spread, use_ready, A_hi, A_lo, o_ps, o_hi, o_lo, sq_made, msq_made, rms_made, z_made,
                   var_made, rstd_made]
        dve_gate = sem("dve_gate"); pool_gate = sem("pool_gate")
        SPREADS = HT * 16

        xr = x.rearrange("b (t p) d -> b p t d", p=P)
        outr = x_out.rearrange("b (t p) d -> b p t d", p=P)
        flat = lambda t: t.rearrange("p k t -> p (k t)")

        def half(t, h, which):
            return t.rearrange("p (n two h) -> p n two h", two=2, h=h)[:, :, which, :]

        def key_parts(n, part):
            if n == 4:
                return flat(part_of(cross_k, part)[:]), level_f[:, n, 0]
            h = LEVELS[n]
            return (half(part_of(level_k, part)[:, n], h, 0),
                    level_f[:, n, 0].rearrange("p (n h) -> p n h", h=h))

        def part_of(split, part):
            return split.hi if part == 0 else split.lo

        def element(t, n):
            return t[bass.ds(n, 1)].rearrange("a p t d -> (a p) t d")

        def chained(n, step):
            return n * NC + CHAIN.index(step) + 2

        RMS_AFTER = 3

        block = ctx.enter_context(nc.Block())

        @block.sync
        def _(sp):
            for s in counted:
                sp.sem_inc(s, 1)
            sp.sem_inc(merged, SPARE)
            sp.dma_start(x_in[:], element(xr, 0)).then_inc(x_loaded, 16)
            with nc.allow_non_contiguous_dma(reason="256 scales, once"):
                sp.dma_start(g_cols[:], g_weight.rearrange("(k p) -> p k", p=P)).then_inc(g_loaded, 16)
            for n, w in enumerate([wq, wf, wi, wo]):
                if n:
                    sp.wait_ge(w_ready, n)
                sp.dma_start(stage[:], w.rearrange("(k p) n -> p k n", p=P)).then_inc(loaded_w, 16)

            def spread_heads(n):
                for piece, (lo, hi) in enumerate(((0, 1), (1, 4), (4, 6))):
                    sp.wait_ge(fac_lo, n * 6 + hi + 1)
                    if piece == 0:
                        sp.wait_ge(A_hi, n * 4 + 1)
                    for j in range(HT):
                        rows = slice(DK * j, DK * j + DK)
                        if piece == 0:
                            src, dst = base_q[rows], base_x[rows, :, :, j, :]
                            src = src.rearrange("p s k t -> p (s k) t")
                            dst = dst.rearrange("p s k t -> p (s k) t")
                        else:
                            src, dst = level_q[rows, lo - 1:hi - 1], level_x[rows, lo - 1:hi - 1, :, :, j, :]
                            src = src.rearrange("p n s k t -> p (n s k) t")
                            dst = dst.rearrange("p n s k t -> p (n s k) t")
                        sp.dma_start(dst.bitcast(F32), src.bitcast(F32)).then_inc(spread[piece], 16)

            def residual(n):
                sp.wait_ge(x_stored, n * 16 + 1)
                sp.dma_start(z[:], element(xr, n)).then_inc(res_loaded, 16)

            def store(n):
                sp.wait_ge(x1_made, n * TT + TT + 1)
                sp.dma_start(element(outr, n), z[:]).then_inc(x_stored, 16)

            def next_input(n):
                sp.wait_ge(xT_ps, n + 1)
                sp.dma_start(x_in[:], element(xr, n)).then_inc(x_loaded, 16)

            spread_heads(0)
            next_input(1)
            sp.wait_ge(w_ready, 4)
            with sp.Fori(0, B - 2) as i:
                residual(i)
                next_input(i + 2)
                spread_heads(i + 1)
                store(i)
            residual(B - 2)
            spread_heads(B - 1)
            store(B - 2)
            residual(B - 1)
            store(B - 1)
            sp.wait_ge(x_stored, 16 * B + 1)

        @block.gpsimd
        def _(pool):
            build_identity(nc, pool, ident, const_made)
            nc.gpsimd.memset(ones_col[:], 1.0).then_inc(const_made, 1)
            nc.gpsimd.memset(neg_half[:], -0.5).then_inc(const_made, 1)
            nc.gpsimd.memset(base_mask[:], 1.0).then_inc(pool_self, 1)
            nc.gpsimd.memset(level_mask[:], 1.0).then_inc(pool_self, 1)
            pool.wait_ge(pool_self, 2)
            nc.gpsimd.affine_select(out=base_mask[:], in_=base_mask[:], compare_op=ALU.is_ge, fill=0.0,
                                    base=0, pattern=[[1, P]], channel_multiplier=-1).then_inc(pool_self, 1)
            pool.wait_ge(pool_self, 3)
            bm = base_mask[:].rearrange("p (b e) -> p b e", e=8)
            nc.gpsimd.affine_select(out=bm, in_=bm, compare_op=ALU.is_ge, fill=0.0, base=0,
                                    pattern=[[-8, P // 8], [0, 8]], channel_multiplier=1).then_inc(const_made, 1)
            for n, h in enumerate(LEVELS[:INNER]):
                lm = level_mask[:, n].rearrange("p (b e) -> p b e", e=h)
                nc.gpsimd.affine_select(out=lm, in_=lm, compare_op=ALU.is_ge, fill=0.0, base=0,
                                        pattern=[[-2 * h, P // 2 // h], [0, h]],
                                        channel_multiplier=1).then_inc(pool_self, 1)
                pool.wait_ge(pool_self, 4 + n)
                nc.gpsimd.affine_select(out=lm, in_=lm, compare_op=ALU.is_ge, fill=0.0, base=h - 1,
                                        pattern=[[2 * h, P // 2 // h], [0, h]],
                                        channel_multiplier=-1).then_inc(const_made, 1)
            for t in (V.hi, V.lo, level_k.hi, level_k.lo, base_x, level_x):
                nc.gpsimd.memset(t[:].bitcast(F32), 0.0).then_inc(const_made, 1)
            for t in A:
                nc.gpsimd.memset(t[:], 0.0).then_inc(const_made, 1)
            pool.wait_ge(const_made, CONSTS)

            def reset(n):
                pool.wait_ge(chain, n * NC + 1)
                pool.sem_inc(pool_gate, 1)
                nc.gpsimd.memset(Dx[:], 1.0).then_inc(d_reset, 1)

            def keys(n):
                pool.wait_ge(a_made, n + 2)
                pool.sem_inc(pool_gate, 1)
                nc.gpsimd.tensor_scalar(k[:], a[:], -1.0, 1.0, ALU.mult, ALU.add).then_inc(k_made, 1)

            def factor_rests(n, m):
                pool.wait_ge(fac_hi, n * 6 + m + 2)
                if m == 0:
                    nc.gpsimd.tensor_tensor(flat(base_k.lo[:]), base_f[:, 0], flat(base_k.hi[:]).bitcast(F32), ALU.subtract)
                    nc.gpsimd.tensor_tensor(flat(base_q[:, 1]), base_f[:, 1], flat(base_q[:, 0]).bitcast(F32),
                                            ALU.subtract).then_inc(fac_lo, 1)
                else:
                    lo, src = key_parts(m - 1, 1)
                    hi, _ = key_parts(m - 1, 0)
                    nc.gpsimd.tensor_tensor(lo, src, hi.bitcast(F32), ALU.subtract)
                    nc.gpsimd.tensor_tensor(flat(level_q[:, m - 1, 1]), level_f[:, m - 1, 1],
                                            flat(level_q[:, m - 1, 0]).bitcast(F32), ALU.subtract).then_inc(fac_lo, 1)

            def score_rests(n, c):
                for s in range(TT):
                    pool.wait_ge(A_hi, n * 4 + c * 2 + s + 2)
                    nc.gpsimd.tensor_tensor(AS[s].lo[:, c], A[s][:, c], AS[s].hi[:, c].bitcast(F32),
                                            ALU.subtract).then_inc(A_lo, 1)

            def power(n, made, out, src, done):
                pool.wait_ge(made, n + 2)
                nc.gpsimd.tensor_tensor(out[:], src[:], neg_half[:], ALU.pow).then_inc(done, 1)

            reset(0)
            keys(0)
            for m in range(6):
                factor_rests(0, m)
            with pool.Fori(0, B - 1) as i:
                reset(i + 1)
                score_rests(i, 0)
                keys(i + 1)
                score_rests(i, 1)
                for m in range(6):
                    factor_rests(i + 1, m)
                    if m == RMS_AFTER:
                        power(i, msq_made, rms, msq, rms_made)
                power(i, var_made, rstd, var, rstd_made)
            for c in range(KT):
                score_rests(B - 1, c)
            power(B - 1, msq_made, rms, msq, rms_made)
            power(B - 1, var_made, rstd, var, rstd_made)

        @block.tensor
        def _(pe):
            pe.wait_ge(const_made, CONSTS)
            pe.wait_ge(w_ready, 4)

            def transposed(n):
                pe.wait_ge(x_loaded, n * 16 + 17)
                for kt in range(KT):
                    for tt in range(TT):
                        mm = nc.tensor.transpose(ps[:, 0, kt * T + tt * P:kt * T + tt * P + P],
                                                 x_in[:, tt, kt * P:kt * P + P], ident[:])
                mm.then_inc(xT_ps, 1)

            def project(n, bank, w, done, freed):
                pe.wait_ge(xT_lo, n + 2)
                pe.wait_ge(freed, n + 1)
                for m in range(KT):
                    for kt in range(KT):
                        mm = product(nc, ps[:, bank, m * T:m * T + T], W[w], xT,
                                     lambda t, kt=kt, m=m: t[:, kt, m * P:m * P + P],
                                     lambda t, kt=kt: t[:, kt, :], kt == 0, kt == KT - 1)
                mm.then_inc(done, 1)

            def values(n):
                pe.wait_ge(v_lo, n * 2 + 1)
                for tt in range(TT):
                    for kt in range(KT):
                        mm = product(nc, ps[:, 3, tt * D:tt * D + D], xT, W["wi"],
                                     lambda t, kt=kt, tt=tt: t[:, kt, tt * P:tt * P + P],
                                     lambda t, kt=kt: t[:, kt, :], kt == 0, kt == KT - 1)
                mm.then_inc(v_ps, 1)

            def bank(n, u):
                before = u - 4 if u >= 4 else u - 4 + NU
                elements = 0 if u >= 4 else -1
                if USES[before][2] == "cross":
                    pe.wait_ge(cross_read, n * KT + elements * KT + before // PER_C + 2)
                else:
                    pe.wait_ge(merged, n * NM + elements * NM + merged_after(before) + SPARE)
                return grp[:, u % 4]

            def scores(n):
                ahead = not isinstance(n, int)
                for u, (c, b, kind) in enumerate(USES[:KT * PER_C]):
                    if u == 3 and ahead:
                        transposed(n + 1)
                    if u == PER_C and ahead:
                        project(n + 1, 1, "wf", f_ps, a_made)
                    to = bank(n, u)
                    if u == 0:
                        pe.wait_ge(spread[0], n * SPREADS + SPREADS + 1)
                    if u == 2:
                        pe.wait_ge(spread[1], n * SPREADS + SPREADS + 1)
                    if u == 4:
                        pe.wait_ge(spread[2], n * SPREADS + SPREADS + 1)
                    for part_k, part_q in ((0, 0), (0, 1), (1, 0)):
                        first, last = (part_k, part_q) == (0, 0), part_k == 1
                        if kind == "base":
                            mm = nc.tensor.matmul(to, part_of(base_k, part_k)[:, c, b * P:b * P + P],
                                                  base_x[:, part_q, c, :, b * P:b * P + P], start=first, stop=last,
                                                  skip_group_check=True)
                        elif kind == "cross":
                            mm = nc.tensor.matmul(to, part_of(cross_k, part_k)[:, c, :],
                                                  level_x[:, 4, part_q, c, :, :], start=first, stop=last,
                                                  skip_group_check=True)
                    if kind in ("low", "high"):
                        for m in range(2):
                            lev = m + (2 if kind == "high" else 0)
                            for part_k, part_q in ((0, 0), (0, 1), (1, 0)):
                                mm = nc.tensor.matmul(to[:, 256 * m:256 * m + 256],
                                                      part_of(level_k, part_k)[:, lev, c * T + b * P:c * T + b * P + P],
                                                      level_x[:, lev, part_q, c, :, b * 64:b * 64 + 64],
                                                      start=(part_k, part_q) == (0, 0), stop=part_k == 1,
                                                      skip_group_check=True)
                    mm.then_inc(use_ready, 1)

            def weigh_values(n, c):
                if c == 0:
                    pe.wait_ge(v_lo, n * 2 + 3)
                for s in range(TT):
                    pe.wait_ge(A_lo, n * 4 + 2 * c + s + 2)
                    for j in range(HT):
                        mm = product(nc, ps[:, 0, c * T + s * P:c * T + T], V, AS[s],
                                     lambda t, c=c, s=s, j=j: t[:, s, c].rearrange("p j v -> p (j v)")[:, P * j:P * j + P],
                                     lambda t, c=c, j=j: t[:, c, j, :],
                                     s == 0 and j == 0, s == TT - 1 and j == HT - 1)
                if c == KT - 1:
                    mm.then_inc(o_ps, 1)

            def outputs(n):
                to = bank(n, NU - 2)
                pe.wait_ge(sq_made, n + 2)
                for tt in range(TT):
                    for c in range(KT):
                        mm = nc.tensor.matmul(to[:, tt:tt + 1], sq[:, c, tt * P:tt * P + P], ones_col[:],
                                              start=(c == 0), stop=(c == KT - 1), skip_group_check=True)
                mm.then_inc(use_ready, 1)
                to = bank(n, NU - 1)
                pe.wait_ge(o_lo, n + 2)
                for tt in range(TT):
                    for c in range(KT):
                        mm = product(nc, to[:, tt * D:tt * D + D], oT, W["wo"],
                                     lambda t, c=c, tt=tt: t[:, c, tt * P:tt * P + P],
                                     lambda t, c=c: t[:, c, :], c == 0, c == KT - 1)
                mm.then_inc(use_ready, 1)

            transposed(0)
            project(0, 1, "wf", f_ps, a_made)
            project(0, 2, "wq", q_ps, q_made)
            values(0)
            with pe.Fori(0, B - 1) as i:
                scores(i)
                project(i + 1, 2, "wq", q_ps, q_made)
                weigh_values(i, 0)
                values(i + 1)
                weigh_values(i, 1)
                outputs(i)
            scores(B - 1)
            weigh_values(B - 1, 0)
            weigh_values(B - 1, 1)
            outputs(B - 1)

        @block.scalar
        def _(act):
            for n, name in enumerate(names):
                act.wait_ge(loaded_w, 16 * (n + 1))
                if name == "wo":
                    act.wait_ge(wo_made, KT)
                nc.scalar.activation(W[name].hi[:], stage[:], ACT.Copy).then_inc(w_hi_made, 1)
            act.wait_ge(const_made, CONSTS)

            def round_x(n):
                act.wait_ge(xT_ps, n + 2)
                nc.scalar.activation(flat(xT.hi[:]), ps[:, 0], ACT.Copy).then_inc(xT_hi, 1)

            def gates(n):
                act.wait_ge(f_ps, n + 2)
                act.wait_ge(chain, n * NC + 1)
                nc.scalar.activation(a[:], ps[:, 1], ACT.Sigmoid).then_inc(a_made, 1)

            def query_gates(n):
                act.wait_ge(q_ps, n + 2)
                act.wait_ge(chain, n * NC + 1)
                nc.scalar.activation(q[:], ps[:, 2], ACT.Sigmoid).then_inc(gate_made, 1)

            def value_round(n):
                act.wait_ge(v_ps, n + 2)
                act.wait_ge(o_ps, n + 1)
                for tt in range(TT):
                    nc.scalar.activation(V.hi[:, tt, :, :, 0:DK],
                                         ps[:, 3, tt * D:tt * D + D].rearrange("p (c j d) -> p c j d", c=KT, d=DK),
                                         ACT.Copy).then_inc(v_hi, 1)

            def factor_round(n, m):
                if m == 0:
                    for s in spread:
                        act.wait_ge(s, n * SPREADS + 1)
                act.wait_ge(chain, chained(n, FACTORS[m]))
                if m == 0:
                    nc.scalar.activation(flat(base_k.hi[:]), base_f[:, 0], ACT.Copy)
                    nc.scalar.activation(flat(base_q[:, 0]), base_f[:, 1], ACT.Copy).then_inc(fac_hi, 1)
                else:
                    hi, src = key_parts(m - 1, 0)
                    nc.scalar.activation(hi, src, ACT.Copy)
                    nc.scalar.activation(flat(level_q[:, m - 1, 0]), level_f[:, m - 1, 1], ACT.Copy).then_inc(fac_hi, 1)

            def score_round(n, c):
                if c == 0:
                    act.wait_ge(o_ps, n + 1)
                u = c * PER_C + PER_C - 1
                act.wait_ge(use_ready, n * NU + u + 2)
                act.wait_ge(A_lo, n * 4 + 1)
                nc.scalar.activation(A[0][:, c, :, P:2 * P], grp[:, u % 4].rearrange("p (j t) -> p j t", j=HT),
                                     ACT.Copy).then_inc(cross_read, 1)
                act.wait_ge(cross_read, n * KT + c + 2)
                act.wait_ge(merged, n * NM + merged_after(u - 1) + SPARE)
                for s in range(TT):
                    nc.scalar.activation(AS[s].hi[:, c], A[s][:, c], ACT.Copy).then_inc(A_hi, 1)

            def output_round(n):
                act.wait_ge(o_ps, n + 2)
                nc.scalar.activation(flat(oT.hi[:]), ps[:, 0], ACT.Copy).then_inc(o_hi, 1)
                nc.scalar.activation(flat(sq[:]), ps[:, 0], ACT.Square).then_inc(sq_made, 1)

            round_x(0)
            gates(0)
            query_gates(0)
            value_round(0)
            for m in range(6):
                factor_round(0, m)
            with act.Fori(0, B - 1) as i:
                round_x(i + 1)
                score_round(i, 0)
                gates(i + 1)
                score_round(i, 1)
                query_gates(i + 1)
                for m in range(6):
                    factor_round(i + 1, m)
                    if m == 1:
                        output_round(i)
                        value_round(i + 1)
            for c in range(KT):
                score_round(B - 1, c)
            output_round(B - 1)

        @block.vector
        def _(ve):
            dve = nc.vector
            ve.wait_ge(g_loaded, 16)
            for n, name in enumerate(names):
                if name == "wo":
                    ve.wait_ge(loaded_w, 64)
                    for kt in range(KT):
                        dve.tensor_scalar(stage[:, kt], stage[:, kt], g_cols[:, kt:kt + 1], None, ALU.mult).then_inc(wo_made, 1)
                ve.wait_ge(w_hi_made, n + 1)
                dve.tensor_tensor(W[name].lo[:], stage[:], W[name].hi[:].bitcast(F32), ALU.subtract).then_inc(w_ready, 1)
            ve.wait_ge(const_made, CONSTS)

            def x_rest(n):
                ve.wait_ge(xT_hi, n + 2)
                dve.tensor_tensor(flat(xT.lo[:]), ps[:, 0], flat(xT.hi[:]).bitcast(F32), ALU.subtract).then_inc(xT_lo, 1)

            def factors(n, outputs_of=None):
                shape = lambda h: [P, N // (2 * h), h]

                def do(step, ins):
                    assert CHAIN[done[0]] == step
                    done[0] += 1
                    ins.then_inc(chain, 1)

                def after(*steps):
                    ve.wait_ge(chain, chained(n, max(steps, key=CHAIN.index)))

                done = [0]
                ve.wait_ge(a_made, n + 2)
                do("clamp", dve.tensor_scalar(C[:], a[:], A_MIN, None, ALU.max))
                ve.wait_ge(d_reset, n + 2)

                def grow_d(h):
                    d0, c1 = half(Dx[:], h, 0), half(C[:], h, 1)
                    if h == 1:
                        after("clamp")
                        do("D1", dve.tensor_copy(d0, c1))
                        return
                    if h == 4:
                        after(f"C{h // 2}", "base3")
                    elif h > 4:
                        after(f"C{h // 2}", f"K{h}")
                    else:
                        after(f"C{h // 2}")
                    do(f"D{h}", dve.tensor_tensor(d0, d0, c1[:, :, h - 1:h].broadcast_to(shape(h)), ALU.mult))

                def grow_c(h):
                    c0, c1 = half(C[:], h, 0), half(C[:], h, 1)
                    if outputs_of is not None and h == 16:
                        output_rest(outputs_of)
                    if outputs_of is not None and h == 32:
                        value_rest(n)
                    if outputs_of is not None and h == 64:
                        squares(outputs_of)
                    after(f"D{h}")
                    do(f"C{h}", dve.tensor_tensor(c1, c1, c0[:, :, h - 1:h].broadcast_to(shape(h)), ALU.mult))

                for h in (1, 2):
                    grow_d(h)
                    grow_c(h)
                ve.wait_ge(k_made, n + 2)
                after("D2")
                do("R0", dve.reciprocal(half(R[:], 4, 0), half(Dx[:], 4, 0)))
                after("C2")
                do("R1", dve.reciprocal(half(R[:], 4, 1), half(C[:], 4, 1)))
                ve.wait_ge(gate_made, n + 2)
                dve.scalar_tensor_tensor(out=q[:], in0=ps[:, 2], scalar=float(DK) ** -0.5, in1=q[:],
                                         op0=ALU.mult, op1=ALU.mult).then_inc(q_made, 1)
                ve.wait_ge(fac_lo, n * 6 + 1)
                order = ((0, 0, k, Dx), (1, 0, q, R), (0, 1, k, R), (1, 1, q, C))
                for u, (side, w, t, f) in enumerate(order):
                    if u == 2:
                        after("R1")
                    elif u == 1:
                        ve.wait_ge(q_made, n + 2)
                        after("R0")
                    do(f"base{u}", dve.tensor_tensor(half(base_f[:, side], 4, w), half(t[:], 4, w),
                                                             half(f[:], 4, w), ALU.mult))
                grow_d(4)
                grow_c(4)
                for m, h in enumerate(LEVELS):
                    after(f"D{h // 2}")
                    do(f"K{h}", dve.tensor_tensor(level_f[:, m, 0].rearrange("p (n h) -> p n h", h=h),
                                                          half(k[:], h, 0), half(Dx[:], h, 0), ALU.mult))
                    after(f"C{h // 2}")
                    do(f"Q{h}", dve.tensor_tensor(level_f[:, m, 1].rearrange("p (n h) -> p n h", h=h),
                                                          half(q[:], h, 1), half(C[:], h, 1), ALU.mult))
                    if h < LEVELS[-1]:
                        grow_d(h)
                        grow_c(h)

            def value_rest(n):
                ve.wait_ge(v_hi, n * 2 + 3)
                for tt in range(TT):
                    dve.tensor_tensor(V.lo[:, tt, :, :, 0:DK],
                                      ps[:, 3, tt * D:tt * D + D].rearrange("p (c j d) -> p c j d", c=KT, d=DK),
                                      V.hi[:, tt, :, :, 0:DK].bitcast(F32), ALU.subtract).then_inc(v_lo, 1)

            def merge(n, normalise_of=None, x_of=None):
                ve.wait_ge(A_lo, n * 4 + 1)
                for k_, (u, m) in enumerate(MERGES):
                    if k_ == 3 and normalise_of is not None:
                        normalise(normalise_of)
                    if k_ == 4 and x_of is not None:
                        x_rest(x_of)
                    c, b, kind = USES[u]
                    tile = A[b][:, c, :, 0:P]
                    bank = grp[:, u % 4]
                    ve.wait_ge(use_ready, n * NU + u + 2)
                    ve.wait_ge(merged, n * NM + k_ - 1 + SPARE)
                    ve.sem_inc(dve_gate, 1)
                    if kind == "base":
                        mask = base_mask[:].unsqueeze(1).broadcast_to([P, HT, P]).bitcast(I32)
                        dve.copy_predicated(tile, mask, bank.rearrange("p (j t) -> p j t", j=HT)).then_inc(merged, 1)
                        continue
                    lev = m + (2 if kind == "high" else 0)
                    h = LEVELS[lev]
                    to = tile.rearrange("p j (n two h) -> p j n two h", two=2, h=h)[:, :, :, 1, :]
                    data = bank[:, 256 * m:256 * m + 256].rearrange("p (j n h) -> p j n h", j=HT, h=h)
                    mask = level_mask[:, lev].rearrange("p (n h) -> p n h", h=h).unsqueeze(1)
                    mask = mask.broadcast_to([P, HT, P // 2 // h, h]).bitcast(I32)
                    dve.copy_predicated(to, mask, data).then_inc(merged, 1)

            def output_rest(n):
                ve.wait_ge(o_hi, n + 2)
                ve.wait_ge(sq_made, n + 2)
                dve.tensor_tensor(flat(oT.lo[:]), ps[:, 0], flat(oT.hi[:]).bitcast(F32), ALU.subtract).then_inc(o_lo, 1)

            def squares(n):
                ve.wait_ge(use_ready, n * NU + NU)
                dve.tensor_scalar(msq[:], grp[:, (NU - 2) % 4, 0:TT], 1.0 / D, EPS, ALU.mult, ALU.add).then_inc(msq_made, 1)
                ve.wait_ge(msq_made, n + 2)
                ve.sem_inc(merged, 1)

            def residual_sum(n):
                ve.wait_ge(use_ready, n * NU + NU + 1)
                ve.wait_ge(rms_made, n + 2)
                ve.wait_ge(res_loaded, n * 16 + 17)
                for tt in range(TT):
                    dve.scalar_tensor_tensor(out=z[:, tt], in0=grp[:, (NU - 1) % 4, tt * D:tt * D + D],
                                             scalar=rms[:, tt:tt + 1], in1=z[:, tt],
                                             op0=ALU.mult, op1=ALU.add).then_inc(z_made, 1)

            def moments(n):
                ve.wait_ge(z_made, n * 2 + 3)
                ve.sem_inc(merged, 1)
                for tt in range(TT):
                    ins = dve.bn_stats(stats[:, tt], z[:, tt])
                ins.then_inc(tail_chain, 1)

            def variance(n):
                ve.wait_ge(tail_chain, n * 2 + 2)
                ve.sem_inc(dve_gate, 1)
                for tt in range(TT):
                    ins = dve.bn_aggr(mv[:, tt], stats[:, tt])
                ins.then_inc(tail_chain, 1)
                ve.wait_ge(tail_chain, n * 2 + 3)
                dve.tensor_scalar(var[:], mv[:, :, 1], EPS, None, ALU.add).then_inc(var_made, 1)

            def normalise(n):
                ve.wait_ge(rstd_made, n + 2)
                for tt in range(TT):
                    dve.tensor_scalar(z[:, tt], z[:, tt], mv[:, tt, 0:1], rstd[:, tt:tt + 1],
                                      ALU.subtract, ALU.mult).then_inc(x1_made, 1)

            x_rest(0)
            value_rest(0)
            factors(0)
            merge(0, x_of=1)

            def step(n):
                factors(n + 1, outputs_of=n)
                residual_sum(n)
                moments(n)
                variance(n)
                merge(n + 1, normalise_of=n, x_of=None if isinstance(n, int) else n + 2)

            with ve.Fori(0, B - 2) as i:
                step(i)
            step(B - 2)
            output_rest(B - 1)
            squares(B - 1)
            residual_sum(B - 1)
            moments(B - 1)
            variance(B - 1)
            normalise(B - 1)


def cross_attention_pass(nc, x, context, w_kv, w_q, w_out1, w_out2, gamma, x_out):
    B, T, D = x.shape
    INNER = w_q.shape[1]
    DH = 64
    PAIRS = INNER // P
    KT = D // P
    TT = T // P
    SCALE = float(DH) ** -0.5

    INPUTS = ["c"] + [f"k{u}" for u in range(4)] + ["x"] + [f"q{u}" for u in range(4)]
    START = [f"v{u}" for u in range(4)] + ["t0,0", "t0,1"]
    for p in range(1, PAIRS - 1):
        START += [f"t{p},0", f"t{p},1", f"o{p - 1}"]
    START += [f"t{PAIRS - 1},0", f"t{PAIRS - 1},1"]
    STEP = START + ["c", f"o{PAIRS - 2}", f"o{PAIRS - 1}", "k0", "k1", "k2", "k3", "x", "h", "q0", "z", "q1", "q2", "q3"]
    LAST = START + [f"o{PAIRS - 2}", f"o{PAIRS - 1}", "h", "z"]
    NU = len(STEP)
    assert NU % 4 == 0
    FREE = 4

    def unit_place(n):
        if n is None:
            return INPUTS, 0
        return (LAST if isinstance(n, int) else STEP), len(INPUTS)

    def bank_of(n, unit):
        units, base = unit_place(n)
        return (base + units.index(unit)) % 4

    def number(n, unit, rounded=False):
        units, base = unit_place(n)
        before = units[:units.index(unit)]
        if rounded:
            before = [u for u in before if u != "z"]
        return len(before) + base + (0 if n is None else n * (NU - 1 if rounded else NU))

    with ExitStack() as ctx:
        def sb(name, shape, dt=F32):
            return ctx.enter_context(nc.sbuf_tensor("c_" + name, shape, dt))

        def sem(name):
            return ctx.enter_context(nc.semaphore("c_" + name))

        wkv = Split(sb, "wkv", [P, KT, 2 * INNER])
        wq = Split(sb, "wq", [P, KT, INNER])
        w1 = Split(sb, "w1", [P, PAIRS, D])
        w2 = Split(sb, "w2", [P, KT, D])
        gam = sb("gamma", [P, D])
        ident = sb("ident", [P, P])
        neg_half = sb("neg_half", [P, TT])
        c_in = sb("c_in", [P, TT, D])
        x_in = sb("x_in", [P, TT, D])
        cT = Split(sb, "cT", [P, KT, T])
        xT = Split(sb, "xT", [P, KT, T])
        kT = Split(sb, "kT", [P, PAIRS, T])
        qT = Split(sb, "qT", [P, PAIRS, T])
        V = Split(sb, "V", [P, TT, PAIRS, 3, DH])
        E = sb("E", [P, 4, 2, TT, T])
        stage = E[:].rearrange("p (two a) j t n -> p two (a j t n)", two=2)
        PT = Split(sb, "PT", [P, 2, 4, T])
        oT = Split(sb, "oT", [P, PAIRS, T])
        hT = Split(sb, "hT", [P, KT, T])
        top = sb("top", [P, 4, 2, TT])
        bias = sb("bias", [P, 4, 2, TT])
        total = sb("total", [P, 4, 2, TT])
        recip = sb("recip", [P, 4, 2, TT])
        stats = sb("stats", [P, TT, 6])
        mv = sb("mv", [P, TT, 2])
        var = sb("var", [P, 2, TT])
        rstd = sb("rstd", [P, 2, TT])
        yg = sb("yg", [P, TT, D])
        z = sb("z", [P, TT, D])
        x2 = sb("x2", [P, TT, D])

        ring = ctx.enter_context(nc.psum_tensor("c_ring", [P, 4, 512], F32))
        score = ctx.enter_context(nc.psum_tensor("c_score", [P, 4, TT, T], F32))

        w_loaded = [sem(f"w_loaded{n}") for n in range(2)]
        w_hi = sem("w_hi"); w_lo = sem("w_lo"); gamma_loaded = sem("gamma_loaded")
        const_made = sem("const_made")
        c_loaded = sem("c_loaded"); x_loaded = sem("x_loaded"); res_loaded = sem("res_loaded"); x_stored = sem("x_stored")
        unit_ready = sem("unit_ready"); unit_hi = sem("unit_hi"); unit_lo = sem("unit_lo")
        scores = sem("scores"); bias_made = sem("bias_made"); exp_made = sem("exp_made")
        recip_made = sem("recip_made"); normal = sem("normal")
        chain = sem("chain"); top_made = sem("top_made"); z_made = sem("z_made"); var_made = sem("var_made"); rstd_made = sem("rstd_made")
        x2_made = sem("x2_made")
        dve_gate = sem("dve_gate"); pool_gate = sem("pool_gate")
        counted = [c_loaded, x_loaded, res_loaded, x_stored, scores, bias_made,
                   recip_made, normal, chain, top_made, z_made, var_made, rstd_made, x2_made]

        xr = x.rearrange("b (t p) d -> b p t d", p=P)
        cr = context.rearrange("b (t p) d -> b p t d", p=P)
        outr = x_out.rearrange("b (t p) d -> b p t d", p=P)
        flat = lambda t: t.rearrange("p k t -> p (k t)")

        kvr = w_kv.rearrange("(k p) n -> p k n", p=P)
        pieces = [(kvr[:, k], wkv, (lambda t, k=k: t[:, k, :]), 2048) for k in range(KT)]
        pieces += [(w_q.rearrange("(k p) n -> p k n", p=P), wq, lambda t: flat(t[:]), 2048)]
        pieces += [(w_out1.rearrange("(k p) n -> p k n", p=P), w1, lambda t: flat(t[:]), 2048)]
        pieces += [(w_out2.rearrange("(k p) n -> p k n", p=P), w2, lambda t: flat(t[:]), 512)]

        block = ctx.enter_context(nc.Block())

        @block.sync
        def _(sp):
            for s in counted:
                sp.sem_inc(s, 1)
            sp.sem_inc(unit_lo, FREE)
            sp.sem_inc(exp_made, 2)
            sp.dma_start(gam[:], gamma.rearrange("(a d) -> a d", a=1).broadcast_to([P, D])).then_inc(gamma_loaded, 16)
            for n, (src, _, _, cols) in enumerate(pieces):
                if n >= 2:
                    sp.wait_ge(w_lo, n - 1)
                dst = stage[:, n % 2, 0:cols]
                if len(src.shape) == 3:
                    dst = dst.rearrange("p (k n) -> p k n", k=src.shape[1])
                sp.dma_start(dst, src).then_inc(w_loaded[n % 2], 16)

            def element(t, n):
                return t[bass.ds(n, 1)].rearrange("a p t d -> (a p) t d")

            def inputs(n, before, first=False):
                if not first:
                    sp.wait_ge(unit_ready, number(before, "c") + 1)
                sp.dma_start(c_in[:], element(cr, n)).then_inc(c_loaded, 16)
                if not first:
                    sp.wait_ge(unit_ready, number(before, "x") + 1)
                sp.dma_start(x_in[:], element(xr, n)).then_inc(x_loaded, 16)

            def residual(n):
                sp.wait_ge(x2_made, n * TT + 1)
                sp.dma_start(z[:], element(xr, n)).then_inc(res_loaded, 16)

            def store(n):
                sp.wait_ge(x2_made, n * TT + TT + 1)
                sp.dma_start(element(outr, n), x2[:]).then_inc(x_stored, 16)

            inputs(0, None, first=True)
            inputs(1, None)
            residual(0)
            with sp.Fori(0, B - 2) as i:
                inputs(i + 2, i)
                store(i)
                residual(i + 1)
            store(B - 2)
            residual(B - 1)
            store(B - 1)
            sp.wait_ge(x_stored, 16 * B + 1)

        @block.gpsimd
        def _(pool):
            build_identity(nc, pool, ident, const_made)
            nc.gpsimd.memset(neg_half[:], -0.5).then_inc(const_made, 1)
            for t in (V.hi, V.lo):
                nc.gpsimd.memset(t[:].bitcast(F32), 0.0).then_inc(const_made, 1)
            with pool.Fori(0, B) as i:
                for p in range(PAIRS):
                    for j in range(2):
                        for tt in range(TT):
                            if j == 0 and tt == 0:
                                pool.wait_ge(recip_made, i * PAIRS + p + 2)
                                pool.sem_inc(pool_gate, 1)
                            e = E[:, p % 4, j, tt, :]
                            ins = nc.gpsimd.tensor_scalar(e, e, recip[:, p % 4, j, tt:tt + 1], 1.0, ALU.mult, ALU.mult)
                    ins.then_inc(normal, 1)
                for n in range(2):
                    pool.wait_ge(var_made, i * 2 + n + 2)
                    nc.gpsimd.tensor_tensor(rstd[:, n], var[:, n], neg_half[:], ALU.pow).then_inc(rstd_made, 1)

        @block.tensor
        def _(pe):
            pe.wait_ge(const_made, 5)
            pe.wait_ge(w_lo, len(pieces))

            def bank(n, unit):
                pe.wait_ge(unit_lo, number(n, unit) + 1)
                return ring[:, bank_of(n, unit)]

            def drained(n, unit):
                pe.wait_ge(unit_lo, FREE + number(n, unit) + 1)

            def transposed(n, unit, src, loaded):
                pe.wait_ge(loaded, (0 if n is None else n + 1) * 16 + 17)
                to = bank(n, unit)
                for kt in range(KT):
                    for tt in range(TT):
                        mm = nc.tensor.transpose(to[:, kt * T + tt * P:kt * T + tt * P + P],
                                                 src[:, tt, kt * P:kt * P + P], ident[:])
                mm.then_inc(unit_ready, 1)

            def keys_or_queries(n, unit):
                w, src = (wkv, cT) if unit[0] == "k" else (wq, xT)
                to = bank(n, unit)
                for m in range(2):
                    p = 2 * int(unit[1]) + m
                    for kt in range(KT):
                        mm = product(nc, to[:, m * T:m * T + T], w, src,
                                     lambda t, kt=kt, p=p: t[:, kt, p * P:p * P + P],
                                     lambda t, kt=kt: t[:, kt, :], kt == 0, kt == KT - 1)
                mm.then_inc(unit_ready, 1)

            def values(n, u):
                to = bank(n, f"v{u}")
                st, half = divmod(u, 2)
                for kt in range(KT):
                    mm = product(nc, to[:, :], cT, wkv,
                                 lambda t, kt=kt, st=st: t[:, kt, st * P:st * P + P],
                                 lambda t, kt=kt, half=half: t[:, kt, INNER + half * 512:INNER + half * 512 + 512],
                                 kt == 0, kt == KT - 1)
                mm.then_inc(unit_ready, 1)

            def score_pair(e, p):
                pe.wait_ge(exp_made, e * PAIRS + p + 1)
                for tt in range(TT):
                    for wpart, mpart in ((qT.hi, kT.hi), (qT.hi, kT.lo), (qT.lo, kT.hi)):
                        for j in range(2):
                            rows = slice(DH * j, DH * j + DH)
                            mm = nc.tensor.matmul(score[:, 2 * (p % 2) + j, tt, :],
                                                  wpart[rows, p, tt * P:tt * P + P], mpart[rows, p, :],
                                                  start=(wpart is qT.hi and mpart is kT.hi), stop=(wpart is qT.lo),
                                                  tile_position=(DH * j, 0), skip_group_check=True)
                mm.then_inc(scores, 1)

            def probabilities_transposed(n, p):
                pe.wait_ge(normal, n * PAIRS + p + 2)
                for tt in range(TT):
                    to = bank(n, f"t{p},{tt}")
                    for j in range(2):
                        for st in range(TT):
                            m = 2 * j + st
                            mm = nc.tensor.transpose(to[:, m * P:m * P + P], E[:, p % 4, j, tt, st * P:st * P + P],
                                                     ident[:])
                    mm.then_inc(unit_ready, 1)

            def weigh_values(n, p):
                drained(n, f"t{p},1")
                to = bank(n, f"o{p}")
                for j in range(2):
                    for st in range(TT):
                        mm = product(nc, to[:, 0:T], V, PT,
                                     lambda t, st=st, j=j, p=p: t[:, st, p, j:j + 2, :].rearrange("p a d -> p (a d)"),
                                     lambda t, st=st, j=j, p=p: t[:, p % 2, 2 * j + st, :],
                                     j == 0 and st == 0, j == 1 and st == TT - 1)
                mm.then_inc(unit_ready, 1)

            def project_heads(n):
                drained(n, f"o{PAIRS - 1}")
                to = bank(n, "h")
                for m in range(KT):
                    for p in range(PAIRS):
                        mm = product(nc, to[:, m * T:m * T + T], w1, oT,
                                     lambda t, p=p, m=m: t[:, p, m * P:m * P + P],
                                     lambda t, p=p: t[:, p, :], p == 0, p == PAIRS - 1)
                mm.then_inc(unit_ready, 1)

            def project_out(n):
                drained(n, "h")
                to = bank(n, "z")
                for tt in range(TT):
                    for kt in range(KT):
                        mm = product(nc, to[:, tt * D:tt * D + D], hT, w2,
                                     lambda t, kt=kt, tt=tt: t[:, kt, tt * P:tt * P + P],
                                     lambda t, kt=kt: t[:, kt, :], kt == 0, kt == KT - 1)
                mm.then_inc(unit_ready, 1)

            def step(n):
                last = isinstance(n, int)
                for u in range(4):
                    values(n, u)
                    if u == 1:
                        score_pair(n, 2)
                for p in range(PAIRS):
                    probabilities_transposed(n, p)
                    if p == PAIRS - 1 and not last:
                        transposed(n, "c", c_in, c_loaded)
                    if p + 3 < PAIRS:
                        score_pair(n, p + 3)
                    if p >= 1:
                        weigh_values(n, p - 1)
                weigh_values(n, PAIRS - 1)
                if last:
                    project_heads(n)
                    project_out(n)
                    return
                for u in range(4):
                    if u == 0:
                        drained(n, "c")
                    keys_or_queries(n, f"k{u}")
                transposed(n, "x", x_in, x_loaded)
                project_heads(n)
                drained(n, "x")
                keys_or_queries(n, "q0")
                project_out(n)
                for u in range(1, 4):
                    keys_or_queries(n, f"q{u}")
                drained(n, "q0")
                score_pair(n + 1, 0)
                score_pair(n + 1, 1)

            transposed(None, "c", c_in, c_loaded)
            drained(None, "c")
            for u in range(4):
                keys_or_queries(None, f"k{u}")
            transposed(None, "x", x_in, x_loaded)
            drained(None, "x")
            for u in range(4):
                keys_or_queries(None, f"q{u}")
            drained(None, "q3")
            score_pair(0, 0)
            score_pair(0, 1)
            with pe.Fori(0, B - 1) as i:
                step(i)
            step(B - 1)

        def unit_tiles(unit):
            kind = unit[0]
            if kind in "cx":
                t = cT if kind == "c" else xT
                return t, lambda part: flat(part[:]), lambda b: b
            if kind in "kq":
                t, n = (kT if kind == "k" else qT), int(unit[1])
                return t, lambda part: flat(part[:, 2 * n:2 * n + 2]), lambda b: b
            if kind == "v":
                st, half = divmod(int(unit[1]), 2)
                return (V, lambda part: part[:, st, 4 * half:4 * half + 4, 0:3:2, :],
                        lambda b: b.rearrange("p (q j d) -> p q j d", j=2, d=DH))
            if kind == "t":
                p, tt = (int(s) for s in unit[1:].split(","))
                return (PT, lambda part: part[:, p % 2, :, tt * P:tt * P + P],
                        lambda b: b.rearrange("p (n t) -> p n t", n=4))
            if kind == "o":
                return oT, lambda part: part[:, int(unit[1]), :], lambda b: b[:, 0:T]
            return hT, lambda part: flat(part[:]), lambda b: b

        @block.scalar
        def _(act):
            for n, (_, split, at, cols) in enumerate(pieces):
                act.wait_ge(w_loaded[n % 2], 16 * (n // 2 + 1))
                nc.scalar.activation(at(split.hi), stage[:, n % 2, 0:cols], ACT.Copy).then_inc(w_hi, 1)
            act.wait_ge(const_made, 5)

            def round_unit(n, unit):
                if unit == "z":
                    return
                act.wait_ge(unit_ready, number(n, unit) + 1)
                split, at, view = unit_tiles(unit)
                nc.scalar.activation(at(split.hi), view(ring[:, bank_of(n, unit)]),
                                     ACT.Relu if unit == "h" else ACT.Copy).then_inc(unit_hi, 1)

            def exponentials(e, p):
                act.wait_ge(bias_made, e * PAIRS + p + 2)
                for j in range(2):
                    for tt in range(TT):
                        ins = nc.scalar.activation(E[:, p % 4, j, tt, :], score[:, 2 * (p % 2) + j, tt, :], ACT.Exp,
                                                   bias=bias[:, p % 4, j, tt:tt + 1], scale=SCALE,
                                                   accum_out=total[:, p % 4, j, tt:tt + 1])
                ins.then_inc(exp_made, 1)

            def step(n):
                exponentials(n, 0)
                round_unit(n, "v0")
                round_unit(n, "v1")
                exponentials(n, 1)
                round_unit(n, "v2")
                round_unit(n, "v3")
                for p in range(PAIRS):
                    round_unit(n, f"t{p},0")
                    round_unit(n, f"t{p},1")
                    if p + 2 < PAIRS:
                        exponentials(n, p + 2)
                    if 1 <= p < PAIRS - 1:
                        round_unit(n, f"o{p - 1}")
                for unit in (LAST if isinstance(n, int) else STEP)[len(START):]:
                    round_unit(n, unit)

            for unit in INPUTS:
                round_unit(None, unit)
            with act.Fori(0, B - 1) as i:
                step(i)
            step(B - 1)

        @block.vector
        def _(ve):
            dve = nc.vector
            for n, (_, split, at, cols) in enumerate(pieces):
                ve.wait_ge(w_hi, n + 1)
                dve.tensor_tensor(at(split.lo), stage[:, n % 2, 0:cols], at(split.hi).bitcast(F32),
                                  ALU.subtract).then_inc(w_lo, 1)
            ve.wait_ge(const_made, 5)
            ve.wait_ge(gamma_loaded, 16)

            def rest_unit(n, unit):
                split, at, view = unit_tiles(unit)
                ve.wait_ge(unit_hi, number(n, unit, rounded=True) + 1)
                src, hi, lo = view(ring[:, bank_of(n, unit)]), at(split.hi).bitcast(F32), at(split.lo)
                if unit == "h":
                    dve.scalar_tensor_tensor(out=lo, in0=src, scalar=0.0, in1=hi, op0=ALU.max,
                                             op1=ALU.subtract).then_inc(unit_lo, 1)
                else:
                    dve.tensor_tensor(lo, src, hi, ALU.subtract).then_inc(unit_lo, 1)

            def maxima(e, p):
                ve.wait_ge(scores, e * PAIRS + p + 2)
                dve.tensor_reduce(top[:, p % 4], score[:, 2 * (p % 2):2 * (p % 2) + 2], AX.X, ALU.max).then_inc(top_made, 1)
                ve.wait_ge(top_made, e * PAIRS + p + 2)
                dve.tensor_scalar(bias[:, p % 4], top[:, p % 4], -SCALE, None, ALU.mult).then_inc(bias_made, 1)

            def reciprocals(e, p):
                ve.wait_ge(exp_made, e * PAIRS + p + 3)
                dve.reciprocal(recip[:, p % 4], total[:, p % 4]).then_inc(recip_made, 1)

            def moments(n, which, src):
                for tt in range(TT):
                    ins = dve.bn_stats(stats[:, tt], src(tt))
                ins.then_inc(chain, 1)
                ve.wait_ge(chain, n * 4 + 2 * which + 2)
                ve.sem_inc(dve_gate, 1)
                for tt in range(TT):
                    ins = dve.bn_aggr(mv[:, tt], stats[:, tt])
                ins.then_inc(chain, 1)
                ve.wait_ge(chain, n * 4 + 2 * which + 3)
                dve.tensor_scalar(var[:, which], mv[:, :, 1], EPS, None, ALU.add).then_inc(var_made, 1)

            def centre(n):
                bank = ring[:, bank_of(n, "z")]
                ve.wait_ge(unit_ready, number(n, "z") + 1)
                moments(n, 0, lambda tt: bank[:, tt * D:tt * D + D])
                for tt in range(TT):
                    ins = dve.scalar_tensor_tensor(out=yg[:, tt], in0=bank[:, tt * D:tt * D + D], scalar=mv[:, tt, 0:1],
                                                   in1=gam[:], op0=ALU.subtract, op1=ALU.mult)
                ins.then_inc(unit_lo, 1)

            def add_residual(n):
                ve.wait_ge(unit_lo, FREE + number(n, "z") + 1)
                ve.wait_ge(rstd_made, n * 2 + 2)
                ve.wait_ge(res_loaded, n * 16 + 17)
                for tt in range(TT):
                    dve.scalar_tensor_tensor(out=z[:, tt], in0=yg[:, tt], scalar=rstd[:, 0, tt:tt + 1], in1=z[:, tt],
                                             op0=ALU.mult, op1=ALU.add).then_inc(z_made, 1)
                ve.wait_ge(z_made, n * TT + TT + 1)
                moments(n, 1, lambda tt: z[:, tt])

            def normalise(n):
                ve.wait_ge(rstd_made, n * 2 + 3)
                ve.wait_ge(x_stored, n * 16 + 1)
                for tt in range(TT):
                    dve.tensor_scalar(x2[:, tt], z[:, tt], mv[:, tt, 0:1], rstd[:, 1, tt:tt + 1],
                                      ALU.subtract, ALU.mult).then_inc(x2_made, 1)

            def step(n):
                rest_unit(n, "v0")
                reciprocals(n, 0)
                rest_unit(n, "v1")
                maxima(n, 2)
                rest_unit(n, "v2")
                rest_unit(n, "v3")
                for p in range(PAIRS):
                    if p + 1 < PAIRS:
                        reciprocals(n, p + 1)
                    rest_unit(n, f"t{p},0")
                    rest_unit(n, f"t{p},1")
                    if p + 3 < PAIRS:
                        maxima(n, p + 3)
                    if 1 <= p < PAIRS - 1:
                        rest_unit(n, f"o{p - 1}")
                for unit in (LAST if isinstance(n, int) else STEP)[len(START):]:
                    if unit == "z":
                        centre(n)
                    else:
                        rest_unit(n, unit)
                    if unit == "q1":
                        add_residual(n)
                if isinstance(n, int):
                    add_residual(n)
                else:
                    maxima(n + 1, 0)
                    maxima(n + 1, 1)
                normalise(n)

            for unit in INPUTS:
                rest_unit(None, unit)
            maxima(0, 0)
            maxima(0, 1)
            with ve.Fori(0, B - 1) as i:
                step(i)
            step(B - 1)


def experts_pass(nc, x, gate_w, gate_b, w1, b1, w2, b2, out):
    BATCH, T, D = x.shape
    TOKENS = 512
    B = BATCH * T // TOKENS
    NE, _, HID = w1.shape
    KT = D // P
    HT = HID // P
    TT = TOKENS // P
    SLOTS = [0, "turn", 1, "b2"] + list(range(2, NE))
    NS = len(SLOTS)
    assert NS % 2 == 0

    with ExitStack() as ctx:
        def sb(name, shape, dt=F32):
            return ctx.enter_context(nc.sbuf_tensor("e_" + name, shape, dt))

        def sem(name):
            return ctx.enter_context(nc.semaphore("e_" + name))

        STAGES = 4
        stage = sb("stage", [P, STAGES, KT * HID])
        W1 = Split(sb, "w1", [P, NE, KT, HID])
        W2 = Split(sb, "w2", [P, NE, HT, D])
        gate_f = sb("gate_f", [P, KT, NE])
        GW = Split(sb, "gate_w", [P, KT, NE])
        gb = sb("gate_b", [P, NE])
        b1_cols = sb("b1", [P, NE, HT])
        b2_rows = sb("b2", [NE, D])
        ident = sb("ident", [P, P])
        neg_half = sb("neg_half", [P, TT])
        x_in = sb("x_in", [P, TT, D])
        xT = Split(sb, "xT", [P, KT, TOKENS])
        h_f = sb("h_f", [P, 2, TOKENS])
        hT = Split(sb, "hT", [P, 2, HT, TOKENS])
        logit = sb("logit", [P, TT, NE])
        peak = sb("peak", [P, TT])
        shifted = sb("shifted", [P, TT, NE])
        exps = sb("exps", [P, TT, NE])
        total = sb("total", [P, TT])
        recip = sb("recip", [P, TT])
        prob = sb("prob", [P, TT, 16])
        best = sb("best", [P, TT, 8])
        chosen = sb("chosen", [P, TT, 8])
        others = sb("others", [P, TT, 16])
        weight = sb("weight", [P, TT, NE])
        wT = sb("wT", [NE, TOKENS])
        acc = sb("acc", [P, TT, D])
        stats = sb("stats", [P, TT, 6])
        mv = sb("mv", [P, TT, 2])
        var = sb("var", [P, TT])
        rstd = sb("rstd", [P, TT])
        res = sb("res", [P, TT, D])

        hps = ctx.enter_context(nc.psum_tensor("e_hps", [P, 4, 512], F32))
        yps = ctx.enter_context(nc.psum_tensor("e_yps", [P, 4, 2, D], F32))

        w_loaded = [sem(f"w_loaded{n}") for n in range(STAGES)]
        small_loaded = sem("small_loaded")
        w_hi = sem("w_hi"); w_lo = sem("w_lo"); gate_split = sem("gate_split")
        const_made = sem("const_made")
        x_loaded = sem("x_loaded"); stored = sem("stored")
        xT_ps = sem("xT_ps"); xT_hi = sem("xT_hi"); xT_lo = sem("xT_lo")
        gate_ps = sem("gate_ps"); gate_read = sem("gate_read"); shifted_made = sem("shifted_made")
        e_made = sem("e_made"); weight_made = sem("weight_made")
        wT_made = sem("wT_made")
        h_ps = sem("h_ps"); h_made = sem("h_made"); h_split = sem("h_split"); h_rounded = sem("h_rounded"); peak_made = sem("peak_made")
        y_ps = sem("y_ps"); y_read = sem("y_read");
        var_made = sem("var_made"); rstd_made = sem("rstd_made"); res_made = sem("res_made")
        chain = sem("chain"); tail_chain = sem("tail_chain"); dve_gate = sem("dve_gate")
        counted = [x_loaded, stored, xT_ps, xT_hi, xT_lo, gate_ps, gate_read, shifted_made, e_made, weight_made,
                   wT_made, h_ps, h_made, h_split, h_rounded, peak_made, y_ps, var_made, rstd_made, res_made, chain, tail_chain]

        xr = x.rearrange("(g b) (t p) d -> g p (b t) d", b=TOKENS // T, p=P)
        outr = out.rearrange("(g b) (t p) d -> g p (b t) d", b=TOKENS // T, p=P)
        flat = lambda t: t.rearrange("p k t -> p (k t)")
        FREE = 4

        pieces = []
        for n in range(NE):
            pieces.append((w1[n].rearrange("(k p) h -> p k h", p=P), W1, n, KT))
            pieces.append((w2[n].rearrange("(k p) c -> p k c", p=P), W2, n, HT))

        block = ctx.enter_context(nc.Block())

        @block.sync
        def _(sp):
            for s in counted:
                sp.sem_inc(s, 1)
            sp.sem_inc(y_read, FREE)
            sp.dma_start(x_in[:], xr[0]).then_inc(x_loaded, 16)
            with nc.allow_non_contiguous_dma(reason="small, once"):
                sp.dma_start(b1_cols[:], b1.rearrange("e (k p) -> p e k", p=P)).then_inc(small_loaded, 16)
                sp.dma_start(gate_f[:], gate_w.rearrange("(k p) e -> p k e", p=P)).then_inc(small_loaded, 16)
            sp.dma_start(gb[:], gate_b.rearrange("(a e) -> a e", a=1).broadcast_to([P, NE])).then_inc(small_loaded, 16)
            sp.dma_start(b2_rows[:], b2).then_inc(small_loaded, 16)
            for n, (src, _, _, k) in enumerate(pieces):
                if n >= STAGES:
                    sp.wait_ge(w_lo, n - STAGES + 1)
                sp.dma_start(stage[:, n % STAGES].rearrange("p (k n) -> p k n", k=k), src).then_inc(w_loaded[n % STAGES], 16)

            def load(n):
                sp.wait_ge(y_read, n * 2 * NS - 2 * NS + 2 + FREE)
                sp.dma_start(x_in[:], xr[bass.ds(n, 1)].rearrange("a p t d -> (a p) t d")).then_inc(x_loaded, 16)

            def store(n):
                sp.wait_ge(res_made, n * TT + TT + 1)
                for b in range(TOKENS // T):
                    t = slice(b * (T // P), (b + 1) * (T // P))
                    sp.dma_start(outr[bass.ds(n, 1)].rearrange("a p t d -> (a p) t d")[:, t], res[:, t]).then_inc(stored, 16)

            with sp.Fori(0, B - 1) as i:
                load(i + 1)
                store(i)
            store(B - 1)
            sp.wait_ge(stored, 16 * B * (TOKENS // T) + 1)

        @block.gpsimd
        def _(pool):
            build_identity(nc, pool, ident, const_made)
            nc.gpsimd.memset(neg_half[:], -0.5).then_inc(const_made, 1)
            nc.gpsimd.memset(prob[:], -1.0).then_inc(const_made, 1)
            nc.gpsimd.memset(chosen[:], -1.0).then_inc(const_made, 1)
            with pool.Fori(0, B) as i:
                pool.wait_ge(var_made, i + 2)
                nc.gpsimd.tensor_tensor(rstd[:], var[:], neg_half[:], ALU.pow).then_inc(rstd_made, 1)

        @block.tensor
        def _(pe):
            pe.wait_ge(const_made, 5)
            pe.wait_ge(small_loaded, 64)
            pe.wait_ge(gate_split, 2)

            def transposed(n):
                pe.wait_ge(x_loaded, n * 16 + 17)
                if not isinstance(n, int):
                    pe.wait_ge(h_made, n * NE * HT + 1 - (HT - KT))
                for kt in range(KT):
                    for tt in range(TT):
                        mm = nc.tensor.transpose(hps[:, kt, tt * P:tt * P + P], x_in[:, tt, kt * P:kt * P + P], ident[:])
                mm.then_inc(xT_ps, 1)

            def gate(n):
                pe.wait_ge(xT_lo, n + 2)
                pe.wait_ge(h_made, n * NE * HT + 1)
                for tt in range(TT):
                    for kt in range(KT):
                        mm = product(nc, hps[:, 2, tt * NE:tt * NE + NE], xT, GW,
                                     lambda t, kt=kt, tt=tt: t[:, kt, tt * P:tt * P + P],
                                     lambda t, kt=kt: t[:, kt, :], kt == 0, kt == KT - 1)
                mm.then_inc(gate_ps, 1)

            def hidden(n, e):
                for m in range(HT):
                    if e == 0 and m == 2:
                        pe.wait_ge(gate_read, n + 2)
                    pe.wait_ge(h_made, n * NE * HT + max(e * HT + m - 3, 0) + 1)
                    for kt in range(KT):
                        mm = product(nc, hps[:, m, :], W1, xT,
                                     lambda t, kt=kt, m=m: t[:, e, kt, m * P:m * P + P],
                                     lambda t, kt=kt: t[:, kt, :], kt == 0, kt == KT - 1)
                    mm.then_inc(h_ps, 1)

            def slot(n, what):
                k = SLOTS.index(what)
                for pair in range(TT // 2):
                    pe.wait_ge(y_read, n * 2 * NS + 2 * k + pair + 1)
                    yield pair, yps[:, 2 * (k % 2) + pair]

            def combine(n, e):
                pe.wait_ge(h_split, n * NE * HT + e * HT + HT + 1)
                for pair, bank in slot(n, e):
                    for half in range(2):
                        tt = 2 * pair + half
                        for k in range(HT):
                            mm = product(nc, bank[:, half, :], hT, W2,
                                         lambda t, k=k, tt=tt: t[:, e % 2, k, tt * P:tt * P + P],
                                         lambda t, k=k: t[:, e, k, :], k == 0, k == HT - 1)
                    mm.then_inc(y_ps, 1)

            def turn_weights(n):
                pe.wait_ge(weight_made, n + 2)
                for pair, bank in slot(n, "turn"):
                    for half in range(2):
                        mm = nc.tensor.transpose(bank[0:NE, 0, half * P:half * P + P], weight[:, 2 * pair + half, :],
                                                 ident[:])
                    mm.then_inc(y_ps, 1)

            def share_b2(n):
                pe.wait_ge(wT_made, n * 2 + 3)
                for pair, bank in slot(n, "b2"):
                    for half in range(2):
                        tt = 2 * pair + half
                        mm = nc.tensor.matmul(bank[:, half, :], wT[:, tt * P:tt * P + P], b2_rows[:],
                                              start=True, stop=True, skip_group_check=True)
                    mm.then_inc(y_ps, 1)

            def step(n):
                hidden(n, 1)
                for e in range(NE):
                    if e == NE - 2 and not isinstance(n, int):
                        transposed(n + 1)
                    combine(n, e)
                    if e == 0:
                        turn_weights(n)
                    if e + 2 < NE:
                        hidden(n, e + 2)
                    if e == 1:
                        share_b2(n)
                    if e == NE - 2 and not isinstance(n, int):
                        gate(n + 1)
                if not isinstance(n, int):
                    hidden(n + 1, 0)

            transposed(0)
            gate(0)
            pe.wait_ge(w_lo, len(pieces))
            hidden(0, 0)
            with pe.Fori(0, B - 1) as i:
                step(i)
            step(B - 1)

        @block.scalar
        def _(act):
            act.wait_ge(small_loaded, 64)
            nc.scalar.activation(GW.hi[:], gate_f[:], ACT.Copy).then_inc(gate_split, 1)
            for n, (_, split, at, k) in enumerate(pieces):
                act.wait_ge(w_loaded[n % STAGES], 16 * (n // STAGES + 1))
                nc.scalar.activation(flat(split.hi[:, at]), stage[:, n % STAGES], ACT.Copy).then_inc(w_hi, 1)

            def hidden(n, e):
                for m in range(HT):
                    t = e * HT + m
                    act.wait_ge(h_ps, n * NE * HT + t + 2)
                    act.wait_ge(h_split, n * NE * HT + max(t - 1, 0) + 1)
                    nc.scalar.activation(h_f[:, t % 2], hps[:, m, :], ACT.Relu,
                                         bias=b1_cols[:, e, m:m + 1]).then_inc(h_made, 1)

            def round_x(n):
                act.wait_ge(xT_ps, n + 2)
                nc.scalar.activation(xT.hi[:], hps[:, 0:KT], ACT.Copy).then_inc(xT_hi, 1)

            def exponentials(n):
                act.wait_ge(shifted_made, n + 2)
                nc.scalar.activation(exps[:], shifted[:], ACT.Exp).then_inc(e_made, 1)

            round_x(0)
            exponentials(0)
            hidden(0, 0)
            with act.Fori(0, B - 1) as i:
                for e in range(1, NE):
                    hidden(i, e)
                round_x(i + 1)
                exponentials(i + 1)
                hidden(i + 1, 0)
            for e in range(1, NE):
                hidden(B - 1, e)

        @block.vector
        def _(ve):
            dve = nc.vector
            ve.wait_ge(gate_split, 1)
            dve.tensor_tensor(GW.lo[:], gate_f[:], GW.hi[:].bitcast(F32), ALU.subtract).then_inc(gate_split, 1)
            for n, (_, split, at, k) in enumerate(pieces):
                ve.wait_ge(w_hi, n + 1)
                dve.tensor_tensor(flat(split.lo[:, at]), stage[:, n % STAGES], flat(split.hi[:, at]).bitcast(F32),
                                  ALU.subtract).then_inc(w_lo, 1)
            ve.wait_ge(const_made, 5)

            def linker(sem_, n, total):
                linked = [0]

                def link(ins):
                    linked[0] += 1
                    assert linked[0] <= total
                    ins.then_inc(sem_, 1)
                    ve.wait_ge(sem_, n * total + linked[0] + 1)
                return link

            def split_hidden(n, e):
                for m in range(HT):
                    t = e * HT + m
                    ve.wait_ge(h_made, n * NE * HT + t + 2)
                    if m == 0:
                        if e >= 2:
                            ve.wait_ge(y_ps, n * NS * 2 + 2 * SLOTS.index(e - 2) + 3)
                        elif not isinstance(n, int) or n > 0:
                            ve.wait_ge(y_ps, n * NS * 2 + 2 * SLOTS.index(e + NE - 2) + 3 - 2 * NS)
                    hi = hT.hi[:, e % 2, m]
                    dve.tensor_copy(hi, h_f[:, t % 2]).then_inc(h_rounded, 1)
                    ve.wait_ge(h_rounded, n * NE * HT + t + 2)
                    dve.tensor_tensor(hT.lo[:, e % 2, m], h_f[:, t % 2], hi.bitcast(F32), ALU.subtract).then_inc(h_split, 1)

            def read_slot(n, what):
                k = SLOTS.index(what)
                for pair in range(TT // 2):
                    ve.wait_ge(y_ps, n * NS * 2 + 2 * k + pair + 2)
                    yield pair, yps[:, 2 * (k % 2) + pair]

            def add_expert(n, e):
                if e == 0:
                    ve.wait_ge(weight_made, n + 2)
                    ve.wait_ge(res_made, n * TT + 1)
                else:
                    before = SLOTS.index("b2" if e == 2 else e - 1)
                    ve.wait_ge(y_read, n * NS * 2 + 2 * before + 2 + FREE)
                for pair, bank in read_slot(n, e):
                    for half in range(2):
                        tt = 2 * pair + half
                        ins = dve.scalar_tensor_tensor(out=acc[:, tt], in0=bank[:, half, :], scalar=weight[:, tt, e:e + 1],
                                                       in1=(x_in if e == 0 else acc)[:, tt], op0=ALU.mult, op1=ALU.add)
                    ins.then_inc(y_read, 1)

            def turned_weights(n):
                ve.wait_ge(y_ps, n * NS * 2 + 2)
                for pair, bank in read_slot(n, "turn"):
                    dve.tensor_copy(wT[:, pair * 2 * P:(pair + 1) * 2 * P], bank[0:NE, 0, :]).then_inc(wT_made, 1)
                    ve.wait_ge(wT_made, n * 2 + pair + 2)
                    ve.sem_inc(y_read, 1)

            def add_b2(n):
                ve.wait_ge(y_read, n * NS * 2 + 2 * SLOTS.index(1) + 2 + FREE)
                for pair, bank in read_slot(n, "b2"):
                    dve.tensor_tensor(acc[:, 2 * pair:2 * pair + 2], bank, acc[:, 2 * pair:2 * pair + 2],
                                      ALU.add).then_inc(y_read, 1)

            def x_rest(n):
                ve.wait_ge(xT_hi, n + 2)
                dve.tensor_tensor(xT.lo[:], hps[:, 0:KT], xT.hi[:].bitcast(F32), ALU.subtract).then_inc(xT_lo, 1)

            def shift_logits(n):
                ve.wait_ge(gate_ps, n + 2)
                gates = hps[:, 2, 0:TT * NE].rearrange("p (t e) -> p t e", e=NE)
                dve.tensor_tensor(logit[:], gates, gb[:].unsqueeze(1).broadcast_to([P, TT, NE]), ALU.add).then_inc(gate_read, 1)
                ve.wait_ge(gate_read, n + 2)
                dve.tensor_reduce(peak[:], logit[:], AX.X, ALU.max).then_inc(peak_made, 1)
                ve.wait_ge(peak_made, n + 2)
                dve.tensor_tensor(shifted[:], logit[:], peak[:].unsqueeze(2).broadcast_to([P, TT, NE]),
                                  ALU.subtract).then_inc(shifted_made, 1)

            def choose(n):
                link = linker(chain, n, 6)
                ve.wait_ge(e_made, n + 2)
                link(dve.tensor_reduce(total[:], exps[:], AX.X, ALU.add))
                link(dve.reciprocal(recip[:], total[:]))
                link(dve.tensor_tensor(prob[:, :, 0:NE], exps[:], recip[:].unsqueeze(2).broadcast_to([P, TT, NE]), ALU.mult))
                ve.sem_inc(dve_gate, 1)
                for tt in range(TT):
                    ins = dve.max(best[:, tt], prob[:, tt])
                link(ins)
                link(dve.tensor_copy(chosen[:, :, 0:2], best[:, :, 0:2]))
                ve.sem_inc(dve_gate, 1)
                for tt in range(TT):
                    ins = dve.match_replace(others[:, tt], chosen[:, tt], prob[:, tt], 0.0)
                link(ins)
                dve.tensor_tensor(weight[:], prob[:, :, 0:NE], others[:, :, 0:NE], ALU.subtract).then_inc(weight_made, 1)

            def moments(n):
                link = linker(tail_chain, n, 2)
                ve.wait_ge(y_read, n * NS * 2 + 2 * NS + FREE)
                for tt in range(TT):
                    ins = dve.bn_stats(stats[:, tt], acc[:, tt])
                link(ins)
                ve.sem_inc(dve_gate, 1)
                for tt in range(TT):
                    ins = dve.bn_aggr(mv[:, tt], stats[:, tt])
                link(ins)
                dve.tensor_scalar(var[:], mv[:, :, 1], EPS, None, ALU.add).then_inc(var_made, 1)

            def normalise(n):
                ve.wait_ge(rstd_made, n + 2)
                ve.wait_ge(stored, n * 16 * (TOKENS // T) + 1)
                for tt in range(TT):
                    dve.tensor_scalar(res[:, tt], acc[:, tt], mv[:, tt, 0:1], rstd[:, tt:tt + 1],
                                      ALU.subtract, ALU.mult).then_inc(res_made, 1)

            def step(n):
                last = isinstance(n, int)
                split_hidden(n, 1)
                for e in range(NE):
                    if e == NE - 2 and not last:
                        x_rest(n + 1)
                    if e == NE - 1 and not last:
                        shift_logits(n + 1)
                    add_expert(n, e)
                    if e == 0:
                        turned_weights(n)
                    if e + 2 < NE:
                        split_hidden(n, e + 2)
                    if e == 1:
                        add_b2(n)
                if not last:
                    choose(n + 1)
                moments(n)
                if not last:
                    split_hidden(n + 1, 0)
                normalise(n)

            x_rest(0)
            shift_logits(0)
            choose(0)
            split_hidden(0, 0)
            with ve.Fori(0, B - 1) as i:
                step(i)
            step(B - 1)



def decoder_layer(nc, x, context, wq, wf, wi, g_weight, wo, w_kv, w_q, w_out1, w_out2, gamma,
                  gate_w, gate_b, w1, b1, w2, b2, out):
    x1 = nc.dram_tensor("after_linear_attention", x.shape, F32, kind="Internal").ap()
    x2 = nc.dram_tensor("after_cross_attention", x.shape, F32, kind="Internal").ap()
    linear_attention_pass(nc, x, wq, wf, wi, g_weight, wo, x1)
    cross_attention_pass(nc, x1, context, w_kv, w_q, w_out1, w_out2, gamma, x2)
    experts_pass(nc, x2, gate_w, gate_b, w1, b1, w2, b2, out)


_INS = ["x", "ctx_1024", "L0_attn_Wq", "L0_attn_Wf", "L0_attn_Wi", "L0_attn_g_weight", "L0_attn_Wo",
        "L0_xattn_w_kv", "L0_xattn_w_q", "L0_xattn_w_out1", "L0_xattn_w_out2", "L0_xattn_gamma",
        "L0_ffn_gate_w", "L0_ffn_gate_b", "L0_ffn_w1", "L0_ffn_b1", "L0_ffn_w2", "L0_ffn_b2"]


def kernel(**inputs):
    import numpy as _np
    import concourse.bacc as _bacc
    from concourse import mybir as _mybir
    from concourse.bass_utils import run_bass_kernel_spmd as _run

    nc = _bacc.Bacc("TRN2", target_bir_lowering=False, num_devices=1)
    arrays, args = {}, []
    for name in _INS:
        a = _np.ascontiguousarray(inputs[name])
        arrays[f"in_{name}_dram"] = a
        args.append(nc.dram_tensor(f"in_{name}_dram", a.shape, _mybir.dt.from_np(a.dtype), kind="ExternalInput").ap())
    out = nc.dram_tensor("out_dram", inputs["x"].shape, _mybir.dt.float32, kind="ExternalOutput").ap()
    decoder_layer(nc, *args, out)
    r = _run(nc, [arrays], core_ids=[0])
    return r.results[0]["out_dram"]
```
